# Optimizing a Trainium2 kernel written in Bass

```python
import numpy as np
import jax
import jax.numpy as jnp

def _softmax(x, axis=-1):
    return jax.nn.softmax(x, axis=axis)

def _gelu(x):
    return jax.nn.gelu(x, approximate=True)

def _silu(x):
    return jax.nn.silu(x)

def _sigmoid(x):
    return jax.nn.sigmoid(x)

def _layernorm(x, axis=-1, eps=1e-05):
    m = jnp.mean(x, axis=axis, keepdims=True)
    v = jnp.var(x, axis=axis, keepdims=True)
    return (x - m) / jnp.sqrt(v + eps)

def _scatter_add(tgt, idx, src, axis=0):
    return tgt.at[idx].add(src)

def _segment_sum(src, seg, n):
    return jax.ops.segment_sum(src, seg, n)
kernel_name = 'mk_recurrent_d2_jaxref_r4_2cc86b'

def setup_inputs(seed: int=0):
    np.random.seed(seed)
    _w = jnp.asarray

    def _L0_attn_setup():
        import jax, jax.numpy as jnp
        import numpy as np
        D_MODEL, D_INNER, D_STATE, DT_RANK, D_CONV = (256, 512, 16, 64, 4)
        BATCH, SEQLEN = (2, 256)

        def _silu(x):
            return x * jax.nn.sigmoid(x)

        def _branch(xz, conv_w, conv_b, Wx, Wdt, bdt, A_log, D):
            d_inner = conv_w.shape[0]
            n = A_log.shape[1]
            dt_rank = Wdt.shape[1]
            x, z = jnp.split(xz, 2, axis=1)
            x = jax.lax.conv_general_dilated(x, conv_w, window_strides=(1,), padding=[(conv_w.shape[-1] - 1, 0)], feature_group_count=d_inner, dimension_numbers=('NCH', 'OIH', 'NCH')) + conv_b[None, :, None]
            x = _silu(x).transpose(0, 2, 1)
            x_dbl = x @ Wx.T
            dt = jax.nn.softplus(x_dbl[..., :dt_rank] @ Wdt.T + bdt)
            B = x_dbl[..., dt_rank:dt_rank + n]
            C = x_dbl[..., dt_rank + n:]
            A = -jnp.exp(A_log)
            deltaA = jnp.exp(jnp.einsum('bld,dn->bldn', dt, A))
            dBu = dt[..., None] * B[:, :, None, :] * x[..., None]

            def step(carry, inp):
                dA_t, dBu_t, C_t = inp
                carry = dA_t * carry + dBu_t
                y_t = jnp.einsum('bdn,bn->bd', carry, C_t)
                return (carry, y_t)
            init = jnp.zeros((x.shape[0], d_inner, n), x.dtype)
            _, ys = jax.lax.scan(step, init, (deltaA.transpose(1, 0, 2, 3), dBu.transpose(1, 0, 2, 3), C.transpose(1, 0, 2)))
            y = ys.transpose(1, 0, 2) + x * D
            return y * _silu(z.transpose(0, 2, 1))
        key = jax.random.key(seed)
        ks = jax.random.split(key, 12)
        s = 0.02
        A_init = jnp.tile(jnp.arange(1, D_STATE + 1, dtype=jnp.float32)[None, :], (D_INNER, 1))
        return {'hidden': jax.random.normal(ks[0], (BATCH, SEQLEN, D_MODEL), jnp.float32), 'W_in': s * jax.random.normal(ks[1], (2 * D_INNER, D_MODEL), jnp.float32), 'conv_w': s * jax.random.normal(ks[2], (D_INNER, 1, D_CONV), jnp.float32), 'conv_b': s * jax.random.normal(ks[3], (D_INNER,), jnp.float32), 'Wx': s * jax.random.normal(ks[4], (DT_RANK + 2 * D_STATE, D_INNER), jnp.float32), 'Wdt': s * jax.random.normal(ks[5], (D_INNER, DT_RANK), jnp.float32), 'bdt': s * jax.random.normal(ks[6], (D_INNER,), jnp.float32), 'A_log': jnp.log(A_init), 'D': jnp.ones((D_INNER,), jnp.float32), 'conv_w_b': s * jax.random.normal(ks[7], (D_INNER, 1, D_CONV), jnp.float32), 'conv_b_b': s * jax.random.normal(ks[8], (D_INNER,), jnp.float32), 'Wx_b': s * jax.random.normal(ks[9], (DT_RANK + 2 * D_STATE, D_INNER), jnp.float32), 'Wdt_b': s * jax.random.normal(ks[10], (D_INNER, DT_RANK), jnp.float32), 'bdt_b': s * jax.random.normal(ks[11], (D_INNER,), jnp.float32), 'A_b_log': jnp.log(A_init), 'D_b': jnp.ones((D_INNER,), jnp.float32), 'W_out': s * jax.random.normal(jax.random.fold_in(key, 99), (D_MODEL, D_INNER), jnp.float32)}
    _L0_attn_in = _L0_attn_setup()

    def _L0_ffn_setup():
        import jax, jax.numpy as jnp
        import numpy as np
        D, H, N, K = (256, 512, 8, 2)
        B, S = (4, 512)
        key = jax.random.key(seed)
        ks = jax.random.split(key, 4)
        x = jax.random.normal(ks[0], (B, S, D), dtype=jnp.float32)
        Wr = jax.random.normal(ks[1], (N, D), dtype=jnp.float32) / np.sqrt(D)
        br = jnp.zeros((N,), jnp.float32)
        Wl1 = jax.random.normal(ks[2], (N, D, 2 * H), dtype=jnp.float32) / np.sqrt(D)
        bl1 = jnp.zeros((N, 2 * H), jnp.float32)
        Wl2 = jax.random.normal(ks[3], (N, H, D), dtype=jnp.float32) / np.sqrt(H)
        bl2 = jnp.zeros((N, D), jnp.float32)
        biases_N = jnp.zeros((N,), jnp.float32)
        return {'x': x, 'Wr': Wr, 'br': br, 'Wl1': Wl1, 'bl1': bl1, 'Wl2': Wl2, 'bl2': bl2, 'biases_N': biases_N}
    _L0_ffn_in = _L0_ffn_setup()

    def _L1_attn_setup():
        import jax, jax.numpy as jnp
        import numpy as np
        DIM = 256
        HEADS = 16
        HD = DIM // HEADS
        B, S = (4, 1024)
        LEVELS = 3
        HID = 4 * DIM
        CHUNK = 128
        EPS = 1e-05

        def layernorm(x, g, b):
            m = jnp.mean(x, axis=-1, keepdims=True)
            v = jnp.var(x, axis=-1, keepdims=True)
            return (x - m) * jax.lax.rsqrt(v + EPS) * g + b

        def _linear_attn_with_memory(h, wq, wk, wv, wo):
            b, s, d = h.shape

            def heads(w):
                return (h @ w).reshape(b, s, HEADS, HD).transpose(0, 2, 1, 3)
            q, k, v = (heads(wq), heads(wk), heads(wv))
            nc = s // CHUNK

            def to_chunks(a):
                return a.reshape(b, HEADS, nc, CHUNK, HD).transpose(2, 0, 1, 3, 4)
            mask = jnp.tril(jnp.ones((CHUNK, CHUNK), h.dtype))

            def step(M, qkv):
                qc, kc, vc = qkv
                inter = jnp.einsum('bhvk,bhck->bhcv', M, qc)
                scores = jnp.einsum('bhcd,bhed->bhce', qc, kc) * mask
                intra = jnp.einsum('bhce,bhev->bhcv', scores, vc)
                M_new = M + jnp.einsum('bhcv,bhck->bhvk', vc, kc)
                return (M_new, inter + intra)
            M0 = jnp.zeros((b, HEADS, HD, HD), h.dtype)
            _, ys = jax.lax.scan(step, M0, (to_chunks(q), to_chunks(k), to_chunks(v)))
            y = ys.transpose(1, 2, 0, 3, 4).reshape(b, HEADS, s, HD)
            y = y.transpose(0, 2, 1, 3).reshape(b, s, d)
            return y @ wo
        key = jax.random.key(seed)
        ks = jax.random.split(key, 10)
        std = 0.02
        return {'x': jax.random.normal(ks[0], (B, S, DIM), jnp.float32), 'ln1_g': jnp.ones((DIM,), jnp.float32), 'ln1_b': jnp.zeros((DIM,), jnp.float32), 'wq': jax.random.normal(ks[1], (DIM, DIM), jnp.float32) * std, 'wk': jax.random.normal(ks[2], (DIM, DIM), jnp.float32) * std, 'wv': jax.random.normal(ks[3], (DIM, DIM), jnp.float32) * std, 'wo': jax.random.normal(ks[4], (DIM, DIM), jnp.float32) * std, 'ln2_g': jnp.ones((DIM,), jnp.float32), 'ln2_b': jnp.zeros((DIM,), jnp.float32), 'cms_w1': jax.random.normal(ks[5], (LEVELS, DIM, HID), jnp.float32) * std, 'cms_b1': jnp.zeros((LEVELS, HID), jnp.float32), 'cms_w2': jax.random.normal(ks[6], (LEVELS, HID, DIM), jnp.float32) * std, 'cms_b2': jnp.zeros((LEVELS, DIM), jnp.float32)}
    _L1_attn_in = _L1_attn_setup()

    def _L1_ffn_setup():
        import jax, jax.numpy as jnp
        import numpy as np
        key = jax.random.key(seed)
        k1, k2, k3, k4, k5 = jax.random.split(key, 5)
        d_in, d_out, r = (256, 256, 32)
        x = jax.random.normal(k1, (8, 2048, d_in), dtype=jnp.float32)
        W = jax.random.normal(k2, (d_out, d_in), dtype=jnp.float32) * (1.0 / np.sqrt(d_in))
        b = jax.random.normal(k3, (d_out,), dtype=jnp.float32) * 0.01
        V_r = jax.random.normal(k4, (d_in, r), dtype=jnp.float32) * (1.0 / np.sqrt(d_in))
        C = jax.random.normal(k5, (d_out, r), dtype=jnp.float32) * (1.0 / np.sqrt(r))
        return {'x': x, 'W': W, 'b': b, 'V_r': V_r, 'C': C}
    _L1_ffn_in = _L1_ffn_setup()
    _d = {'L0_attn_hidden': _L0_attn_in['hidden'], 'L0_attn_W_in': _L0_attn_in['W_in'], 'L0_attn_conv_w': _L0_attn_in['conv_w'], 'L0_attn_conv_b': _L0_attn_in['conv_b'], 'L0_attn_Wx': _L0_attn_in['Wx'], 'L0_attn_Wdt': _L0_attn_in['Wdt'], 'L0_attn_bdt': _L0_attn_in['bdt'], 'L0_attn_A_log': _L0_attn_in['A_log'], 'L0_attn_D': _L0_attn_in['D'], 'L0_attn_conv_w_b': _L0_attn_in['conv_w_b'], 'L0_attn_conv_b_b': _L0_attn_in['conv_b_b'], 'L0_attn_Wx_b': _L0_attn_in['Wx_b'], 'L0_attn_Wdt_b': _L0_attn_in['Wdt_b'], 'L0_attn_bdt_b': _L0_attn_in['bdt_b'], 'L0_attn_A_b_log': _L0_attn_in['A_b_log'], 'L0_attn_D_b': _L0_attn_in['D_b'], 'L0_attn_W_out': _L0_attn_in['W_out'], 'L0_ffn_Wr': _L0_ffn_in['Wr'], 'L0_ffn_br': _L0_ffn_in['br'], 'L0_ffn_Wl1': _L0_ffn_in['Wl1'], 'L0_ffn_bl1': _L0_ffn_in['bl1'], 'L0_ffn_Wl2': _L0_ffn_in['Wl2'], 'L0_ffn_bl2': _L0_ffn_in['bl2'], 'L0_ffn_biases_N': _L0_ffn_in['biases_N'], 'L1_attn_ln1_g': _L1_attn_in['ln1_g'], 'L1_attn_ln1_b': _L1_attn_in['ln1_b'], 'L1_attn_wq': _L1_attn_in['wq'], 'L1_attn_wk': _L1_attn_in['wk'], 'L1_attn_wv': _L1_attn_in['wv'], 'L1_attn_wo': _L1_attn_in['wo'], 'L1_attn_ln2_g': _L1_attn_in['ln2_g'], 'L1_attn_ln2_b': _L1_attn_in['ln2_b'], 'L1_attn_cms_w1': _L1_attn_in['cms_w1'], 'L1_attn_cms_b1': _L1_attn_in['cms_b1'], 'L1_attn_cms_w2': _L1_attn_in['cms_w2'], 'L1_attn_cms_b2': _L1_attn_in['cms_b2'], 'L1_ffn_W': _L1_ffn_in['W'], 'L1_ffn_b': _L1_ffn_in['b'], 'L1_ffn_V_r': _L1_ffn_in['V_r'], 'L1_ffn_C': _L1_ffn_in['C']}
    _x0 = _d['L0_attn_hidden']
    _d['L0_attn_hidden'] = jax.random.normal(jax.random.fold_in(jax.random.key(seed), 1), (8, 512, 256), dtype=_x0.dtype)
    del _x0
    return _d

def reference(L0_attn_hidden, L0_attn_W_in, L0_attn_conv_w, L0_attn_conv_b, L0_attn_Wx, L0_attn_Wdt, L0_attn_bdt, L0_attn_A_log, L0_attn_D, L0_attn_conv_w_b, L0_attn_conv_b_b, L0_attn_Wx_b, L0_attn_Wdt_b, L0_attn_bdt_b, L0_attn_A_b_log, L0_attn_D_b, L0_attn_W_out, L0_ffn_Wr, L0_ffn_br, L0_ffn_Wl1, L0_ffn_bl1, L0_ffn_Wl2, L0_ffn_bl2, L0_ffn_biases_N, L1_attn_ln1_g, L1_attn_ln1_b, L1_attn_wq, L1_attn_wk, L1_attn_wv, L1_attn_wo, L1_attn_ln2_g, L1_attn_ln2_b, L1_attn_cms_w1, L1_attn_cms_b1, L1_attn_cms_w2, L1_attn_cms_b2, L1_ffn_W, L1_ffn_b, L1_ffn_V_r, L1_ffn_C):

    def _L0_attn_ref(hidden, W_in, conv_w, conv_b, Wx, Wdt, bdt, A_log, D, conv_w_b, conv_b_b, Wx_b, Wdt_b, bdt_b, A_b_log, D_b, W_out):
        import jax, jax.numpy as jnp
        import numpy as np
        D_MODEL, D_INNER, D_STATE, DT_RANK, D_CONV = (256, 512, 16, 64, 4)
        BATCH, SEQLEN = (2, 256)

        def _silu(x):
            return x * jax.nn.sigmoid(x)

        def _branch(xz, conv_w, conv_b, Wx, Wdt, bdt, A_log, D):
            d_inner = conv_w.shape[0]
            n = A_log.shape[1]
            dt_rank = Wdt.shape[1]
            x, z = jnp.split(xz, 2, axis=1)
            x = jax.lax.conv_general_dilated(x, conv_w, window_strides=(1,), padding=[(conv_w.shape[-1] - 1, 0)], feature_group_count=d_inner, dimension_numbers=('NCH', 'OIH', 'NCH')) + conv_b[None, :, None]
            x = _silu(x).transpose(0, 2, 1)
            x_dbl = x @ Wx.T
            dt = jax.nn.softplus(x_dbl[..., :dt_rank] @ Wdt.T + bdt)
            B = x_dbl[..., dt_rank:dt_rank + n]
            C = x_dbl[..., dt_rank + n:]
            A = -jnp.exp(A_log)
            deltaA = jnp.exp(jnp.einsum('bld,dn->bldn', dt, A))
            dBu = dt[..., None] * B[:, :, None, :] * x[..., None]

            def step(carry, inp):
                dA_t, dBu_t, C_t = inp
                carry = dA_t * carry + dBu_t
                y_t = jnp.einsum('bdn,bn->bd', carry, C_t)
                return (carry, y_t)
            init = jnp.zeros((x.shape[0], d_inner, n), x.dtype)
            _, ys = jax.lax.scan(step, init, (deltaA.transpose(1, 0, 2, 3), dBu.transpose(1, 0, 2, 3), C.transpose(1, 0, 2)))
            y = ys.transpose(1, 0, 2) + x * D
            return y * _silu(z.transpose(0, 2, 1))
        xz = (hidden @ W_in.T).transpose(0, 2, 1)
        out_f = _branch(xz, conv_w, conv_b, Wx, Wdt, bdt, A_log, D)
        out_b = _branch(xz[..., ::-1], conv_w_b, conv_b_b, Wx_b, Wdt_b, bdt_b, A_b_log, D_b)
        out = (out_f + out_b[:, ::-1]) / 2.0
        return out @ W_out.T

    def _L0_ffn_ref(x, Wr, br, Wl1, bl1, Wl2, bl2, biases_N):
        import jax, jax.numpy as jnp
        import numpy as np
        D, H, N, K = (256, 512, 8, 2)
        B, S = (4, 512)
        Bb, Ss, Dd = x.shape
        scores_BSN = jnp.einsum('bsd,nd->bsn', x, Wr) + br
        w_BSN = jax.nn.softmax(scores_BSN, axis=-1)
        _, idx_BSK = jax.lax.top_k(scores_BSN + biases_N[None, None, :], K)
        val_BSK = jnp.take_along_axis(w_BSN, idx_BSK, axis=-1)
        val_BSK = val_BSK / jnp.sum(val_BSK, axis=-1, keepdims=True)
        M = Bb * Ss
        x_MD = x.reshape(M, Dd)
        idx_MK = idx_BSK.reshape(M, K)
        val_MK = val_BSK.reshape(M, K)
        h_NM2H = jnp.einsum('md,ndh->nmh', x_MD, Wl1) + bl1[:, None, :]
        a_NMH, b_NMH = (h_NM2H[..., :H], h_NM2H[..., H:])
        y_NMD = jnp.einsum('nmh,nhd->nmd', jax.nn.silu(a_NMH) * b_NMH, Wl2) + bl2[:, None, :]
        ew_MN = jnp.zeros((M, N), x.dtype)
        ew_MN = ew_MN.at[jnp.arange(M)[:, None], idx_MK].set(val_MK)
        y_MD = jnp.einsum('mn,nmd->md', ew_MN, y_NMD)
        return y_MD.reshape(Bb, Ss, Dd)

    def _L1_attn_ref(x, ln1_g, ln1_b, wq, wk, wv, wo, ln2_g, ln2_b, cms_w1, cms_b1, cms_w2, cms_b2):
        import jax, jax.numpy as jnp
        import numpy as np
        DIM = 256
        HEADS = 16
        HD = DIM // HEADS
        B, S = (4, 1024)
        LEVELS = 3
        HID = 4 * DIM
        CHUNK = 128
        EPS = 1e-05

        def layernorm(x, g, b):
            m = jnp.mean(x, axis=-1, keepdims=True)
            v = jnp.var(x, axis=-1, keepdims=True)
            return (x - m) * jax.lax.rsqrt(v + EPS) * g + b

        def _linear_attn_with_memory(h, wq, wk, wv, wo):
            b, s, d = h.shape

            def heads(w):
                return (h @ w).reshape(b, s, HEADS, HD).transpose(0, 2, 1, 3)
            q, k, v = (heads(wq), heads(wk), heads(wv))
            nc = s // CHUNK

            def to_chunks(a):
                return a.reshape(b, HEADS, nc, CHUNK, HD).transpose(2, 0, 1, 3, 4)
            mask = jnp.tril(jnp.ones((CHUNK, CHUNK), h.dtype))

            def step(M, qkv):
                qc, kc, vc = qkv
                inter = jnp.einsum('bhvk,bhck->bhcv', M, qc)
                scores = jnp.einsum('bhcd,bhed->bhce', qc, kc) * mask
                intra = jnp.einsum('bhce,bhev->bhcv', scores, vc)
                M_new = M + jnp.einsum('bhcv,bhck->bhvk', vc, kc)
                return (M_new, inter + intra)
            M0 = jnp.zeros((b, HEADS, HD, HD), h.dtype)
            _, ys = jax.lax.scan(step, M0, (to_chunks(q), to_chunks(k), to_chunks(v)))
            y = ys.transpose(1, 2, 0, 3, 4).reshape(b, HEADS, s, HD)
            y = y.transpose(0, 2, 1, 3).reshape(b, s, d)
            return y @ wo
        x = x + _linear_attn_with_memory(layernorm(x, ln1_g, ln1_b), wq, wk, wv, wo)
        h = layernorm(x, ln2_g, ln2_b)
        for l in range(LEVELS):
            h = jax.nn.gelu(h @ cms_w1[l] + cms_b1[l]) @ cms_w2[l] + cms_b2[l]
        return x + h

    def _L1_ffn_ref(x, W, b, V_r, C):
        import jax, jax.numpy as jnp
        import numpy as np
        base = jnp.einsum('bsd,od->bso', x, W) + b
        correction = jnp.einsum('bsr,or->bso', jnp.einsum('bsd,dr->bsr', x, V_r), C)
        return base + correction
    x = L0_attn_hidden
    xn = _layernorm(x, axis=-1)
    s = _L0_attn_ref(xn, L0_attn_W_in, L0_attn_conv_w, L0_attn_conv_b, L0_attn_Wx, L0_attn_Wdt, L0_attn_bdt, L0_attn_A_log, L0_attn_D, L0_attn_conv_w_b, L0_attn_conv_b_b, L0_attn_Wx_b, L0_attn_Wdt_b, L0_attn_bdt_b, L0_attn_A_b_log, L0_attn_D_b, L0_attn_W_out)
    g = _silu(_L0_ffn_ref(xn, L0_ffn_Wr, L0_ffn_br, L0_ffn_Wl1, L0_ffn_bl1, L0_ffn_Wl2, L0_ffn_bl2, L0_ffn_biases_N))
    x = x + s * g
    xn = _layernorm(x, axis=-1)
    s = _L1_attn_ref(xn, L1_attn_ln1_g, L1_attn_ln1_b, L1_attn_wq, L1_attn_wk, L1_attn_wv, L1_attn_wo, L1_attn_ln2_g, L1_attn_ln2_b, L1_attn_cms_w1, L1_attn_cms_b1, L1_attn_cms_w2, L1_attn_cms_b2)
    g = _silu(_L1_ffn_ref(xn, L1_ffn_W, L1_ffn_b, L1_ffn_V_r, L1_ffn_C))
    x = x + s * g
    return x

_drawn_inputs = setup_inputs


def setup_inputs(seed=0):
    import zlib

    import numpy as np

    out = dict(_drawn_inputs(seed))
    spreads = {'L0_attn_D': (1.0, 0.2),
     'L0_attn_D_b': (1.0, 0.2),
     'L0_ffn_br': (0.0, 0.1),
     'L0_ffn_bl1': (0.0, 0.1),
     'L0_ffn_bl2': (0.0, 0.1),
     'L0_ffn_biases_N': (0.0, 0.1),
     'L1_attn_ln1_g': (1.0, 0.2),
     'L1_attn_ln1_b': (0.0, 0.1),
     'L1_attn_ln2_g': (1.0, 0.2),
     'L1_attn_ln2_b': (0.0, 0.1),
     'L1_attn_cms_b1': (0.0, 0.1),
     'L1_attn_cms_b2': (0.0, 0.1)}
    factors = {}
    for name, (base, spread) in spreads.items():
        noise = np.random.default_rng([zlib.crc32(name.encode()), seed]).standard_normal(out[name].shape)
        drawn = base * np.exp(spread * noise) if base else spread * noise
        out[name] = jnp.asarray(drawn.astype(out[name].dtype))
    for name, factor in factors.items():
        out[name] = (out[name] * factor).astype(out[name].dtype)
    return out
```

```python
import concourse.bass as bass
from concourse import mybir
from contextlib import ExitStack

P = 128
NB, L, DM = 8, 512, 256
DI, NS, R, KC = 512, 16, 64, 4
NE, HE = 8, 512
NH, HD = 16, 16
LV, HID = 3, 1024
RC = 32
NC = L // P
KD = DM // P
DB = DI // P
SEG = L + 1
EPS = 1e-5

CW = 0
CB = CW + 2 * DB * KC
BD = CB + 2 * DB
SD = BD + 2 * DB
AL = SD + 2 * DB
B1 = AL + 2 * DB * NS
NCOL0 = B1 + NE * 2 * HE // P
G1, O1, G2, O2 = 0, KD, 2 * KD, 3 * KD
C1 = 4 * KD
C2 = C1 + LV * HID // P
NCOL1 = C2 + LV * KD

V0_PER, V1_PER, G0_PER, A0_PER = 29, 14, 2, 4


class Chain:

    def __init__(self, eng, sem, i, per):
        self.eng, self.sem, self.base, self.n = eng, sem, i * per, 0

    def mark(self, ins):
        self.n += 1
        ins.then_inc(self.sem, 1)

    def settle(self):
        self.eng.wait_ge(self.sem, self.base + self.n)

    def link(self, ins):
        self.mark(ins)
        self.settle()


def apart(eng, sem):
    eng.sem_inc(sem, 1)


def bass_mamba_moe_then_linear_attention_mlp(nc, x, w_inT, w_xT, w_dtT, w_outT, cols0, rows0, w_rT, wl1, wl2, bl2,
                                             wqkv, wo, cols1, rows1, cms1, cms2, w_fT, v_r, c_fT, out):
    f32 = mybir.dt.float32
    u32 = mybir.dt.uint32
    ALU = mybir.AluOpType
    ACT = mybir.ActivationFunctionType
    AX = mybir.AxisListType.X

    x1_dram = nc.dram_tensor("x1_scratch", (NB, L, DM), f32, kind="Internal").ap()
    b_dram = nc.dram_tensor("b_scratch", (NS, L), f32, kind="Internal").ap()
    x_v = x.rearrange("b (c p) d -> b p c d", p=P)
    x1_v = x1_dram.rearrange("b (c p) d -> b p c d", p=P)
    out_v = out.rearrange("b (c p) d -> b p c d", p=P)

    ctx = ExitStack()
    with ctx:
        def sb(name, shape, dt=f32, where=ctx):
            return where.enter_context(nc.sbuf_tensor(name, shape, dt))

        def sem(name):
            return ctx.enter_context(nc.semaphore(name))

        bank = [ctx.enter_context(nc.psum_tensor(f"bank{i}", [P, 512], f32)) for i in range(8)]
        ident = sb("ident", [P, P])
        idle = sem("idle")

        lay0 = ExitStack()
        with lay0:
            def s0(name, shape, dt=f32):
                return sb(name, shape, dt, lay0)

            w_in = s0("w_in", [P, KD, 2 * DI])
            w_x = s0("w_x", [P, 2, DB, R + 2 * NS])
            w_dt = s0("w_dt", [R, 2, DI])
            w_out = s0("w_out", [P, DB, DM])
            w_r = s0("w_r", [P, KD, NE])
            cols = s0("cols", [P, NCOL0])
            rows = s0("rows", [P, 2 * NE])
            bl2_sb = s0("bl2_sb", [NE, DM])
            iota = s0("iota", [P, NE])
            w1 = [s0(f"w1_{i}", [P, KD, 2 * HE]) for i in range(2)]
            w2 = [s0(f"w2_{i}", [P, HE // P, DM]) for i in range(2)]
            xs = s0("xs", [P, NC, DM])
            xn = s0("xn", [P, NC, DM])
            xnT = s0("xnT", [P, KD, L])
            xpad = s0("xpad", [P, DB, L + 2 * (KC - 1)])
            zs = s0("zs", [P, DB, L])
            xc = s0("xc", [P, DB, L])
            dt = s0("dt", [P, DB, L])
            u = s0("u", [P, DB, L])
            xdT = s0("xdT", [R + 2 * NS, L])
            ct = s0("ct", [P, NC, NS])
            bb = [s0(f"bb{i}", [P, 4, L]) for i in range(2)]
            dA = [s0(f"dA{i}", [P, DB, SEG]) for i in range(2)]
            dBu = [s0(f"dBu{i}", [P, DB, SEG]) for i in range(2)]
            hs = [s0(f"hs{i}", [P, DB, SEG]) for i in range(2)]
            yacc = s0("yacc", [P, NC, DI])
            ysum = s0("ysum", [P, DB, L])
            moe = s0("moe", [P, NC, DM])
            sa = [s0(f"sa{i}", [P, L]) for i in range(2)]
            hE = s0("hE", [P, HE // P, L])
            st = s0("st", [P, NC, 6])
            mv = s0("mv", [P, NC, 2])
            sd = s0("sd", [P, NC])
            rs = s0("rs", [P, NC])
            rt = s0("rt", [P, 8, NC, NE])
            rti = s0("rti", [P, NC, NE], u32)
            ewT = s0("ewT", [NE, L])
            tmp = hs[0][:, :, 1:]

            w_sem = sem("weights_in")
            setup_v, setup_g, setup_a = sem("setup_v"), sem("setup_g"), sem("setup_a")
            x_in, x1_ready, x1_stored = sem("x_in"), sem("x1_ready"), sem("x1_stored")
            v_chain, g_chain, a_chain = sem("v_chain"), sem("g_chain"), sem("a_chain")
            ln_var, ln_std, xn_ready = sem("ln_var"), sem("ln_std"), sem("xn_ready")
            xnT_ps, xnT_ready = sem("xnT_ps"), sem("xnT_ready")
            inp_ps, inp_ready = sem("inp_ps"), sem("inp_ready")
            rt_ps, rt_shift, rt_exp, ew_ready = sem("rt_ps"), sem("rt_shift"), sem("rt_exp"), sem("ew_ready")
            ewT_ps, ewT_ready, b2_ps, b2_used = sem("ewT_ps"), sem("ewT_ready"), sem("b2_ps"), sem("b2_used")
            conv_done, xc_ready = sem("conv_done"), sem("xc_ready")
            xd_ps, xd_ready = sem("xd_ps"), sem("xd_ready")
            b_stored, b_in = sem("b_stored"), [sem("b_in0"), sem("b_in1")]
            dt_ps, sp_done, dt_ready, y_zero = sem("dt_ps"), sem("sp_done"), sem("dt_ready"), sem("y_zero")
            dA_ready, dBu_ready, scan_done = sem("dA_ready"), sem("dBu_ready"), sem("scan_done")
            hT_ready, hT_used = sem("hT_ready"), sem("hT_used")
            ab_ready, silu_done, hE_ready = sem("ab_ready"), sem("silu_done"), sem("hE_ready")
            l2_ready, l2_used = sem("l2_ready"), sem("l2_used")
            e_in = [sem("expert_in0"), sem("expert_in1")]
            yb_ps, y_ready, o_ps, gate_ready = sem("yb_ps"), sem("y_ready"), sem("o_ps"), sem("gate_ready")
            N_W = 9

            block = lay0.enter_context(nc.Block())

            @block.sync
            def _(sp):
                def load_expert(e):
                    sp.dma_start(w1[e % 2][:, :, :], wl1[e].rearrange("(k p) h -> p k h", p=P)).then_inc(e_in[e % 2], 16)
                    sp.dma_start(w2[e % 2][:, :, :], wl2[e].rearrange("(k p) d -> p k d", p=P)).then_inc(e_in[e % 2], 16)

                sp.dma_start(w_in[:, :, :], w_inT.rearrange("(k p) m -> p k m", p=P)).then_inc(w_sem, 16)
                sp.dma_start(cols[:, :], cols0).then_inc(w_sem, 16)
                sp.dma_start(rows[:, :], rows0.partition_broadcast(P)).then_inc(w_sem, 16)
                sp.dma_start(w_r[:, :, :], w_rT.rearrange("(k p) m -> p k m", p=P)).then_inc(w_sem, 16)
                sp.dma_start(bl2_sb[:, :], bl2).then_inc(w_sem, 16)
                for d in range(2):
                    sp.dma_start(w_x[:, d, :, :], w_xT[d].rearrange("(k p) m -> p k m", p=P)).then_inc(w_sem, 16)
                sp.dma_start(w_dt[:, :, :], w_dtT.rearrange("d r m -> r d m")).then_inc(w_sem, 16)
                sp.dma_start(w_out[:, :, :], w_outT.rearrange("(k p) m -> p k m", p=P)).then_inc(w_sem, 16)
                load_expert(0)
                load_expert(1)
                with sp.Fori(0, NB) as b:
                    sp.dma_start(xs[:, :, :], x_v[b]).then_inc(x_in, 16)
                    for d in range(2):
                        sp.wait_ge(xd_ready, 4 * b + 2 * d + 1)
                        apart(sp, idle)
                        sp.dma_start(b_dram, xdT[R:R + NS, :]).then_inc(b_stored, 16)
                        sp.wait_ge(b_stored, 16 * (2 * b + d + 1))
                        apart(sp, idle)
                        for q in range(2):
                            sp.dma_start(bb[q][:, :, :], b_dram[4 * q:4 * q + 4, :].partition_broadcast(P)).then_inc(b_in[q], 16)
                        for g in range(4):
                            if g < 2:
                                sp.wait_ge(dBu_ready, 32 * b + 16 * d + 4 * g + 4)
                                sp.dma_start(bb[g][:, :, :], b_dram[4 * g + 8:4 * g + 12, :].partition_broadcast(P))\
                                  .then_inc(b_in[g], 16)
                            e = 4 * d + g
                            sp.wait_ge(l2_ready, 32 * b + 4 * e + 4)
                            load_expert((e + 2) % NE)
                        for q in range(2):
                            sp.wait_ge(b_in[q], 16 * (4 * b + 2 * d + 2))
                            apart(sp, idle)
                        sp.wait_ge(dBu_ready, 32 * b + 16 * d + 16)
                        apart(sp, idle)
                    sp.wait_ge(x1_ready, b + 1)
                    sp.dma_start(x1_v[b], xs[:, :, :]).then_inc(x1_stored, 16)
                    sp.wait_ge(x1_stored, 16 * (b + 1))
                    apart(sp, idle)
                for s in e_in:
                    sp.wait_ge(s, 32 * (NB * NE // 2 + 1))

            @block.gpsimd
            def _(pool):
                nc.gpsimd.memset(ident[:, :], 0.0).then_inc(setup_g, 1)
                pool.wait_ge(setup_g, 1)
                nc.gpsimd.affine_select(out=ident[:, :], in_=ident[:, :], compare_op=ALU.not_equal, fill=1.0, base=0,
                                        pattern=[[-1, P]], channel_multiplier=1).then_inc(setup_g, 1)
                for i in range(2):
                    nc.gpsimd.memset(dBu[i][:, :, 0:1], 0.0).then_inc(setup_g, 1)
                nc.gpsimd.iota(iota[:, :], pattern=[[1, NE]], base=0, channel_multiplier=0,
                               allow_small_or_imprecise_dtypes=True).then_inc(setup_g, 1)
                with pool.Fori(0, NB) as b:
                    ch = Chain(pool, g_chain, b, G0_PER)
                    for d in range(2):
                        pool.wait_ge(sp_done, 2 * b + d + 1)
                        ch.link(nc.gpsimd.tensor_tensor(dt[:, :, :], dt[:, :, :], tmp, ALU.add))
                        apart(pool, idle)
                        nc.gpsimd.memset(yacc[:, :, :], 0.0).then_inc(y_zero, 1)
                        nc.gpsimd.tensor_tensor(u[:, :, :], dt[:, :, :], xc[:, :, :], ALU.mult).then_inc(dt_ready, 1)
                        pool.wait_ge(dt_ready, 2 * b + d + 1)
                        for n in range(NS):
                            if n % 4 == 0:
                                pool.wait_ge(b_in[n // 4 % 2], 16 * (4 * b + 2 * d + n // 8 + 1))
                            pool.wait_ge(scan_done, 32 * b + 16 * d + n + 1)
                            row = bb[n // 4 % 2][:, n % 4:n % 4 + 1, :].broadcast_to([P, DB, L])
                            nc.gpsimd.tensor_tensor(dBu[n % 2][:, :, 1:], u[:, :, :], row, ALU.mult).then_inc(dBu_ready, 1)

            @block.scalar
            def _(act):
                act.wait_ge(w_sem, 16 * N_W)
                a_cols = cols[:, AL:AL + 2 * DB * NS]
                nc.scalar.activation(a_cols, a_cols, ACT.Exp).then_inc(setup_a, 1)
                act.wait_ge(setup_v, 1)
                with act.Fori(0, NB) as b:
                    ch = Chain(act, a_chain, b, A0_PER)
                    act.wait_ge(ln_var, b + 1)
                    nc.scalar.activation(sd[:, :], rs[:, :], ACT.Sqrt).then_inc(ln_std, 1)
                    for k in range(KD):
                        act.wait_ge(xnT_ps, KD * b + k + 1)
                        nc.scalar.activation(xnT[:, k, :], bank[k][:, :], ACT.Copy).then_inc(xnT_ready, 1)
                    for m in range(2 * DB):
                        act.wait_ge(inp_ps, 8 * b + m + 1)
                        if m < DB:
                            nc.scalar.activation(xpad[:, m, KC - 1:KC - 1 + L], bank[2 + m][:, :], ACT.Copy).then_inc(inp_ready, 1)
                        else:
                            nc.scalar.activation(zs[:, m - DB, :], bank[(2 + m) % 8][:, :], ACT.Silu).then_inc(inp_ready, 1)
                    act.wait_ge(rt_shift, b + 1)
                    nc.scalar.activation(rt[:, 2, :, :], rt[:, 2, :, :], ACT.Exp).then_inc(rt_exp, 1)
                    act.wait_ge(ewT_ps, b + 1)
                    nc.scalar.activation(ewT[:, :], bank[3][0:NE, :], ACT.Copy).then_inc(ewT_ready, 1)
                    for d in range(2):
                        for k in range(DB):
                            act.wait_ge(conv_done, 8 * b + 4 * d + k + 1)
                            nc.scalar.activation(xc[:, k, :], u[:, k, :], ACT.Silu,
                                                 bias=cols[:, CB + 4 * d + k:CB + 4 * d + k + 1]).then_inc(xc_ready, 1)
                        act.wait_ge(xd_ps, 4 * b + 2 * d + 1)
                        nc.scalar.activation(xdT[:, :], bank[6][0:R + 2 * NS, :], ACT.Copy).then_inc(xd_ready, 1)
                        act.wait_ge(xd_ps, 4 * b + 2 * d + 2)
                        nc.scalar.activation(ct[:, :, :], bank[7][:, 0:NC * NS].rearrange("p (c n) -> p c n", n=NS), ACT.Copy)\
                          .then_inc(xd_ready, 1)
                        for k in range(DB):
                            act.wait_ge(dt_ps, 8 * b + 4 * d + k + 1)
                            bias = cols[:, BD + 4 * d + k:BD + 4 * d + k + 1]
                            nc.scalar.activation(dt[:, k, :], bank[k][:, :], ACT.Relu, bias=bias)
                            last = nc.scalar.activation(tmp[:, k, :], bank[k][:, :], ACT.Abs, bias=bias)
                        ch.link(last)
                        ch.link(nc.scalar.activation(tmp, tmp, ACT.Exp, scale=-1.0))
                        nc.scalar.activation(tmp, tmp, ACT.Ln, bias=1.0).then_inc(sp_done, 1)
                        act.wait_ge(dt_ready, 2 * b + d + 1)
                        with act.Fori(0, 2) as i:
                            for q in range(2):
                                for j in range(4):
                                    step = 32 * b + 16 * d + 8 * i + 4 * q + j
                                    n_col = 8 * i + 4 * q + j
                                    act.wait_ge(scan_done, step + 1)
                                    for k in range(DB):
                                        last = nc.scalar.activation(
                                            dA[j % 2][:, k, 1:], dt[:, k, :], ACT.Exp,
                                            scale=cols[:, bass.ds(AL + (d * DB + k) * NS + n_col, 1)])
                                    last.then_inc(dA_ready, 1)
                                    for t in ((0, 1), (2, 3), (), ())[j]:
                                        e_col = B1 + (4 * d + q) * 8 + 2 * 8 * i + t
                                        act.wait_ge(ab_ready, 32 * b + 16 * d + 8 * i + 4 * q + t + 1)
                                        nc.scalar.activation(sa[t % 2][:, :], bank[4 + 2 * (t % 2)][:, :], ACT.Silu,
                                                             bias=cols[:, bass.ds(e_col, 1)]).then_inc(silu_done, 1)
                    act.wait_ge(l2_used, 32 * b + 32)
                    nc.scalar.activation(xn[:, :, :], moe[:, :, :], ACT.Silu).then_inc(gate_ready, 1)
                    assert ch.n == A0_PER, ch.n

            @block.vector
            def _(dve):
                for i in range(2):
                    nc.vector.memset(dA[i][:, :, 0:1], 0.0).then_inc(scan_done, 1)
                nc.vector.memset(xpad[:, :, 0:KC - 1], 0.0).then_inc(hT_used, 1)
                nc.vector.memset(xpad[:, :, KC - 1 + L:], 0.0).then_inc(hT_used, 1)
                for i in range(2):
                    nc.vector.memset(hs[i][:, :, 0:1], 0.0).then_inc(hT_used, 1)
                dve.wait_ge(hT_used, 4)
                dve.wait_ge(w_sem, 16 * N_W)
                dve.wait_ge(setup_a, 1)
                dve.wait_ge(setup_g, 5)
                a_cols = cols[:, AL:AL + 2 * DB * NS]
                nc.vector.tensor_scalar(a_cols, a_cols, -1.0, None, ALU.mult).then_inc(setup_v, 1)
                with dve.Fori(0, NB) as b:
                    ch = Chain(dve, v_chain, b, V0_PER)
                    dve.wait_ge(x_in, 16 * (b + 1))
                    for c in range(NC):
                        last = nc.vector.bn_stats(st[:, c, :], xs[:, c, :])
                    ch.link(last)
                    apart(dve, idle)
                    for c in range(NC):
                        last = nc.vector.bn_aggr(mv[:, c, :], st[:, c, :])
                    ch.link(last)
                    nc.vector.tensor_scalar(rs[:, :], mv[:, :, 1], EPS, None, ALU.add).then_inc(ln_var, 1)
                    dve.wait_ge(ln_std, b + 1)
                    ch.link(nc.vector.reciprocal(rs[:, :], sd[:, :]))
                    for c in range(NC):
                        last = nc.vector.tensor_scalar(xn[:, c, :], xs[:, c, :], mv[:, c, 0:1], rs[:, c:c + 1],
                                                       ALU.subtract, ALU.mult)
                    last.then_inc(xn_ready, 1)
                    dve.wait_ge(rt_ps, b + 1)
                    pr = bank[2][:, 0:NC * NE].rearrange("p (c e) -> p c e", e=NE)

                    def over_chunks(row):
                        return row.rearrange("p (c e) -> p c e", c=1).broadcast_to([P, NC, NE])

                    def over_experts(col):
                        return col.broadcast_to([P, NC, NE])

                    def tt(o, a, c, op):
                        ch.link(nc.vector.tensor_tensor(o, a, c, op))

                    s, sb_, ex, idxf, m0, m1 = (rt[:, i, :, :] for i in range(6))
                    top = rt[:, 6, :, :]
                    red = rt[:, 7, :, 0:1]
                    tt(s, pr, over_chunks(rows[:, 0:NE]), ALU.add)
                    tt(sb_, s, over_chunks(rows[:, NE:2 * NE]), ALU.add)
                    ch.link(nc.vector.reduce_max(red, s, axis=AX))
                    nc.vector.tensor_tensor(ex, s, over_experts(red), ALU.subtract).then_inc(rt_shift, 1)
                    for c in range(NC):
                        last = nc.vector.max(top[:, c, :], sb_[:, c, :])
                    ch.link(last)
                    apart(dve, idle)
                    for c in range(NC):
                        last = nc.vector.max_index(rti[:, c, :], top[:, c, :], sb_[:, c, :])
                    ch.link(last)
                    ch.link(nc.vector.tensor_copy(idxf, rti[:, :, :]))
                    tt(m0, over_chunks(iota[:, :]), over_experts(idxf[:, :, 0:1]), ALU.is_equal)
                    tt(m1, over_chunks(iota[:, :]), over_experts(idxf[:, :, 1:2]), ALU.is_equal)
                    tt(m0, m0, m1, ALU.add)
                    dve.wait_ge(rt_exp, b + 1)
                    ch.link(nc.vector.reduce_sum(red, ex, axis=AX))
                    ch.link(nc.vector.reciprocal(red, red))
                    tt(ex, ex, over_experts(red), ALU.mult)
                    tt(ex, ex, m0, ALU.mult)
                    ch.link(nc.vector.reduce_sum(red, ex, axis=AX))
                    ch.link(nc.vector.reciprocal(red, red))
                    nc.vector.tensor_tensor(ex, ex, over_experts(red), ALU.mult).then_inc(ew_ready, 1)
                    ew = ex
                    for d in range(2):
                        if d == 0:
                            dve.wait_ge(inp_ready, 8 * b + 4)
                        for t in range(KC):
                            for k in range(DB):
                                at = t if d == 0 else 2 * (KC - 1) - t
                                tap = cols[:, CW + (d * DB + k) * KC + t:CW + (d * DB + k) * KC + t + 1]
                                src = xpad[:, k, at:at + L]
                                if t == 0:
                                    last = nc.vector.tensor_scalar(u[:, k, :], src, tap, None, ALU.mult)
                                else:
                                    last = nc.vector.scalar_tensor_tensor(out=u[:, k, :], in0=src, scalar=tap,
                                                                          in1=u[:, k, :], op0=ALU.mult, op1=ALU.add)
                                if t == KC - 1:
                                    last.then_inc(conv_done, 1)
                            if t < KC - 1:
                                ch.link(last)
                        if d == 0:
                            dve.wait_ge(b2_ps, b + 1)
                            for h in range(2):
                                nc.vector.tensor_copy(moe[:, 2 * h:2 * h + 2, :],
                                                      bank[4 + h][:, :].rearrange("p (c d) -> p c d", d=DM)).then_inc(b2_used, 1)
                            dve.wait_ge(b2_used, 2 * (b + 1))
                        dve.wait_ge(y_zero, 2 * b + d + 1)
                        dve.wait_ge(xd_ready, 4 * b + 2 * d + 2)

                        def weigh(step, j, n_col):
                            for c in range(NC):
                                dve.wait_ge(hT_ready, 4 * step + c + 1)
                                if c == 0:
                                    dve.wait_ge(hT_used, 4 * step + 4)
                                nc.vector.scalar_tensor_tensor(
                                    out=yacc[:, c, :], in0=bank[c][:, :], scalar=ct[:, c, bass.ds(n_col, 1)],
                                    in1=yacc[:, c, :], op0=ALU.mult, op1=ALU.add).then_inc(hT_used, 1)

                        apart(dve, idle)
                        with dve.Fori(0, 2) as i:
                            for q in range(2):
                                for j in range(4):
                                    step = 32 * b + 16 * d + 8 * i + 4 * q + j
                                    gi = 8 * b + 4 * d + 2 * i + q
                                    dve.wait_ge(dA_ready, step + 1)
                                    dve.wait_ge(dBu_ready, step + 1)
                                    flat = [t[j % 2][:, :, :].rearrange("p k l -> p (k l)") for t in (hs, dA, dBu)]
                                    if d == 1:
                                        flat = [t[:, ::-1] for t in flat]
                                    dve.wait_ge(scan_done, step + 2)
                                    nc.vector.tensor_tensor_scan(flat[0], flat[1], flat[2], 0.0, ALU.mult, ALU.add)\
                                      .then_inc(scan_done, 1)
                                    if j > 0 or q > 0:
                                        weigh(step - 1, j, 8 * i + 4 * q + j - 1)
                                    e = 4 * d + q
                                    for t in ((0, 1), (2, 3), (), ())[j]:
                                        dve.wait_ge(silu_done, 4 * gi + t + 1)
                                        nc.vector.scalar_tensor_tensor(
                                            out=hE[:, t, :], in0=bank[5 + 2 * (t % 2)][:, :],
                                            scalar=cols[:, bass.ds(B1 + e * 8 + 16 * i + 4 + t, 1)],
                                            in1=sa[t % 2][:, :], op0=ALU.add, op1=ALU.mult).then_inc(hE_ready, 1)
                                    for c in ((), (), (0, 1), (2, 3))[j]:
                                        dve.wait_ge(l2_ready, 4 * gi + 2 * (c // 2) + 2)
                                        nc.vector.scalar_tensor_tensor(
                                            out=moe[:, c, :], in0=bank[4 + 2 * (c // 2)][:, DM * (c % 2):DM * (c % 2 + 1)],
                                            scalar=ew[:, c, bass.ds(e + 2 * i, 1)],
                                            in1=moe[:, c, :], op0=ALU.mult, op1=ALU.add).then_inc(l2_used, 1)
                                dve.wait_ge(l2_used, 4 * gi + 4)
                                apart(dve, idle)
                            weigh(32 * b + 16 * d + 8 * i + 7, 3, 8 * i + 7)
                        for k in range(DB):
                            dve.wait_ge(yb_ps, 8 * b + 4 * d + k + 1)
                            dst = ysum if d == 0 else xc
                            last = nc.vector.scalar_tensor_tensor(
                                out=dst[:, k, :], in0=xc[:, k, :], scalar=cols[:, SD + 4 * d + k:SD + 4 * d + k + 1],
                                in1=bank[k][:, :], op0=ALU.mult, op1=ALU.add)
                        ch.link(last)
                    ch.link(nc.vector.tensor_tensor(ysum[:, :, :], ysum[:, :, :], xc[:, :, :], ALU.add))
                    nc.vector.scalar_tensor_tensor(out=ysum[:, :, :], in0=ysum[:, :, :], scalar=0.5, in1=zs[:, :, :],
                                                   op0=ALU.mult, op1=ALU.mult).then_inc(y_ready, 1)
                    dve.wait_ge(gate_ready, b + 1)
                    for h in range(2):
                        dve.wait_ge(o_ps, 2 * b + h + 1)
                        ch.link(nc.vector.tensor_tensor(xn[:, 2 * h:2 * h + 2, :], xn[:, 2 * h:2 * h + 2, :],
                                                        bank[4 + h][:, :].rearrange("p (c d) -> p c d", d=DM), ALU.mult))
                    nc.vector.tensor_tensor(xs[:, :, :], xs[:, :, :], xn[:, :, :], ALU.add).then_inc(x1_ready, 1)
                    assert ch.n == V0_PER, ch.n

            @block.tensor
            def _(pe):
                mm = nc.tensor.matmul
                pe.wait_ge(w_sem, 16 * N_W)
                pe.wait_ge(setup_g, 5)
                with pe.Fori(0, NB) as b:
                    pe.wait_ge(xn_ready, b + 1)
                    for k in range(KD):
                        for c in range(NC):
                            last = nc.tensor.transpose(bank[k][:, c * P:(c + 1) * P], xn[:, c, k * P:(k + 1) * P], ident[:, :])
                        last.then_inc(xnT_ps, 1)
                    pe.wait_ge(xnT_ready, KD * (b + 1))
                    for m in range(2 * DB):
                        for k in range(KD):
                            last = mm(bank[(2 + m) % 8][:, :], w_in[:, k, m * P:(m + 1) * P], xnT[:, k, :],
                                      start=(k == 0), stop=(k == KD - 1))
                        last.then_inc(inp_ps, 1)
                    pe.wait_ge(inp_ready, 8 * b + 1)
                    for c in range(NC):
                        for k in range(KD):
                            last = mm(bank[2][:, c * NE:(c + 1) * NE], xnT[:, k, c * P:(c + 1) * P], w_r[:, k, :],
                                      start=(k == 0), stop=(k == KD - 1))
                    last.then_inc(rt_ps, 1)
                    pe.wait_ge(ew_ready, b + 1)
                    pe.wait_ge(inp_ready, 8 * b + 8)
                    for c in range(NC):
                        last = nc.tensor.transpose(bank[3][0:NE, c * P:(c + 1) * P], rt[:, 2, c, :], ident[:, :])
                    last.then_inc(ewT_ps, 1)
                    pe.wait_ge(ewT_ready, b + 1)
                    for c in range(NC):
                        last = mm(bank[4 + c // 2][:, DM * (c % 2):DM * (c % 2 + 1)], ewT[:, c * P:(c + 1) * P], bl2_sb[:, :],
                                  start=True, stop=True)
                    last.then_inc(b2_ps, 1)
                    for d in range(2):
                        pe.wait_ge(xc_ready, 8 * b + 4 * d + 4)
                        for k in range(DB):
                            last = mm(bank[6][0:R + 2 * NS, :], w_x[:, d, k, :], xc[:, k, :], start=(k == 0), stop=(k == DB - 1))
                        last.then_inc(xd_ps, 1)
                        for c in range(NC):
                            for k in range(DB):
                                last = mm(bank[7][:, c * NS:(c + 1) * NS], xc[:, k, c * P:(c + 1) * P], w_x[:, d, k, R + NS:],
                                          start=(k == 0), stop=(k == DB - 1))
                        last.then_inc(xd_ps, 1)
                        pe.wait_ge(xd_ready, 4 * b + 2 * d + 1)
                        for k in range(DB):
                            mm(bank[k][:, :], w_dt[:, d, k * P:(k + 1) * P], xdT[0:R, :], start=True, stop=True).then_inc(dt_ps, 1)
                        pe.wait_ge(sp_done, 2 * b + d + 1)
                        pe.wait_ge(xd_ready, 4 * b + 2 * d + 2)
                        if d == 0:
                            pe.wait_ge(b2_used, 2 * (b + 1))
                        apart(pe, idle)
                        with pe.Fori(0, 2) as i:
                            for q in range(2):
                                gi = 8 * b + 4 * d + 2 * i + q
                                for j in range(4):
                                    step = 4 * gi + j
                                    if j == 0:
                                        pe.wait_ge(e_in[q], 32 * (4 * b + 2 * d + i + 1))
                                    for t in ((0, 1), (2, 3), (), ())[j]:
                                        if t >= 2:
                                            pe.wait_ge(hE_ready, 4 * gi + t - 1)
                                        for half in range(2):
                                            for k in range(KD):
                                                last = mm(bank[4 + 2 * (t % 2) + half][:, :],
                                                          w1[q][:, k, half * HE + t * P:half * HE + (t + 1) * P], xnT[:, k, :],
                                                          start=(k == 0), stop=(k == KD - 1))
                                        last.then_inc(ab_ready, 1)
                                    if j == 2:
                                        pe.wait_ge(hE_ready, 4 * gi + 4)
                                    for c in ((), (), (0, 1), (2, 3))[j]:
                                        for k in range(HE // P):
                                            last = mm(bank[4 + 2 * (c // 2)][:, DM * (c % 2):DM * (c % 2 + 1)],
                                                      hE[:, k, c * P:(c + 1) * P], w2[q][:, k, :],
                                                      start=(k == 0), stop=(k == HE // P - 1))
                                        last.then_inc(l2_ready, 1)
                                    pe.wait_ge(scan_done, step + 3)
                                    for c in range(NC):
                                        pe.wait_ge(hT_used, 4 * step + c + 1)
                                        for k in range(DB):
                                            last = nc.tensor.transpose(bank[c][:, k * P:(k + 1) * P],
                                                                       hs[j % 2][:, k, 1 + c * P:1 + (c + 1) * P], ident[:, :])
                                        last.then_inc(hT_ready, 1)
                                pe.wait_ge(l2_used, 4 * gi + 4)
                                apart(pe, idle)
                        pe.wait_ge(hT_used, 4 * (32 * b + 16 * d + 16) + 4)
                        for k in range(DB):
                            for c in range(NC):
                                last = nc.tensor.transpose(bank[k][:, c * P:(c + 1) * P], yacc[:, c, k * P:(k + 1) * P], ident[:, :])
                            last.then_inc(yb_ps, 1)
                    pe.wait_ge(y_ready, b + 1)
                    for c in range(NC):
                        for k in range(DB):
                            last = mm(bank[4 + c // 2][:, DM * (c % 2):DM * (c % 2 + 1)], ysum[:, k, c * P:(c + 1) * P],
                                      w_out[:, k, :], start=(k == 0), stop=(k == DB - 1))
                        if c % 2:
                            last.then_inc(o_ps, 1)

        lay1 = ExitStack()
        with lay1:
            def s1(name, shape, dt=f32):
                return sb(name, shape, dt, lay1)

            wqkv_sb = s1("wqkv_sb", [P, KD, 3 * DM])
            wo_sb = s1("wo_sb", [P, KD, DM])
            cms1_sb = s1("cms1_sb", [P, LV, KD, HID])
            cms2_sb = s1("cms2_sb", [P, LV, HID // P, DM])
            wf_sb = s1("wf_sb", [P, KD, DM])
            vr_sb = s1("vr_sb", [P, KD, RC])
            cf_sb = s1("cf_sb", [RC, DM])
            cols_sb = s1("cols_sb", [P, NCOL1])
            rows_sb = s1("rows_sb", [P, 2, DM])
            mask = s1("mask", [P, 4, P])
            hmask = s1("hmask", [P, KD, P])
            par = s1("par", [P, 2])
            x1s = s1("x1s", [P, NC, DM])
            xm = s1("xm", [P, NC, DM])
            xh = s1("xh", [P, NC, DM])
            xmT = s1("xmT", [P, KD, L])
            hT = s1("hT", [P, KD, L])
            qT = s1("qT", [P, KD, L])
            kT = [s1(f"kT{i}", [P, KD, L]) for i in range(2)]
            kv = s1("kv", [P, NC, 2 * DM])
            sm = s1("sm", [P, 4, 4, P])
            Ms = s1("Ms", [P, KD, P])
            yt = s1("yt", [P, NC, DM])
            yT = s1("yT", [P, KD, L])
            gl = s1("gl", [P, HID // P, L])
            gt = s1("gt", [P, NC, DM])
            fT = s1("fT", [RC, L])
            st1 = s1("st1", [P, NC, 6])
            mv1 = s1("mv1", [P, NC, 2])
            sd1 = s1("sd1", [P, NC])
            rs1 = s1("rs1", [P, NC])

            w1_sem, set1_g, x1_in, o_ready, o_stored = sem("weights1_in"), sem("set1_g"), sem("x1_in"), sem("o_ready"), sem("o_stored")
            v1_chain, var1, std1, n1_ready = sem("v1_chain"), sem("var1"), sem("std1"), sem("n1_ready")
            bT_ps, bT_ready, qk_ps, q_ready, kv_ps, kv_ready = (sem(n) for n in ("bT_ps", "bT_ready", "qk_ps", "q_ready", "kv_ps", "kv_ready"))
            f_ps, f_ready, g_ps, g_sum, g_done = (sem(n) for n in ("f_ps", "f_ready", "g_ps", "g_sum", "g_done"))
            s_ps, sm_ready, m_ps, m_ready, y_ps, yt_ready = (sem(n) for n in ("s_ps", "sm_ready", "m_ps", "m_ready", "y_ps", "yt_ready"))
            yT_ps, yT_ready, wo_ps, n2_ready = (sem(n) for n in ("yT_ps", "yT_ready", "wo_ps", "n2_ready"))
            hT_ps, hT_in, h_ps, gl_ready, l_ps, l_ready = (sem(n) for n in ("hT_ps", "hT_in", "h_ps", "gl_ready", "l_ps", "l_ready"))
            N_W1 = 10

            block1 = lay1.enter_context(nc.Block())

            @block1.sync
            def _(sp):
                for dst, src in ((wqkv_sb, wqkv), (wo_sb, wo), (wf_sb, w_fT), (vr_sb, v_r)):
                    sp.dma_start(dst[:, :, :], src.rearrange("(k p) m -> p k m", p=P)).then_inc(w1_sem, 16)
                sp.dma_start(cf_sb[:, :], c_fT).then_inc(w1_sem, 16)
                sp.dma_start(cols_sb[:, :], cols1).then_inc(w1_sem, 16)
                sp.dma_start(rows_sb[:, :, :], rows1.partition_broadcast(P)).then_inc(w1_sem, 16)
                for dst, src in ((cms1_sb, cms1), (cms2_sb, cms2)):
                    sp.dma_start(dst[:, :, :, :], src.rearrange("l (k p) m -> p l k m", p=P)).then_inc(w1_sem, 16)
                with sp.Fori(0, NB) as b:
                    sp.dma_start(x1s[:, :, :], x1_v[b]).then_inc(x1_in, 16)
                    sp.wait_ge(o_ready, b + 1)
                    sp.dma_start(out_v[b], x1s[:, :, :]).then_inc(o_stored, 16)
                    sp.wait_ge(o_stored, 16 * (b + 1))
                    apart(sp, idle)

            @block1.gpsimd
            def _(pool):
                def step(ins):
                    count[0] += 1
                    ins.then_inc(set1_g, 1)
                    pool.wait_ge(set1_g, count[0])

                count = [0]
                for t in (mask, hmask, par):
                    step(nc.gpsimd.memset(t[:], 1.0))
                step(nc.gpsimd.affine_select(out=mask[:, :, :], in_=mask[:, :, :], compare_op=ALU.is_ge, fill=0.0, base=0,
                                             pattern=[[0, 4], [1, P]], channel_multiplier=-1))
                heads = hmask[:, :, :].rearrange("p k (h e) -> p k h e", e=HD)
                hp = [[0, KD], [-HD, P // HD], [0, HD]]
                step(nc.gpsimd.affine_select(out=heads, in_=heads, compare_op=ALU.is_ge, fill=0.0, base=0, pattern=hp,
                                             channel_multiplier=1))
                step(nc.gpsimd.affine_select(out=heads, in_=heads, compare_op=ALU.is_ge, fill=0.0, base=HD - 1,
                                             pattern=[[0, KD], [HD, P // HD], [0, HD]], channel_multiplier=-1))
                odd = hmask[:, 0, :].rearrange("p (h o e) -> p o h e", o=2, e=HD)
                for o in range(2):
                    step(nc.gpsimd.tensor_tensor(par[:, o:o + 1], odd[:, o, 0, 0:1], odd[:, o, 1, 0:1], ALU.add))
                    for h in range(2, P // HD // 2):
                        step(nc.gpsimd.tensor_tensor(par[:, o:o + 1], par[:, o:o + 1], odd[:, o, h, 0:1], ALU.add))

            N_SET1 = 6 + 2 * (P // HD // 2 - 1)

            @block1.scalar
            def _(act):
                act.wait_ge(w1_sem, 16 * (N_W1 - 1))
                act.wait_ge(set1_g, N_SET1)
                with act.Fori(0, NB) as b:
                    def col(i):
                        return cols_sb[:, i:i + 1]

                    for n in range(2):
                        act.wait_ge(var1, 3 * b + n + 1)
                        nc.scalar.activation(sd1[:, :], rs1[:, :], ACT.Sqrt).then_inc(std1, 1)
                    for k in range(KD):
                        act.wait_ge(bT_ps, 4 * b + k + 1)
                        nc.scalar.activation(hT[:, k, :], bank[k][:, :], ACT.Identity, bias=col(O1 + k), scale=col(G1 + k))\
                          .then_inc(bT_ready, 1)
                    for k in range(KD):
                        act.wait_ge(bT_ps, 4 * b + KD + k + 1)
                        nc.scalar.activation(xmT[:, k, :], bank[2 + k][:, :], ACT.Copy).then_inc(bT_ready, 1)
                    for k in range(KD):
                        act.wait_ge(qk_ps, 4 * b + k + 1)
                        nc.scalar.activation(qT[:, k, :], bank[4 + k][:, :], ACT.Copy).then_inc(q_ready, 1)
                    for k in range(KD):
                        act.wait_ge(qk_ps, 4 * b + KD + k + 1)
                        for o in range(2):
                            nc.scalar.activation(kT[o][:, k, :], bank[6 + k][:, :], ACT.Copy, scale=par[:, o:o + 1])\
                              .then_inc(q_ready, 1)
                    act.wait_ge(f_ps, b + 1)
                    nc.scalar.activation(fT[:, :], bank[4][0:RC, :], ACT.Copy).then_inc(f_ready, 1)
                    for c in range(NC):
                        act.wait_ge(y_ps, NC * b + c + 1)
                        nc.scalar.activation(yt[:, c, :], bank[4 + c % 2][:, 0:DM], ACT.Copy).then_inc(yt_ready, 1)
                    for k in range(KD):
                        act.wait_ge(yT_ps, KD * b + k + 1)
                        nc.scalar.activation(yT[:, k, :], bank[k][:, :], ACT.Copy).then_inc(yT_ready, 1)
                    act.wait_ge(var1, 3 * b + 3)
                    nc.scalar.activation(sd1[:, :], rs1[:, :], ACT.Sqrt).then_inc(std1, 1)
                    act.wait_ge(g_sum, b + 1)
                    nc.scalar.activation(gt[:, :, :], gt[:, :, :], ACT.Silu).then_inc(g_done, 1)
                    for k in range(KD):
                        act.wait_ge(hT_ps, KD * b + k + 1)
                        nc.scalar.activation(hT[:, k, :], bank[k][:, :], ACT.Identity, bias=col(O2 + k), scale=col(G2 + k))\
                          .then_inc(hT_in, 1)
                    for lv in range(LV):
                        for m in range(HID // P):
                            act.wait_ge(h_ps, 8 * LV * b + 8 * lv + m + 1)
                            if m == 0 and lv > 0:
                                act.wait_ge(l_ps, 2 * LV * b + 2 * lv)
                            nc.scalar.activation(gl[:, m, :], bank[m % 4][:, :], ACT.Gelu_apprx_tanh, bias=col(C1 + 8 * lv + m))\
                              .then_inc(gl_ready, 1)
                        if lv < LV - 1:
                            for k in range(KD):
                                act.wait_ge(l_ps, 2 * LV * b + 2 * lv + k + 1)
                                nc.scalar.activation(hT[:, k, :], bank[4 + k][:, :], ACT.Identity, bias=col(C2 + KD * lv + k))\
                                  .then_inc(l_ready, 1)

            @block1.vector
            def _(dve):
                dve.wait_ge(w1_sem, 16 * (N_W1 - 1))
                dve.wait_ge(set1_g, N_SET1)
                with dve.Fori(0, NB) as b:
                    ch = Chain(dve, v1_chain, b, V1_PER)

                    def norm(dst, src, nth):
                        for c in range(NC):
                            last = nc.vector.bn_stats(st1[:, c, :], src[:, c, :])
                        ch.link(last)
                        apart(dve, idle)
                        for c in range(NC):
                            last = nc.vector.bn_aggr(mv1[:, c, :], st1[:, c, :])
                        ch.link(last)
                        nc.vector.tensor_scalar(rs1[:, :], mv1[:, :, 1], EPS, None, ALU.add).then_inc(var1, 1)
                        dve.wait_ge(std1, 3 * b + nth + 1)
                        ch.link(nc.vector.reciprocal(rs1[:, :], sd1[:, :]))
                        for c in range(NC):
                            last = nc.vector.tensor_scalar(dst[:, c, :], src[:, c, :], mv1[:, c, 0:1], rs1[:, c:c + 1],
                                                           ALU.subtract, ALU.mult)
                        return last

                    dve.wait_ge(x1_in, 16 * (b + 1))
                    ch.link(norm(xm, x1s, 0))
                    norm(xh, xm, 1).then_inc(n1_ready, 1)
                    for c in range(NC):
                        dve.wait_ge(kv_ps, NC * b + c + 1)
                        nc.vector.tensor_copy(kv[:, c, :], bank[c][:, :]).then_inc(kv_ready, 1)
                    for h in range(2):
                        dve.wait_ge(g_ps, 2 * b + h + 1)
                        row = rows_sb[:, 0:1, :].broadcast_to([P, 2, DM])
                        last = nc.vector.tensor_tensor(gt[:, 2 * h:2 * h + 2, :], bank[6 + h][:, :].rearrange("p (c d) -> p c d", d=DM),
                                                       row, ALU.add)
                    last.then_inc(g_sum, 1)
                    for c in range(NC):
                        if c >= 1:
                            dve.wait_ge(m_ps, (NC - 1) * b + c)
                            nc.vector.tensor_tensor(Ms[:, :, :], bank[6][:, 0:DM].rearrange("p (k m) -> p k m", m=P), hmask[:, :, :],
                                                    ALU.mult).then_inc(m_ready, 1)
                        for r in range(4):
                            dve.wait_ge(s_ps, 16 * b + 4 * c + r + 1)
                            if r == 0 and c >= 1:
                                dve.wait_ge(y_ps, NC * b + c)
                            nc.vector.tensor_tensor(sm[:, r, :, :], bank[r][:, :].rearrange("p (h q) -> p h q", q=P), mask[:, :, :],
                                                    ALU.mult).then_inc(sm_ready, 1)
                    for h in range(2):
                        dve.wait_ge(wo_ps, 2 * b + h + 1)
                        last = nc.vector.tensor_tensor(xm[:, 2 * h:2 * h + 2, :], xm[:, 2 * h:2 * h + 2, :],
                                                       bank[2 + h][:, :].rearrange("p (c d) -> p c d", d=DM), ALU.add)
                    ch.link(last)
                    norm(xh, xm, 2).then_inc(n2_ready, 1)
                    dve.wait_ge(n2_ready, b + 1)
                    ch.link(nc.vector.tensor_tensor(xm[:, :, :], xm[:, :, :], rows_sb[:, 1:2, :].broadcast_to([P, NC, DM]), ALU.add))
                    dve.wait_ge(g_done, b + 1)
                    for h in range(2):
                        dve.wait_ge(l_ps, 2 * LV * b + 2 * (LV - 1) + h + 1)
                        last = nc.vector.tensor_tensor(xm[:, 2 * h:2 * h + 2, :], xm[:, 2 * h:2 * h + 2, :],
                                                       bank[4 + h][:, :].rearrange("p (c d) -> p c d", d=DM), ALU.add)
                    ch.link(last)
                    ch.link(nc.vector.tensor_tensor(xm[:, :, :], xm[:, :, :], gt[:, :, :], ALU.mult))
                    nc.vector.tensor_tensor(x1s[:, :, :], x1s[:, :, :], xm[:, :, :], ALU.add).then_inc(o_ready, 1)
                    assert ch.n == V1_PER, ch.n

            @block1.tensor
            def _(pe):
                mm = nc.tensor.matmul
                pe.wait_ge(w1_sem, 16 * (N_W1 - 1))
                with pe.Fori(0, NB) as b:
                    pe.wait_ge(n1_ready, b + 1)
                    for src, at in ((xh, 0), (xm, 2)):
                        for k in range(KD):
                            for c in range(NC):
                                last = nc.tensor.transpose(bank[at + k][:, c * P:(c + 1) * P], src[:, c, k * P:(k + 1) * P], ident[:, :])
                            last.then_inc(bT_ps, 1)
                    pe.wait_ge(bT_ready, 4 * b + KD)
                    for m in range(2 * KD):
                        for k in range(KD):
                            last = mm(bank[4 + m][:, :], wqkv_sb[:, k, m * P:(m + 1) * P], hT[:, k, :], start=(k == 0), stop=(k == KD - 1))
                        last.then_inc(qk_ps, 1)
                    pe.wait_ge(bT_ready, 4 * b + 4)
                    for c in range(NC):
                        for k in range(KD):
                            last = mm(bank[c][:, :], hT[:, k, c * P:(c + 1) * P], wqkv_sb[:, k, DM:], start=(k == 0), stop=(k == KD - 1))
                        last.then_inc(kv_ps, 1)
                    pe.wait_ge(q_ready, 6 * b + 1)
                    for k in range(KD):
                        last = mm(bank[4][0:RC, :], vr_sb[:, k, :], xmT[:, k, :], start=(k == 0), stop=(k == KD - 1))
                    last.then_inc(f_ps, 1)
                    pe.wait_ge(f_ready, b + 1)
                    pe.wait_ge(q_ready, 6 * b + 6)
                    for c in range(NC):
                        dst = bank[6 + c // 2][:, DM * (c % 2):DM * (c % 2 + 1)]
                        for k in range(KD):
                            mm(dst, xmT[:, k, c * P:(c + 1) * P], wf_sb[:, k, :], start=(k == 0), stop=False)
                        last = mm(dst, fT[:, c * P:(c + 1) * P], cf_sb[:, :], start=False, stop=True)
                        if c % 2:
                            last.then_inc(g_ps, 1)
                    for c in range(NC):
                        cs = slice(c * P, (c + 1) * P)
                        if c == 0:
                            pe.wait_ge(kv_ready, NC * (b + 1))
                        else:
                            pe.wait_ge(sm_ready, 16 * b + 4 * c)
                        for r in range(4):
                            for h in range(4):
                                k, o = h // 2, h % 2
                                last = mm(bank[r][:, h * P:(h + 1) * P], kT[o][32 * r:32 * r + 32, k, cs], qT[32 * r:32 * r + 32, k, cs],
                                          start=True, stop=True)
                            last.then_inc(s_ps, 1)
                        if c >= 2:
                            pe.wait_ge(yt_ready, NC * b + c - 1)
                        elif c == 1:
                            pe.wait_ge(f_ready, b + 1)
                        yb = bank[4 + c % 2]
                        if c >= 1:
                            pe.wait_ge(m_ready, (NC - 1) * b + c)
                            for k in range(KD):
                                mm(yb[:, k * P:(k + 1) * P], qT[:, k, cs], Ms[:, k, :], start=(k == 0), stop=False,
                                   skip_group_check=True)
                        for r in range(4):
                            pe.wait_ge(sm_ready, 16 * b + 4 * c + r + 1)
                            for h in range(4):
                                head = 8 * (h // 2) + 2 * r + h % 2
                                last = mm(yb[:, head * HD:(head + 1) * HD], sm[:, r, h, :], kv[:, c, DM + head * HD:DM + (head + 1) * HD],
                                          start=(c == 0 and r == 0 and h == 0), stop=(r == 3 and h == 3), skip_group_check=True)
                        last.then_inc(y_ps, 1)
                        if c < NC - 1:
                            if c == 0:
                                pe.wait_ge(g_sum, b + 1)
                            for k in range(KD):
                                last = mm(bank[6][:, k * P:(k + 1) * P], kv[:, c, k * P:(k + 1) * P],
                                          kv[:, c, DM + k * P:DM + (k + 1) * P], start=(c == 0 and k == 0), stop=True,
                                          skip_group_check=True)
                            last.then_inc(m_ps, 1)
                    pe.wait_ge(yt_ready, NC * (b + 1))
                    for k in range(KD):
                        for c in range(NC):
                            last = nc.tensor.transpose(bank[k][:, c * P:(c + 1) * P], yt[:, c, k * P:(k + 1) * P], ident[:, :])
                        last.then_inc(yT_ps, 1)
                    pe.wait_ge(yT_ready, KD * (b + 1))
                    for c in range(NC):
                        for k in range(KD):
                            last = mm(bank[2 + c // 2][:, DM * (c % 2):DM * (c % 2 + 1)], yT[:, k, c * P:(c + 1) * P], wo_sb[:, k, :],
                                      start=(k == 0), stop=(k == KD - 1))
                        if c % 2:
                            last.then_inc(wo_ps, 1)
                    pe.wait_ge(n2_ready, b + 1)
                    for k in range(KD):
                        for c in range(NC):
                            last = nc.tensor.transpose(bank[k][:, c * P:(c + 1) * P], xh[:, c, k * P:(k + 1) * P], ident[:, :])
                        last.then_inc(hT_ps, 1)
                    pe.wait_ge(hT_in, KD * (b + 1))
                    for lv in range(LV):
                        if lv > 0:
                            pe.wait_ge(l_ready, 2 * (LV - 1) * b + 2 * lv)

                        def second(m):
                            pe.wait_ge(gl_ready, 8 * LV * b + 8 * lv + m + 1)
                            if lv < LV - 1:
                                for k in range(KD):
                                    last = mm(bank[4 + k][:, :], cms2_sb[:, lv, m, k * P:(k + 1) * P], gl[:, m, :],
                                              start=(m == 0), stop=(m == HID // P - 1))
                                    if m == HID // P - 1:
                                        last.then_inc(l_ps, 1)
                            else:
                                for c in range(NC):
                                    last = mm(bank[4 + c // 2][:, DM * (c % 2):DM * (c % 2 + 1)], gl[:, m, c * P:(c + 1) * P],
                                              cms2_sb[:, lv, m, :], start=(m == 0 and c % 2 == 0), stop=(m == HID // P - 1),
                                              skip_group_check=True)
                                    if m == HID // P - 1 and c % 2:
                                        last.then_inc(l_ps, 1)

                        for m in range(HID // P):
                            if m >= 4 or lv > 0:
                                pe.wait_ge(gl_ready, 8 * LV * b + 8 * lv + m - 3)
                            for k in range(KD):
                                last = mm(bank[m % 4][:, :], cms1_sb[:, lv, k, m * P:(m + 1) * P], hT[:, k, :],
                                          start=(k == 0), stop=(k == KD - 1))
                            last.then_inc(h_ps, 1)
                            if m > 0:
                                second(m - 1)
                        second(HID // P - 1)




def kernel(**inputs):
    import numpy as _np
    import concourse.bacc as _bacc
    from concourse import mybir as _mybir
    from concourse.bass_utils import run_bass_kernel_spmd as _run

    a = {k: _np.asarray(v) for k, v in inputs.items()}
    f0, f1 = ("L0_attn_", "L0_ffn_"), ("L1_attn_", "L1_ffn_")

    def columns(v):
        return v.reshape(-1, P).T

    def pair(name, back):
        return a[f0[0] + name], a[f0[0] + back]

    cols0 = _np.concatenate(
        [w[:, 0, :].reshape(DB, P, KC).transpose(1, 0, 2).reshape(P, -1) for w in pair("conv_w", "conv_w_b")]
        + [columns(v) for v in pair("conv_b", "conv_b_b")]
        + [columns(v) for v in pair("bdt", "bdt_b")]
        + [columns(v) for v in pair("D", "D_b")]
        + [v.reshape(DB, P, NS).transpose(1, 0, 2).reshape(P, -1) for v in pair("A_log", "A_b_log")]
        + [columns(a[f0[1] + "bl1"])], axis=1)
    cols1 = _np.concatenate([columns(a[f1[0] + n]) for n in ("ln1_g", "ln1_b", "ln2_g", "ln2_b", "cms_b1", "cms_b2")], axis=1)
    arrays = {
        "x": a[f0[0] + "hidden"], "w_inT": a[f0[0] + "W_in"].T, "w_xT": _np.stack([w.T for w in pair("Wx", "Wx_b")]),
        "w_dtT": _np.stack([w.T for w in pair("Wdt", "Wdt_b")]), "w_outT": a[f0[0] + "W_out"].T, "cols0": cols0,
        "rows0": _np.concatenate([a[f0[1] + "br"], a[f0[1] + "biases_N"]]), "w_rT": a[f0[1] + "Wr"].T,
        "wl1": a[f0[1] + "Wl1"], "wl2": a[f0[1] + "Wl2"], "bl2": a[f0[1] + "bl2"],
        "wqkv": _np.concatenate([a[f1[0] + n] for n in ("wq", "wk", "wv")], axis=1), "wo": a[f1[0] + "wo"], "cols1": cols1,
        "rows1": _np.stack([a[f1[1] + "b"], a[f1[0] + "cms_b2"][LV - 1]]),
        "cms1": a[f1[0] + "cms_w1"], "cms2": a[f1[0] + "cms_w2"], "w_fT": a[f1[1] + "W"].T, "v_r": a[f1[1] + "V_r"],
        "c_fT": a[f1[1] + "C"].T,
    }
    arrays = {k: _np.ascontiguousarray(v) for k, v in arrays.items()}
    nc = _bacc.Bacc("TRN2", target_bir_lowering=False, num_devices=1)
    args = [nc.dram_tensor(k, v.shape, _mybir.dt.from_np(v.dtype), kind="ExternalInput").ap() for k, v in arrays.items()]
    args.append(nc.dram_tensor("out", (NB, L, DM), _mybir.dt.float32, kind="ExternalOutput").ap())
    bass_mamba_moe_then_linear_attention_mlp(nc, *args)
    r = _run(nc, [arrays], core_ids=[0])
    return r.results[0]["out"]
```

```python
import concourse.bass as bass
from concourse import mybir
from contextlib import ExitStack

P = 128
NB, L, DM = 8, 512, 256
DI, NS, R, KC = 512, 16, 64, 4
NE, HE = 8, 512
NH, HD = 16, 16
LV, HID = 3, 1024
RC = 32
NC = L // P
TC = NB * NC
KD = DM // P
DB = DI // P
HB = HE // P
SEG = L + 1
EPS = 1e-5
RING = 2
TPB = -(-(2 * TC + NE - 1) // (NB * RING)) * RING
NT = TPB * NB
T0 = (TPB + 1) // 2

CW = 0
CB = CW + 2 * DB * KC
BD = CB + 2 * DB
SD = BD + 2 * DB
AL = SD + 2 * DB
NCOL0 = AL + 2 * DB * NS
G1, O1, G2, O2 = 0, KD, 2 * KD, 3 * KD
C1 = 4 * KD
C2 = C1 + LV * HID // P
NCOL1 = C2 + LV * KD

V1_PER = 20


class Chain:

    def __init__(self, eng, sem, base=0):
        self.eng, self.sem, self.base, self.n = eng, sem, base, 0

    def mark(self, ins):
        self.n += 1
        ins.then_inc(self.sem, 1)

    def link(self, ins):
        self.mark(ins)
        self.eng.wait_ge(self.sem, self.base + self.n)


def apart(eng, sem):
    eng.sem_inc(sem, 1)


def bass_mamba_moe_then_linear_attention_mlp(nc, x, w_inT, w_xT, w_dtT, w_outT, cols0, rows0, w_rT, wl1, bl1c, wl2, bl2,
                                             wqkv, wo, cols1, rows1, cms1, cms2, w_fT, v_r, c_fT, out):
    f32 = mybir.dt.float32
    u32 = mybir.dt.uint32
    i32 = mybir.dt.int32
    ALU = mybir.AluOpType
    ACT = mybir.ActivationFunctionType
    AX = mybir.AxisListType.X

    def scratch(name, shape):
        return nc.dram_tensor(name, shape, f32, kind="Internal").ap()

    xnT_dram = scratch("xnT_scratch", (NB, P, KD, L))
    xg_dram = scratch("xg_scratch", (NT * P, DM))
    yg_dram = scratch("yg_scratch", (NT * P, DM))
    b_dram = scratch("b_scratch", (2, NS, L))
    s_dram = scratch("s_scratch", (NB, P, NC, DM))
    x_v = x.rearrange("b (c p) d -> b p c d", p=P)
    out_v = out.rearrange("b (c p) d -> b p c d", p=P)

    ctx = ExitStack()
    with ctx:
        def sb(name, shape, dt=f32, where=ctx):
            return where.enter_context(nc.sbuf_tensor(name, shape, dt))

        def sem(name):
            return ctx.enter_context(nc.semaphore(name))

        bank = [ctx.enter_context(nc.psum_tensor(f"bank{i}", [P, 512], f32)) for i in range(8)]
        ident = sb("ident", [P, P])
        idle = sem("idle")
        slot = sb("slot", [P, 2, TC], u32)
        share = sb("share", [P, 2, TC])
        owner = sb("owner", [P, NT], i32)

        layR = ExitStack()
        with layR:
            def sr(name, shape, dt=f32):
                return sb(name, shape, dt, layR)

            xa = sr("xa", [P, TC, DM])
            xaT = [sr(f"xaT{i}", [P, KD, L]) for i in range(2)]
            zero = sr("zero", [P, 2048])
            w_r = sr("w_r", [P, KD, NE])
            rows = sr("rows", [P, 2, NE])
            iota_e = sr("iota_e", [P, NE])
            iota_c = sr("iota_c", [P, TC])
            iota_t = sr("iota_t", [P, NT])
            before = sr("before", [P, P])
            ones = sr("ones", [P, P])
            st = sr("st", [P, TC, 6])
            mv = sr("mv", [P, TC, 2])
            sd = sr("sd", [P, TC])
            rs = sr("rs", [P, TC])
            sc, sb_, ex, idxf, m0, m1, ms, top, cum, tmp = (sr(f"rt{i}", [P, TC, NE]) for i in range(10))
            idx = sr("idx", [P, TC, NE], u32)
            red = sr("red", [P, TC, 1])
            cnt, ntl, ends, base = (sr(n, [P, NE, 1]) for n in ("cnt", "ntl", "ends", "base"))
            many = sr("many", [P, NE, TC])
            own = sr("own", [P, NT, NE])
            ownf = sr("ownf", [P, NT, 1])
            posf = sr("posf", [P, TC, 1])

            wr_in = sem("routing_in")
            xa_in = [sem(f"xa_in{b}") for b in range(NB)]
            g0, gz, v0 = sem("routing_consts"), sem("zero_tile"), sem("routing_chain")
            var0, std0, xa_ready, aT_ps, aT_ready, aT_out = (sem(n) for n in ("var0", "std0", "xa_ready", "aT_ps", "aT_ready", "aT_out"))
            sc_ps, shift, exped, chosen, cnt_ps, placed, zeroed, grouped = (
                sem(n) for n in ("sc_ps", "shift", "exped", "chosen", "cnt_ps", "placed", "zeroed", "grouped"))
            aT_outs = [sem("aT_out0"), sem("aT_out1")]
            blockR = layR.enter_context(nc.Block())

            @blockR.sync
            def _(sp):
                for b in range(NB):
                    sp.dma_start(xa[:, NC * b:NC * (b + 1), :], x_v[b]).then_inc(xa_in[b], 16)
                    if b == 0:
                        sp.dma_start(w_r[:, :, :], w_rT.rearrange("(k p) m -> p k m", p=P)).then_inc(wr_in, 16)
                        sp.dma_start(rows[:, :, :], rows0.partition_broadcast(P)).then_inc(wr_in, 16)
                sp.wait_ge(gz, 1)
                flat = xg_dram.rearrange("(p r) d -> p (r d)", p=P)
                per = NT * DM // TPB
                for i in range(TPB):
                    sp.dma_start(flat[:, i * per:(i + 1) * per], zero[:, 0:per]).then_inc(zeroed, 16)
                for b in range(NB):
                    sp.wait_ge(aT_ready, KD * (b + 1))
                    sp.dma_start(xnT_dram[b], xaT[b % 2][:, :, :]).then_inc(aT_outs[b % 2], 16)
                for q in aT_outs:
                    sp.wait_ge(q, 16 * NB // 2)

            @blockR.gpsimd
            def _(pool):
                def step(ins):
                    count[0] += 1
                    ins.then_inc(g0, 1)
                    pool.wait_ge(g0, count[0])

                count = [0]
                nc.gpsimd.memset(zero[:, :], 0.0).then_inc(gz, 1)
                step(nc.gpsimd.memset(ident[:, :], 0.0))
                step(nc.gpsimd.affine_select(out=ident[:, :], in_=ident[:, :], compare_op=ALU.not_equal, fill=1.0, base=0,
                                             pattern=[[-1, P]], channel_multiplier=1))
                step(nc.gpsimd.memset(ones[:, :], 1.0))
                step(nc.gpsimd.affine_select(out=before[:, :], in_=ones[:, :], compare_op=ALU.is_gt, fill=0.0, base=0,
                                             pattern=[[1, P]], channel_multiplier=-1))
                for t, by, n in ((iota_e, 1, NE), (iota_c, P, TC), (iota_t, 1, NT)):
                    step(nc.gpsimd.iota(t[:, :], pattern=[[by, n]], base=0, channel_multiplier=0,
                                        allow_small_or_imprecise_dtypes=True))
                pool.wait_ge(placed, 1)
                pool.wait_ge(zeroed, 16 * TPB)
                for c in range(TC):
                    for k in range(2):
                        nc.gpsimd.indirect_dma_start(
                            out=xg_dram, out_offset=bass.IndirectOffsetOnAxis(slot[:, k, c:c + 1], 0),
                            in_=xa[:, c, :], in_offset=None).then_inc(grouped, 16)
                pool.wait_ge(grouped, 16 * 2 * TC)

            @blockR.scalar
            def _(act):
                for b in range(NB):
                    act.wait_ge(var0, b + 1)
                    nc.scalar.activation(sd[:, NC * b:NC * (b + 1)], rs[:, NC * b:NC * (b + 1)], ACT.Sqrt).then_inc(std0, 1)
                    for k in range(KD):
                        act.wait_ge(aT_ps, KD * b + k + 1)
                        if b >= 2 and k == 0:
                            act.wait_ge(aT_outs[b % 2], 16 * (b // 2))
                        nc.scalar.activation(xaT[b % 2][:, k, :], bank[2 * (b % 2) + k][:, :], ACT.Copy).then_inc(aT_ready, 1)
                act.wait_ge(shift, 1)
                nc.scalar.activation(ex[:, :, :], ex[:, :, :], ACT.Exp).then_inc(exped, 1)

            @blockR.vector
            def _(dve):
                ch = Chain(dve, v0)

                def tt(o, a, c, op):
                    ch.link(nc.vector.tensor_tensor(o, a, c, op))

                for b in range(NB):
                    cs = range(NC * b, NC * (b + 1))
                    dve.wait_ge(xa_in[b], 16)
                    for c in cs:
                        last = nc.vector.bn_stats(st[:, c, :], xa[:, c, :])
                    ch.link(last)
                    for c in cs:
                        last = nc.vector.bn_aggr(mv[:, c, :], st[:, c, :])
                    ch.link(last)
                    nc.vector.tensor_scalar(rs[:, cs[0]:cs[-1] + 1], mv[:, cs[0]:cs[-1] + 1, 1], EPS, None, ALU.add).then_inc(var0, 1)
                    dve.wait_ge(std0, b + 1)
                    ch.link(nc.vector.reciprocal(rs[:, cs[0]:cs[-1] + 1], sd[:, cs[0]:cs[-1] + 1]))
                    for c in cs:
                        last = nc.vector.tensor_scalar(xa[:, c, :], xa[:, c, :], mv[:, c, 0:1], rs[:, c:c + 1],
                                                       ALU.subtract, ALU.mult)
                    last.then_inc(xa_ready, 1)
                dve.wait_ge(g0, 7)
                dve.wait_ge(wr_in, 32)
                dve.wait_ge(sc_ps, 1)
                whole = [P, TC, NE]

                def over_chunks(row):
                    return row.rearrange("p (c e) -> p c e", c=1).broadcast_to(whole)

                tt(sc[:, :, :], bank[7][:, 0:TC * NE].rearrange("p (c e) -> p c e", e=NE), over_chunks(rows[:, 0, :]), ALU.add)
                tt(sb_[:, :, :], sc[:, :, :], over_chunks(rows[:, 1, :]), ALU.add)
                ch.link(nc.vector.reduce_max(red[:, :, :], sc[:, :, :], axis=AX))
                nc.vector.tensor_tensor(ex[:, :, :], sc[:, :, :], red[:, :, :].broadcast_to(whole), ALU.subtract).then_inc(shift, 1)
                for c in range(TC):
                    last = nc.vector.max(top[:, c, :], sb_[:, c, :])
                ch.link(last)
                for c in range(TC):
                    last = nc.vector.max_index(idx[:, c, :], top[:, c, :], sb_[:, c, :])
                ch.link(last)
                ch.link(nc.vector.tensor_copy(idxf[:, :, :], idx[:, :, :]))
                tt(m0[:, :, :], over_chunks(iota_e[:, :]), idxf[:, :, 0:1].broadcast_to(whole), ALU.is_equal)
                tt(m1[:, :, :], over_chunks(iota_e[:, :]), idxf[:, :, 1:2].broadcast_to(whole), ALU.is_equal)
                nc.vector.tensor_tensor(ms[:, :, :], m0[:, :, :], m1[:, :, :], ALU.add).then_inc(chosen, 1)
                dve.wait_ge(cnt_ps, 1)
                totals = bank[6][:, 0:TC * NE].rearrange("p (c e) -> p c e", e=NE)
                ch.link(nc.vector.tensor_copy(tmp[:, :, :], totals))
                for e in range(NE):
                    last = nc.vector.tensor_tensor_scan(cum[:, :, e], ones[:, 0:TC], tmp[:, :, e], 0.0, ALU.mult, ALU.add)
                ch.link(last)
                ch.link(nc.vector.tensor_copy(cnt[:, :, :], cum[:, TC - 1:TC, :].rearrange("p a e -> p e a")))
                tt(many[:, :, :], cnt[:, :, :].broadcast_to([P, NE, TC]),
                   iota_c[:, :].rearrange("p (a c) -> p a c", a=1).broadcast_to([P, NE, TC]), ALU.is_gt)
                ch.link(nc.vector.reduce_sum(ntl[:, :, :], many[:, :, :], axis=AX))
                ch.link(nc.vector.tensor_tensor_scan(ends[:, :, 0], ones[:, 0:NE], ntl[:, :, 0], 0.0, ALU.mult, ALU.add))
                tt(base[:, :, :], ends[:, :, :], ntl[:, :, :], ALU.subtract)
                ch.link(nc.vector.tensor_scalar(base[:, :, :], base[:, :, :], float(P), None, ALU.mult))
                tt(cum[:, :, :], cum[:, :, :], tmp[:, :, :], ALU.subtract)
                tt(cum[:, :, :], cum[:, :, :], bank[5][:, 0:TC * NE].rearrange("p (c e) -> p c e", e=NE), ALU.add)
                tt(cum[:, :, :], cum[:, :, :], base[:, :, 0].rearrange("p (c e) -> p c e", c=1).broadcast_to(whole), ALU.add)
                for k, m in enumerate((m0, m1)):
                    tt(tmp[:, :, :], m[:, :, :], cum[:, :, :], ALU.mult)
                    ch.link(nc.vector.reduce_sum(posf[:, :, :], tmp[:, :, :], axis=AX))
                    last = nc.vector.tensor_copy(slot[:, k, :], posf[:, :, 0])
                    if k == 0:
                        ch.link(last)
                last.then_inc(placed, 1)
                tt(own[:, :, :], ends[:, :, 0].rearrange("p (c e) -> p c e", c=1).broadcast_to([P, NT, NE]),
                   iota_t[:, :].rearrange("p (t a) -> p t a", a=1).broadcast_to([P, NT, NE]), ALU.is_le)
                ch.link(nc.vector.reduce_sum(ownf[:, :, :], own[:, :, :], axis=AX))
                ch.link(nc.vector.tensor_scalar(owner[:, :], ownf[:, :, 0], float(NE - 1), None, ALU.min))
                dve.wait_ge(exped, 1)
                ch.link(nc.vector.reduce_sum(red[:, :, :], ex[:, :, :], axis=AX))
                ch.link(nc.vector.reciprocal(red[:, :, :], red[:, :, :]))
                tt(ex[:, :, :], ex[:, :, :], red[:, :, :].broadcast_to(whole), ALU.mult)
                tt(tmp[:, :, :], ex[:, :, :], ms[:, :, :], ALU.mult)
                ch.link(nc.vector.reduce_sum(red[:, :, :], tmp[:, :, :], axis=AX))
                ch.link(nc.vector.reciprocal(red[:, :, :], red[:, :, :]))
                tt(ex[:, :, :], ex[:, :, :], red[:, :, :].broadcast_to(whole), ALU.mult)
                for k, m in enumerate((m0, m1)):
                    tt(tmp[:, :, :], m[:, :, :], ex[:, :, :], ALU.mult)
                    ch.link(nc.vector.reduce_sum(share[:, k, :].rearrange("p (c a) -> p c a", a=1), tmp[:, :, :], axis=AX))

            @blockR.tensor
            def _(pe):
                pe.wait_ge(g0, 7)
                pe.wait_ge(wr_in, 32)

                def scores(b):
                    for c in range(NC):
                        for k in range(KD):
                            last = nc.tensor.matmul(bank[7][:, (NC * b + c) * NE:(NC * b + c + 1) * NE],
                                                    xaT[b % 2][:, k, c * P:(c + 1) * P], w_r[:, k, :],
                                                    start=(k == 0), stop=(k == KD - 1))
                    return last

                for b in range(NB):
                    pe.wait_ge(xa_ready, b + 1)
                    for k in range(KD):
                        for c in range(NC):
                            last = nc.tensor.transpose(bank[2 * (b % 2) + k][:, c * P:(c + 1) * P],
                                                       xa[:, NC * b + c, k * P:(k + 1) * P], ident[:, :])
                        last.then_inc(aT_ps, 1)
                    pe.wait_ge(aT_ready, KD * (b + 1))
                    last = scores(b)
                last.then_inc(sc_ps, 1)
                pe.wait_ge(chosen, 1)
                flat = ms[:, :, :].rearrange("p c e -> p (c e)")
                nc.tensor.matmul(bank[5][:, 0:TC * NE], before[:, :], flat, start=True, stop=True)
                nc.tensor.matmul(bank[6][:, 0:TC * NE], ones[:, :], flat, start=True, stop=True).then_inc(cnt_ps, 1)

        lay0 = ExitStack()
        with lay0:
            def s0(name, shape, dt=f32):
                return sb(name, shape, dt, lay0)

            w_in = s0("w_in", [P, KD, 2 * DI])
            w_x = s0("w_x", [P, 2, DB, R + 2 * NS])
            w_dt = s0("w_dt", [R, 2, DI])
            w_out = s0("w_out", [P, DB, DM])
            cols = s0("cols", [P, NCOL0])
            one_row = s0("one_row", [1, P])
            xnT = s0("xnT", [P, KD, L])
            xpad = s0("xpad", [P, DB, L + 2 * (KC - 1)])
            zs = s0("zs", [P, DB, L])
            xc = [s0(f"xc{i}", [P, DB, L]) for i in range(2)]
            dt = [s0(f"dt{i}", [P, DB, L]) for i in range(2)]
            u = [s0(f"u{i}", [P, DB, L]) for i in range(2)]
            xdT = s0("xdT", [R + 2 * NS, L])
            ct = [s0(f"ct{i}", [P, NC, NS]) for i in range(2)]
            bb = [s0(f"bb{i}", [P, 2, L]) for i in range(2)]
            dA = [s0(f"dA{i}", [P, DB, SEG]) for i in range(2)]
            dBu = [s0(f"dBu{i}", [P, DB, SEG]) for i in range(2)]
            hs = [s0(f"hs{i}", [P, DB, SEG]) for i in range(2)]
            yacc = s0("yacc", [P, NC, DI])
            ysum = s0("ysum", [P, DB, L])
            so = s0("so", [P, NC, DM])
            w1 = [s0(f"w1_{i}", [P, KD, 2 * HE]) for i in range(RING)]
            w2 = [s0(f"w2_{i}", [P, HB, DM]) for i in range(RING)]
            b1 = [s0(f"b1_{i}", [P, 2 * HB]) for i in range(RING)]
            b2 = [s0(f"b2_{i}", [1, DM]) for i in range(RING)]
            xg = [s0(f"xg{i}", [P, DM]) for i in range(RING)]
            yg = [s0(f"yg{i}", [P, DM]) for i in range(RING)]
            xgT = s0("xgT", [P, KD, P])
            sa = s0("sa", [P, HB, P])
            hE = s0("hE", [P, HB, P])

            w_sem, setup_v, setup_g, setup_a = sem("weights_in"), sem("setup_v"), sem("setup_g"), sem("setup_a")
            xnT_in, p_ps, p_used = sem("xnT_in"), sem("prep_ps"), sem("prep_used")
            conv_chain, conv_done, xc_ready = sem("conv_chain"), sem("conv_done"), sem("xc_ready")
            b_stored, bb_in = sem("b_stored"), [sem("bb_in0"), sem("bb_in1")]
            a_chain, sp_done, dt_sum, u_ready = sem("a_chain"), sem("sp_done"), sem("dt_sum"), sem("u_ready")
            dA_ready, dBu_ready, scan_done = sem("dA_ready"), sem("dBu_ready"), sem("scan_done")
            hT_ready, hT_used, yb_ps = sem("hT_ready"), sem("hT_used"), sem("yb_ps")
            y0_done, y_chain, y_ready, o_ps, so_ready, so_stored = (sem(n) for n in ("y0_done", "y_chain", "y_ready", "o_ps", "so_ready", "so_stored"))
            e_in = [sem(f"expert_in{i}") for i in range(RING)]
            y_st = [sem(f"yg_stored{i}") for i in range(RING)]
            xgT_ps, xgT_ready, ab_ps, sa_ready, hE_ready, l2_ps, yg_ready = (
                sem(n) for n in ("xgT_ps", "xgT_ready", "ab_ps", "sa_ready", "hE_ready", "l2_ps", "yg_ready"))
            N_W = 6

            PREP = {n: [] for n in range(NS)}
            for k in range(DB):
                PREP[k].append(("proj", k))
                PREP[k + 1].append(("conv", k))
                PREP[k + 2].append(("silu", k))
                PREP[k + 8].append(("dt", k))
            PREP[6].append(("xd", 0))
            PREP[7].append(("c", 0))
            PREP[11].append(("soft", 0))
            USE = {"proj": 0, "xd": 4, "c": 5, "dt": 6}

            def tile_pieces(d):
                out = {n: [] for n in range(NS)}
                for i in range(T0 if d == 0 else TPB - T0):
                    for at, piece in enumerate(("x", "up", "gate", "down")):
                        out[3 * i + at].append((piece, i + d * T0))
                return out

            def units(b, last):
                for d in range(2):
                    yield d, 2 * b + d, tile_pieces(d), not (last and d == 1)

            def batches(eng, body):
                with eng.Fori(0, NB - 1) as b:
                    body(b, False)
                body(NB - 1, True)

            block = lay0.enter_context(nc.Block())

            @block.sync
            def _(sp):
                def load_tile(t, i):
                    r = i % RING
                    e = sp.value_load(owner[0:1, bass.ds(t, 1)], min_val=0, max_val=NE - 1)
                    sp.dma_start(xg[r][:, :], xg_dram[bass.ds(t * P, P), :]).then_inc(e_in[r], 16)
                    sp.dma_start(w1[r][:, :, :], wl1[e].rearrange("(k p) h -> p k h", p=P)).then_inc(e_in[r], 16)
                    sp.dma_start(w2[r][:, :, :], wl2[e].rearrange("(k p) d -> p k d", p=P)).then_inc(e_in[r], 16)
                    sp.dma_start(b1[r][:, :], bl1c[e]).then_inc(e_in[r], 16)
                    sp.dma_start(b2[r][:, :], bl2[bass.ds(e, 1), :]).then_inc(e_in[r], 16)

                def load_pair(d, p):
                    sp.dma_start(bb[p % 2][:, :, :], b_dram[d, 2 * p:2 * p + 2, :].partition_broadcast(P)).then_inc(bb_in[p % 2], 16)

                def store_b(d, unit):
                    sp.wait_ge(p_used, 10 * unit + USE["xd"] + 1)
                    sp.dma_start(b_dram[d], xdT[R:R + NS, :]).then_inc(b_stored, 16)
                    sp.wait_ge(b_stored, 16 * (unit + 1))
                    apart(sp, idle)

                sp.dma_start(xnT[:, :, :], xnT_dram[0]).then_inc(xnT_in, 16)
                sp.dma_start(w_in[:, :, :], w_inT.rearrange("(k p) m -> p k m", p=P)).then_inc(w_sem, 16)
                sp.dma_start(cols[:, :], cols0).then_inc(w_sem, 16)
                for d in range(2):
                    sp.dma_start(w_x[:, d, :, :], w_xT[d].rearrange("(k p) m -> p k m", p=P)).then_inc(w_sem, 16)
                sp.dma_start(w_dt[:, :, :], w_dtT.rearrange("d r m -> r d m")).then_inc(w_sem, 16)
                sp.dma_start(w_out[:, :, :], w_outT.rearrange("(k p) m -> p k m", p=P)).then_inc(w_sem, 16)
                sp.sem_inc(so_stored, 16)
                for q in y_st:
                    sp.sem_inc(q, 16)
                for i in range(RING):
                    load_tile(i, i)
                store_b(0, 0)
                for p in range(2):
                    load_pair(0, p)

                def body(b, last):
                    for d, unit, tiles, more in units(b, last):
                        for n in range(NS):
                            if n == 4 and d == 0 and not last:
                                sp.wait_ge(p_used, 10 * (unit + 1) + DB)
                                sp.dma_start(xnT[:, :, :], xnT_dram[b + 1]).then_inc(xnT_in, 16)
                            if n == 8 and more:
                                store_b(1 - d, unit + 1)
                            for piece, i in tiles[n]:
                                if piece == "down":
                                    t = TPB * b + i
                                    sp.wait_ge(yg_ready, t + 2)
                                    sp.dma_start(yg_dram[bass.ds(t * P, P), :], yg[i % RING][:, :]).then_inc(y_st[i % RING], 16)
                                    if not (last and i + RING >= TPB):
                                        load_tile(t + RING, i)
                            if n % 2 == 0:
                                p = n // 2 + 2
                                if p < NS // 2 or more:
                                    sp.wait_ge(dBu_ready, NS * unit + n + 2)
                                    load_pair(d if p < NS // 2 else 1 - d, p % (NS // 2))
                    sp.wait_ge(so_ready, 2 * b + 2)
                    sp.dma_start(s_dram[b], so[:, :, :]).then_inc(so_stored, 16)

                batches(sp, body)
                sp.wait_ge(so_stored, 16 * (NB + 1))
                for r, q in enumerate(y_st):
                    sp.wait_ge(q, 16 * (1 + len(range(r, TPB, RING)) * NB))

            @block.gpsimd
            def _(pool):
                for i in range(2):
                    nc.gpsimd.memset(dBu[i][:, :, 0:1], 0.0).then_inc(setup_g, 1)
                nc.gpsimd.memset(one_row[:, :], 1.0).then_inc(setup_g, 1)

                def soft(d, unit):
                    pool.wait_ge(sp_done, unit + 1)
                    nc.gpsimd.tensor_tensor(dt[d][:, :, :], dt[d][:, :, :], u[d][:, :, :], ALU.add).then_inc(dt_sum, 1)
                    pool.wait_ge(dt_sum, unit + 1)
                    nc.gpsimd.tensor_tensor(u[d][:, :, :], dt[d][:, :, :], xc[d][:, :, :], ALU.mult).then_inc(u_ready, 1)

                def state(d, unit, n):
                    step = NS * unit + n
                    if n == 0:
                        pool.wait_ge(u_ready, unit + 1)
                    if n % 2 == 0:
                        pool.wait_ge(bb_in[n // 2 % 2], 16 * (4 * unit + n // 4 + 1))
                    pool.wait_ge(scan_done, step + 1)
                    row = bb[n // 2 % 2][:, n % 2:n % 2 + 1, :].broadcast_to([P, DB, L])
                    nc.gpsimd.tensor_tensor(dBu[n % 2][:, :, 1:], u[d][:, :, :], row, ALU.mult).then_inc(dBu_ready, 1)

                def body(b, last):
                    for d, unit, _, more in units(b, last):
                        for n in range(NS):
                            state(d, unit, n)
                            if n == NS - 2 and more:
                                soft(1 - d, unit + 1)

                soft(0, 0)
                batches(pool, body)

            @block.scalar
            def _(act):
                act.wait_ge(w_sem, 16 * N_W)
                a_cols = cols[:, AL:AL + 2 * DB * NS]
                nc.scalar.activation(a_cols, a_cols, ACT.Exp).then_inc(setup_a, 1)
                act.sem_inc(yg_ready, 1)

                def prepare(what, k, d, unit, first=False):
                    use = 10 * unit + USE.get(what, 0) + k
                    if what in USE:
                        act.wait_ge(p_ps, use + 1)
                    if what == "proj":
                        if d == 0:
                            nc.scalar.activation(xpad[:, k, KC - 1:KC - 1 + L], bank[7][:, :], ACT.Copy).then_inc(p_used, 1)
                        else:
                            nc.scalar.activation(zs[:, k, :], bank[7][:, :], ACT.Silu).then_inc(p_used, 1)
                    elif what == "silu":
                        act.wait_ge(conv_done, DB * unit + k + 1)
                        nc.scalar.activation(xc[d][:, k, :], u[d][:, k, :], ACT.Silu,
                                             bias=cols[:, CB + DB * d + k:CB + DB * d + k + 1]).then_inc(xc_ready, 1)
                    elif what == "xd":
                        if not first:
                            act.wait_ge(b_stored, 16 * unit)
                        nc.scalar.activation(xdT[:, :], bank[7][0:R + 2 * NS, :], ACT.Copy).then_inc(p_used, 1)
                    elif what == "c":
                        nc.scalar.activation(ct[d][:, :, :], bank[7][:, 0:NC * NS].rearrange("p (c n) -> p c n", n=NS), ACT.Copy)\
                          .then_inc(p_used, 1)
                    elif what == "dt":
                        bias = cols[:, BD + DB * d + k:BD + DB * d + k + 1]
                        nc.scalar.activation(dt[d][:, k, :], bank[7][:, :], ACT.Relu, bias=bias)
                        nc.scalar.activation(u[d][:, k, :], bank[7][:, :], ACT.Abs, bias=bias).then_inc(p_used, 1)
                    elif what == "soft":
                        act.wait_ge(p_used, 10 * unit + 10)
                        ch = Chain(act, a_chain, unit)
                        ch.link(nc.scalar.activation(u[d][:, :, :], u[d][:, :, :], ACT.Exp, scale=-1.0))
                        nc.scalar.activation(u[d][:, :, :], u[d][:, :, :], ACT.Ln, bias=1.0).then_inc(sp_done, 1)

                def state(d, unit, n):
                    step = NS * unit + n
                    if n == 0:
                        act.wait_ge(dt_sum, unit + 1)
                    act.wait_ge(scan_done, step + 1)
                    for k in range(DB):
                        at = AL + (d * DB + k) * NS + n
                        last = nc.scalar.activation(dA[n % 2][:, k, 1:], dt[d][:, k, :], ACT.Exp, scale=cols[:, at:at + 1])
                    last.then_inc(dA_ready, 1)

                def tile(piece, b, i):
                    t, r = TPB * b + i, i % RING
                    if piece == "x":
                        act.wait_ge(xgT_ps, t + 1)
                        nc.scalar.activation(xgT[:, :, :], bank[6][:, 0:DM].rearrange("p (k t) -> p k t", t=P), ACT.Copy)\
                          .then_inc(xgT_ready, 1)
                    elif piece == "up":
                        act.wait_ge(ab_ps, t + 1)
                        for m in range(HB):
                            last = nc.scalar.activation(sa[:, m, :], bank[4][:, m * P:(m + 1) * P], ACT.Silu, bias=b1[r][:, m:m + 1])
                        last.then_inc(sa_ready, 1)
                    elif piece == "down":
                        act.wait_ge(l2_ps, t + 1)
                        act.wait_ge(y_st[r], 16 * (TPB // RING * b + i // RING + 1))
                        nc.scalar.activation(yg[r][:, :], bank[5][:, 0:DM], ACT.Copy).then_inc(yg_ready, 1)

                def body(b, last):
                    for d, unit, tiles, more in units(b, last):
                        for n in range(NS):
                            for piece, i in tiles[n]:
                                if piece == "down":
                                    tile(piece, b, i)
                            if n + 2 < NS:
                                state(d, unit, n + 2)
                            elif more:
                                state(1 - d, unit + 1, n + 2 - NS)
                            for piece, i in tiles[n]:
                                if piece != "down":
                                    tile(piece, b, i)
                            if more:
                                for what, k in PREP[n]:
                                    prepare(what, k, 1 - d, unit + 1)
                    act.wait_ge(so_stored, 16 * (b + 1))
                    apart(act, idle)
                    for h in range(2):
                        act.wait_ge(o_ps, 2 * b + h + 1)
                        nc.scalar.activation(so[:, 2 * h:2 * h + 2, :], bank[h][:, :].rearrange("p (c d) -> p c d", d=DM), ACT.Copy)\
                          .then_inc(so_ready, 1)

                for n in range(NS):
                    for what, k in PREP[n]:
                        prepare(what, k, 0, 0, True)
                act.wait_ge(setup_v, 1)
                for n in range(2):
                    state(0, 0, n)
                batches(act, body)

            @block.vector
            def _(dve):
                for i in range(2):
                    nc.vector.memset(dA[i][:, :, 0:1], 0.0).then_inc(scan_done, 1)
                nc.vector.memset(xpad[:, :, 0:KC - 1], 0.0).then_inc(hT_used, 1)
                nc.vector.memset(xpad[:, :, KC - 1 + L:], 0.0).then_inc(hT_used, 1)
                for i in range(2):
                    nc.vector.memset(hs[i][:, :, 0:1], 0.0).then_inc(hT_used, 1)
                dve.wait_ge(hT_used, 4)
                dve.wait_ge(w_sem, 16 * N_W)
                dve.wait_ge(setup_a, 1)
                a_cols = cols[:, AL:AL + 2 * DB * NS]
                nc.vector.tensor_scalar(a_cols, a_cols, -1.0, None, ALU.mult).then_inc(setup_v, 1)

                def conv(k, d, unit):
                    if d == 0:
                        dve.wait_ge(p_used, 10 * unit + k + 1)
                    ch = Chain(dve, conv_chain, (DB * unit + k) * (KC - 1))
                    for t in range(KC):
                        at = t if d == 0 else 2 * (KC - 1) - t
                        tap = cols[:, CW + (d * DB + k) * KC + t:CW + (d * DB + k) * KC + t + 1]
                        src = xpad[:, k, at:at + L]
                        if t == 0:
                            ch.link(nc.vector.tensor_scalar(u[d][:, k, :], src, tap, None, ALU.mult))
                        else:
                            ins = nc.vector.scalar_tensor_tensor(out=u[d][:, k, :], in0=src, scalar=tap, in1=u[d][:, k, :],
                                                                 op0=ALU.mult, op1=ALU.add)
                            if t < KC - 1:
                                ch.link(ins)
                    ins.then_inc(conv_done, 1)

                def scan(d, unit, n):
                    step = NS * unit + n
                    dve.wait_ge(dA_ready, step + 1)
                    dve.wait_ge(dBu_ready, step + 1)
                    flat = [t[n % 2][:, :, :].rearrange("p k l -> p (k l)") for t in (hs, dA, dBu)]
                    if d == 1:
                        flat = [t[:, ::-1] for t in flat]
                    dve.wait_ge(scan_done, step + 2)
                    nc.vector.tensor_tensor_scan(flat[0], flat[1], flat[2], 0.0, ALU.mult, ALU.add).then_inc(scan_done, 1)

                def weigh(d, unit, n):
                    step = NS * unit + n
                    if n == 0:
                        dve.wait_ge(p_used, 10 * unit + USE["c"] + 1)
                    for c in range(NC):
                        dve.wait_ge(hT_ready, 4 * step + c + 1)
                        if c == 0:
                            dve.wait_ge(hT_used, 4 * step + 4)
                        if n == 0:
                            ins = nc.vector.tensor_scalar(yacc[:, c, :], bank[c][:, :], ct[d][:, c, n:n + 1], None, ALU.mult)
                        else:
                            ins = nc.vector.scalar_tensor_tensor(out=yacc[:, c, :], in0=bank[c][:, :], scalar=ct[d][:, c, n:n + 1],
                                                                 in1=yacc[:, c, :], op0=ALU.mult, op1=ALU.add)
                        ins.then_inc(hT_used, 1)

                def gate(b, i):
                    t, r = TPB * b + i, i % RING
                    dve.wait_ge(sa_ready, t + 1)
                    for m in range(HB):
                        last = nc.vector.scalar_tensor_tensor(out=hE[:, m, :], in0=bank[5][:, m * P:(m + 1) * P],
                                                              scalar=b1[r][:, HB + m:HB + m + 1], in1=sa[:, m, :],
                                                              op0=ALU.add, op1=ALU.mult)
                    last.then_inc(hE_ready, 1)

                def finish(d, unit, b):
                    ch = Chain(dve, y_chain, 2 * b)
                    dst = ysum if d == 0 else xc[1]
                    for k in range(DB):
                        dve.wait_ge(yb_ps, DB * unit + k + 1)
                        last = nc.vector.scalar_tensor_tensor(
                            out=dst[:, k, :], in0=xc[d][:, k, :], scalar=cols[:, SD + DB * d + k:SD + DB * d + k + 1],
                            in1=bank[k][:, :], op0=ALU.mult, op1=ALU.add)
                    if d == 0:
                        last.then_inc(y0_done, 1)
                        return
                    ch.link(last)
                    ch.link(nc.vector.tensor_tensor(ysum[:, :, :], ysum[:, :, :], xc[1][:, :, :], ALU.add))
                    nc.vector.scalar_tensor_tensor(out=ysum[:, :, :], in0=ysum[:, :, :], scalar=0.5, in1=zs[:, :, :],
                                                   op0=ALU.mult, op1=ALU.mult).then_inc(y_ready, 1)

                def body(b, last):
                    for d, unit, tiles, more in units(b, last):
                        for n in range(NS):
                            if n + 1 < NS:
                                scan(d, unit, n + 1)
                            elif more:
                                scan(1 - d, unit + 1, 0)
                            for piece, i in tiles[n]:
                                if piece == "gate":
                                    gate(b, i)
                            weigh(d, unit, n)
                            if more:
                                for what, k in PREP[n]:
                                    if what == "conv":
                                        conv(k, 1 - d, unit + 1)
                        finish(d, unit, b)

                for k in range(DB):
                    conv(k, 0, 0)
                scan(0, 0, 0)
                batches(dve, body)

            @block.tensor
            def _(pe):
                mm = nc.tensor.matmul
                pe.wait_ge(w_sem, 16 * N_W)
                pe.wait_ge(setup_g, 3)

                def prepare(what, k, d, unit, b, first=False):
                    if what not in USE:
                        return
                    use = 10 * unit + USE[what] + k
                    if what == "proj":
                        if k == 0 and d == 0:
                            pe.wait_ge(xnT_in, 16 * (b + 1))
                        if not (first and k == 0):
                            pe.wait_ge(p_used, use)
                        at = (d * DB + k) * P
                        for j in range(KD):
                            last = mm(bank[7][:, :], w_in[:, j, at:at + P], xnT[:, j, :], start=(j == 0), stop=(j == KD - 1))
                    elif what == "xd":
                        pe.wait_ge(xc_ready, DB * unit + DB)
                        pe.wait_ge(p_used, use)
                        for j in range(DB):
                            last = mm(bank[7][0:R + 2 * NS, :], w_x[:, d, j, :], xc[d][:, j, :], start=(j == 0), stop=(j == DB - 1))
                    elif what == "c":
                        pe.wait_ge(p_used, use)
                        for c in range(NC):
                            for j in range(DB):
                                last = mm(bank[7][:, c * NS:(c + 1) * NS], xc[d][:, j, c * P:(c + 1) * P], w_x[:, d, j, R + NS:],
                                          start=(j == 0), stop=(j == DB - 1))
                    elif what == "dt":
                        pe.wait_ge(p_used, use)
                        last = mm(bank[7][:, :], w_dt[:, d, k * P:(k + 1) * P], xdT[0:R, :], start=True, stop=True)
                    last.then_inc(p_ps, 1)

                def turn(unit, n):
                    step = NS * unit + n
                    pe.wait_ge(scan_done, step + 3)
                    for c in range(NC):
                        pe.wait_ge(hT_used, 4 * step + c + 1)
                        for k in range(DB):
                            last = nc.tensor.transpose(bank[c][:, k * P:(k + 1) * P], hs[n % 2][:, k, 1 + c * P:1 + (c + 1) * P],
                                                       ident[:, :])
                        last.then_inc(hT_ready, 1)

                def tile(piece, b, i):
                    t, r = TPB * b + i, i % RING
                    if piece == "x":
                        pe.wait_ge(e_in[r], 80 * (TPB // RING * b + i // RING + 1))
                        for k in range(KD):
                            last = nc.tensor.transpose(bank[6][:, k * P:(k + 1) * P], xg[r][:, k * P:(k + 1) * P], ident[:, :])
                        last.then_inc(xgT_ps, 1)
                    elif piece == "up":
                        pe.wait_ge(xgT_ready, t + 1)
                        pe.wait_ge(yg_ready, t + 1)
                        for m in range(2 * HB):
                            for k in range(KD):
                                last = mm(bank[4 + m // HB][:, m % HB * P:(m % HB + 1) * P], w1[r][:, k, m * P:(m + 1) * P], xgT[:, k, :],
                                          start=(k == 0), stop=(k == KD - 1))
                        last.then_inc(ab_ps, 1)
                    elif piece == "down":
                        pe.wait_ge(hE_ready, t + 1)
                        for m in range(HB):
                            mm(bank[5][:, 0:DM], hE[:, m, :], w2[r][:, m, :], start=(m == 0), stop=False)
                        mm(bank[5][:, 0:DM], one_row[:, :], b2[r][:, :], start=False, stop=True).then_inc(l2_ps, 1)

                def body(b, last_batch):
                    for d, unit, tiles, more in units(b, last_batch):
                        for n in range(NS):
                            turn(unit, n)
                            for piece, i in sorted(tiles[n], key=lambda p: p[0] == "x"):
                                tile(piece, b, i)
                            if more:
                                for what, k in PREP[n]:
                                    prepare(what, k, 1 - d, unit + 1, b + d)
                        for k in range(DB):
                            if k == 0:
                                pe.wait_ge(hT_used, 4 * NS * (unit + 1) + 4)
                            for c in range(NC):
                                last = nc.tensor.transpose(bank[k][:, c * P:(c + 1) * P], yacc[:, c, k * P:(k + 1) * P], ident[:, :])
                            last.then_inc(yb_ps, 1)
                        if d == 0:
                            pe.wait_ge(y0_done, b + 1)
                            apart(pe, idle)
                    pe.wait_ge(y_ready, b + 1)
                    for c in range(NC):
                        for k in range(DB):
                            last = mm(bank[c // 2][:, DM * (c % 2):DM * (c % 2 + 1)], ysum[:, k, c * P:(c + 1) * P],
                                      w_out[:, k, :], start=(k == 0), stop=(k == DB - 1))
                        if c % 2:
                            last.then_inc(o_ps, 1)
                    pe.wait_ge(so_ready, 2 * b + 2)
                    apart(pe, idle)

                for n in range(NS):
                    for what, k in PREP[n]:
                        prepare(what, k, 0, 0, 0, True)
                batches(pe, body)

        lay1 = ExitStack()
        with lay1:
            def s1(name, shape, dt=f32):
                return sb(name, shape, dt, lay1)

            wqkv_sb = s1("wqkv_sb", [P, KD, 3 * DM])
            wo_sb = s1("wo_sb", [P, KD, DM])
            cms1_sb = s1("cms1_sb", [P, LV, KD, HID])
            cms2_sb = s1("cms2_sb", [P, LV, HID // P, DM])
            wf_sb = s1("wf_sb", [P, KD, DM])
            vr_sb = s1("vr_sb", [P, KD, RC])
            cf_sb = s1("cf_sb", [RC, DM])
            cols_sb = s1("cols_sb", [P, NCOL1])
            rows_sb = s1("rows_sb", [P, 2, DM])
            mask = s1("mask", [P, 4, P])
            hmask = s1("hmask", [P, KD, P])
            par = s1("par", [P, 2])
            x1s = s1("x1s", [P, NC, DM])
            xm = s1("xm", [P, NC, DM])
            xh = s1("xh", [P, NC, DM])
            xmT = s1("xmT", [P, KD, L])
            hT = s1("hT", [P, KD, L])
            qT = s1("qT", [P, KD, L])
            kT = [s1(f"kT{i}", [P, KD, L]) for i in range(2)]
            kv = s1("kv", [P, NC, 2 * DM])
            sm = s1("sm", [P, 4, 4, P])
            Ms = s1("Ms", [P, KD, P])
            yt = s1("yt", [P, NC, DM])
            yT = s1("yT", [P, KD, L])
            gl = s1("gl", [P, HID // P, L])
            gt = s1("gt", [P, NC, DM])
            fT = s1("fT", [RC, L])
            st1 = s1("st1", [P, NC, 6])
            mv1 = s1("mv1", [P, NC, 2])
            ya = s1("ya", [P, NC, DM])
            yb = s1("yb", [P, NC, DM])
            cur = s1("cur", [P, 2, NC], u32)
            sd1 = s1("sd1", [P, NC])
            rs1 = s1("rs1", [P, NC])

            w1_sem, set1_g, x1_in, o_ready, o_stored = sem("weights1_in"), sem("set1_g"), sem("x1_in"), sem("o_ready"), sem("o_stored")
            v1_chain, var1, std1, n1_ready = sem("v1_chain"), sem("var1"), sem("std1"), sem("n1_ready")
            bT_ps, bT_ready, qk_ps, q_ready, kv_ps, kv_ready = (sem(n) for n in ("bT_ps", "bT_ready", "qk_ps", "q_ready", "kv_ps", "kv_ready"))
            f_ps, f_ready, g_ps, g_sum, g_done = (sem(n) for n in ("f_ps", "f_ready", "g_ps", "g_sum", "g_done"))
            s_ps, sm_ready, m_ps, m_ready, y_ps, yt_ready = (sem(n) for n in ("s_ps", "sm_ready", "m_ps", "m_ready", "y_ps", "yt_ready"))
            yT_ps, yT_ready, wo_ps, n2_ready = (sem(n) for n in ("yT_ps", "yT_ready", "wo_ps", "n2_ready"))
            hT_ps, hT_in, h_ps, gl_ready, l_ps, l_ready = (sem(n) for n in ("hT_ps", "hT_in", "h_ps", "gl_ready", "l_ps", "l_ready"))
            cur_ready = sem("cur_ready")
            y_in, moe_sum, moe_gate = sem("y_in"), sem("moe_sum"), sem("moe_gate")
            N_W1 = 10

            block1 = lay1.enter_context(nc.Block())

            @block1.sync
            def _(sp):
                for dst, src in ((wqkv_sb, wqkv), (wo_sb, wo), (wf_sb, w_fT), (vr_sb, v_r)):
                    sp.dma_start(dst[:, :, :], src.rearrange("(k p) m -> p k m", p=P)).then_inc(w1_sem, 16)
                sp.dma_start(cf_sb[:, :], c_fT).then_inc(w1_sem, 16)
                sp.dma_start(cols_sb[:, :], cols1).then_inc(w1_sem, 16)
                sp.dma_start(rows_sb[:, :, :], rows1.partition_broadcast(P)).then_inc(w1_sem, 16)
                for dst, src in ((cms1_sb, cms1), (cms2_sb, cms2)):
                    sp.dma_start(dst[:, :, :, :], src.rearrange("l (k p) m -> p l k m", p=P)).then_inc(w1_sem, 16)
                with sp.Fori(0, NB) as b:
                    sp.dma_start(x1s[:, :, :], x_v[b]).then_inc(x1_in, 16)
                    sp.dma_start(gt[:, :, :], s_dram[b]).then_inc(x1_in, 16)
                    sp.wait_ge(o_ready, b + 1)
                    sp.dma_start(out_v[b], x1s[:, :, :]).then_inc(o_stored, 16)
                    sp.wait_ge(o_stored, 16 * (b + 1))
                    apart(sp, idle)

            @block1.gpsimd
            def _(pool):
                def step(ins):
                    count[0] += 1
                    ins.then_inc(set1_g, 1)
                    pool.wait_ge(set1_g, count[0])

                count = [0]
                for t in (mask, hmask, par):
                    step(nc.gpsimd.memset(t[:], 1.0))
                step(nc.gpsimd.affine_select(out=mask[:, :, :], in_=mask[:, :, :], compare_op=ALU.is_ge, fill=0.0, base=0,
                                             pattern=[[0, 4], [1, P]], channel_multiplier=-1))
                heads = hmask[:, :, :].rearrange("p k (h e) -> p k h e", e=HD)
                hp = [[0, KD], [-HD, P // HD], [0, HD]]
                step(nc.gpsimd.affine_select(out=heads, in_=heads, compare_op=ALU.is_ge, fill=0.0, base=0, pattern=hp,
                                             channel_multiplier=1))
                step(nc.gpsimd.affine_select(out=heads, in_=heads, compare_op=ALU.is_ge, fill=0.0, base=HD - 1,
                                             pattern=[[0, KD], [HD, P // HD], [0, HD]], channel_multiplier=-1))
                odd = hmask[:, 0, :].rearrange("p (h o e) -> p o h e", o=2, e=HD)
                for o in range(2):
                    step(nc.gpsimd.tensor_tensor(par[:, o:o + 1], odd[:, o, 0, 0:1], odd[:, o, 1, 0:1], ALU.add))
                    for h in range(2, P // HD // 2):
                        step(nc.gpsimd.tensor_tensor(par[:, o:o + 1], par[:, o:o + 1], odd[:, o, h, 0:1], ALU.add))

                with pool.Fori(0, NB) as b:
                    nc.gpsimd.tensor_copy(cur[:, :, :], slot[:, :, bass.ds(NC * b, NC)]).then_inc(cur_ready, 1)
                    pool.wait_ge(cur_ready, b + 1)
                    apart(pool, idle)
                    for c in range(NC):
                        for k, dst in enumerate((ya, yb)):
                            nc.gpsimd.indirect_dma_start(
                                out=dst[:, c, :], out_offset=None, in_=yg_dram,
                                in_offset=bass.IndirectOffsetOnAxis(cur[:, k, c:c + 1], 0)).then_inc(y_in, 16)
                    pool.wait_ge(moe_sum, b + 1)
                    apart(pool, idle)

            N_SET1 = 6 + 2 * (P // HD // 2 - 1)

            @block1.scalar
            def _(act):
                act.wait_ge(w1_sem, 16 * (N_W1 - 1))
                act.wait_ge(set1_g, N_SET1)
                with act.Fori(0, NB) as b:
                    def col(i):
                        return cols_sb[:, i:i + 1]

                    act.wait_ge(moe_sum, b + 1)
                    nc.scalar.activation(xh[:, :, :], xh[:, :, :], ACT.Silu).then_inc(moe_gate, 1)
                    for n in range(2):
                        act.wait_ge(var1, 3 * b + n + 1)
                        nc.scalar.activation(sd1[:, :], rs1[:, :], ACT.Sqrt).then_inc(std1, 1)
                    for k in range(KD):
                        act.wait_ge(bT_ps, 4 * b + k + 1)
                        nc.scalar.activation(hT[:, k, :], bank[k][:, :], ACT.Identity, bias=col(O1 + k), scale=col(G1 + k))\
                          .then_inc(bT_ready, 1)
                    for k in range(KD):
                        act.wait_ge(bT_ps, 4 * b + KD + k + 1)
                        nc.scalar.activation(xmT[:, k, :], bank[2 + k][:, :], ACT.Copy).then_inc(bT_ready, 1)
                    for k in range(KD):
                        act.wait_ge(qk_ps, 4 * b + k + 1)
                        nc.scalar.activation(qT[:, k, :], bank[4 + k][:, :], ACT.Copy).then_inc(q_ready, 1)
                    for k in range(KD):
                        act.wait_ge(qk_ps, 4 * b + KD + k + 1)
                        for o in range(2):
                            nc.scalar.activation(kT[o][:, k, :], bank[6 + k][:, :], ACT.Copy, scale=par[:, o:o + 1])\
                              .then_inc(q_ready, 1)
                    act.wait_ge(f_ps, b + 1)
                    nc.scalar.activation(fT[:, :], bank[4][0:RC, :], ACT.Copy).then_inc(f_ready, 1)
                    for c in range(NC):
                        act.wait_ge(y_ps, NC * b + c + 1)
                        nc.scalar.activation(yt[:, c, :], bank[4 + c % 2][:, 0:DM], ACT.Copy).then_inc(yt_ready, 1)
                    for k in range(KD):
                        act.wait_ge(yT_ps, KD * b + k + 1)
                        nc.scalar.activation(yT[:, k, :], bank[k][:, :], ACT.Copy).then_inc(yT_ready, 1)
                    act.wait_ge(var1, 3 * b + 3)
                    nc.scalar.activation(sd1[:, :], rs1[:, :], ACT.Sqrt).then_inc(std1, 1)
                    act.wait_ge(g_sum, b + 1)
                    nc.scalar.activation(gt[:, :, :], gt[:, :, :], ACT.Silu).then_inc(g_done, 1)
                    for k in range(KD):
                        act.wait_ge(hT_ps, KD * b + k + 1)
                        nc.scalar.activation(hT[:, k, :], bank[k][:, :], ACT.Identity, bias=col(O2 + k), scale=col(G2 + k))\
                          .then_inc(hT_in, 1)
                    for lv in range(LV):
                        for m in range(HID // P):
                            act.wait_ge(h_ps, 8 * LV * b + 8 * lv + m + 1)
                            if m == 0 and lv > 0:
                                act.wait_ge(l_ps, 2 * LV * b + 2 * lv)
                            nc.scalar.activation(gl[:, m, :], bank[m % 4][:, :], ACT.Gelu_apprx_tanh, bias=col(C1 + 8 * lv + m))\
                              .then_inc(gl_ready, 1)
                        if lv < LV - 1:
                            for k in range(KD):
                                act.wait_ge(l_ps, 2 * LV * b + 2 * lv + k + 1)
                                nc.scalar.activation(hT[:, k, :], bank[4 + k][:, :], ACT.Identity, bias=col(C2 + KD * lv + k))\
                                  .then_inc(l_ready, 1)

            @block1.vector
            def _(dve):
                dve.wait_ge(w1_sem, 16 * (N_W1 - 1))
                dve.wait_ge(set1_g, N_SET1)
                with dve.Fori(0, NB) as b:
                    ch = Chain(dve, v1_chain, V1_PER * b)

                    def norm(dst, src, nth):
                        for c in range(NC):
                            last = nc.vector.bn_stats(st1[:, c, :], src[:, c, :])
                        ch.link(last)
                        apart(dve, idle)
                        for c in range(NC):
                            last = nc.vector.bn_aggr(mv1[:, c, :], st1[:, c, :])
                        ch.link(last)
                        nc.vector.tensor_scalar(rs1[:, :], mv1[:, :, 1], EPS, None, ALU.add).then_inc(var1, 1)
                        dve.wait_ge(std1, 3 * b + nth + 1)
                        ch.link(nc.vector.reciprocal(rs1[:, :], sd1[:, :]))
                        for c in range(NC):
                            last = nc.vector.tensor_scalar(dst[:, c, :], src[:, c, :], mv1[:, c, 0:1], rs1[:, c:c + 1],
                                                           ALU.subtract, ALU.mult)
                        return last

                    dve.wait_ge(x1_in, 32 * (b + 1))
                    for c in range(NC):
                        dve.wait_ge(y_in, 16 * 2 * NC * (b + 1))
                        ch.link(nc.vector.tensor_scalar(xh[:, c, :], ya[:, c, :], share[:, 0, bass.ds(NC * b + c, 1)], None, ALU.mult))
                        last = nc.vector.scalar_tensor_tensor(out=xh[:, c, :], in0=yb[:, c, :], scalar=share[:, 1, bass.ds(NC * b + c, 1)],
                                                              in1=xh[:, c, :], op0=ALU.mult, op1=ALU.add)
                    last.then_inc(moe_sum, 1)
                    dve.wait_ge(moe_gate, b + 1)
                    ch.link(nc.vector.tensor_tensor(xh[:, :, :], xh[:, :, :], gt[:, :, :], ALU.mult))
                    ch.link(nc.vector.tensor_tensor(x1s[:, :, :], x1s[:, :, :], xh[:, :, :], ALU.add))
                    ch.link(norm(xm, x1s, 0))
                    norm(xh, xm, 1).then_inc(n1_ready, 1)
                    for c in range(NC):
                        dve.wait_ge(kv_ps, NC * b + c + 1)
                        nc.vector.tensor_copy(kv[:, c, :], bank[c][:, :]).then_inc(kv_ready, 1)
                    for h in range(2):
                        dve.wait_ge(g_ps, 2 * b + h + 1)
                        row = rows_sb[:, 0:1, :].broadcast_to([P, 2, DM])
                        last = nc.vector.tensor_tensor(gt[:, 2 * h:2 * h + 2, :], bank[6 + h][:, :].rearrange("p (c d) -> p c d", d=DM),
                                                       row, ALU.add)
                    last.then_inc(g_sum, 1)
                    for c in range(NC):
                        if c >= 1:
                            dve.wait_ge(m_ps, (NC - 1) * b + c)
                            nc.vector.tensor_tensor(Ms[:, :, :], bank[6][:, 0:DM].rearrange("p (k m) -> p k m", m=P), hmask[:, :, :],
                                                    ALU.mult).then_inc(m_ready, 1)
                        for r in range(4):
                            dve.wait_ge(s_ps, 16 * b + 4 * c + r + 1)
                            if r == 0 and c >= 1:
                                dve.wait_ge(y_ps, NC * b + c)
                            nc.vector.tensor_tensor(sm[:, r, :, :], bank[r][:, :].rearrange("p (h q) -> p h q", q=P), mask[:, :, :],
                                                    ALU.mult).then_inc(sm_ready, 1)
                    for h in range(2):
                        dve.wait_ge(wo_ps, 2 * b + h + 1)
                        last = nc.vector.tensor_tensor(xm[:, 2 * h:2 * h + 2, :], xm[:, 2 * h:2 * h + 2, :],
                                                       bank[2 + h][:, :].rearrange("p (c d) -> p c d", d=DM), ALU.add)
                    ch.link(last)
                    norm(xh, xm, 2).then_inc(n2_ready, 1)
                    dve.wait_ge(n2_ready, b + 1)
                    ch.link(nc.vector.tensor_tensor(xm[:, :, :], xm[:, :, :], rows_sb[:, 1:2, :].broadcast_to([P, NC, DM]), ALU.add))
                    dve.wait_ge(g_done, b + 1)
                    for h in range(2):
                        dve.wait_ge(l_ps, 2 * LV * b + 2 * (LV - 1) + h + 1)
                        last = nc.vector.tensor_tensor(xm[:, 2 * h:2 * h + 2, :], xm[:, 2 * h:2 * h + 2, :],
                                                       bank[4 + h][:, :].rearrange("p (c d) -> p c d", d=DM), ALU.add)
                    ch.link(last)
                    ch.link(nc.vector.tensor_tensor(xm[:, :, :], xm[:, :, :], gt[:, :, :], ALU.mult))
                    nc.vector.tensor_tensor(x1s[:, :, :], x1s[:, :, :], xm[:, :, :], ALU.add).then_inc(o_ready, 1)
                    assert ch.n == V1_PER, ch.n

            @block1.tensor
            def _(pe):
                mm = nc.tensor.matmul
                pe.wait_ge(w1_sem, 16 * (N_W1 - 1))
                with pe.Fori(0, NB) as b:
                    pe.wait_ge(n1_ready, b + 1)
                    for src, at in ((xh, 0), (xm, 2)):
                        for k in range(KD):
                            for c in range(NC):
                                last = nc.tensor.transpose(bank[at + k][:, c * P:(c + 1) * P], src[:, c, k * P:(k + 1) * P], ident[:, :])
                            last.then_inc(bT_ps, 1)
                    pe.wait_ge(bT_ready, 4 * b + KD)
                    for m in range(2 * KD):
                        for k in range(KD):
                            last = mm(bank[4 + m][:, :], wqkv_sb[:, k, m * P:(m + 1) * P], hT[:, k, :], start=(k == 0), stop=(k == KD - 1))
                        last.then_inc(qk_ps, 1)
                    pe.wait_ge(bT_ready, 4 * b + 4)
                    for c in range(NC):
                        for k in range(KD):
                            last = mm(bank[c][:, :], hT[:, k, c * P:(c + 1) * P], wqkv_sb[:, k, DM:], start=(k == 0), stop=(k == KD - 1))
                        last.then_inc(kv_ps, 1)
                    pe.wait_ge(q_ready, 6 * b + 1)
                    for k in range(KD):
                        last = mm(bank[4][0:RC, :], vr_sb[:, k, :], xmT[:, k, :], start=(k == 0), stop=(k == KD - 1))
                    last.then_inc(f_ps, 1)
                    pe.wait_ge(f_ready, b + 1)
                    pe.wait_ge(q_ready, 6 * b + 6)
                    for c in range(NC):
                        dst = bank[6 + c // 2][:, DM * (c % 2):DM * (c % 2 + 1)]
                        for k in range(KD):
                            mm(dst, xmT[:, k, c * P:(c + 1) * P], wf_sb[:, k, :], start=(k == 0), stop=False)
                        last = mm(dst, fT[:, c * P:(c + 1) * P], cf_sb[:, :], start=False, stop=True)
                        if c % 2:
                            last.then_inc(g_ps, 1)
                    for c in range(NC):
                        cs = slice(c * P, (c + 1) * P)
                        if c == 0:
                            pe.wait_ge(kv_ready, NC * (b + 1))
                        else:
                            pe.wait_ge(sm_ready, 16 * b + 4 * c)
                        for r in range(4):
                            for h in range(4):
                                k, o = h // 2, h % 2
                                last = mm(bank[r][:, h * P:(h + 1) * P], kT[o][32 * r:32 * r + 32, k, cs], qT[32 * r:32 * r + 32, k, cs],
                                          start=True, stop=True)
                            last.then_inc(s_ps, 1)
                        if c >= 2:
                            pe.wait_ge(yt_ready, NC * b + c - 1)
                        elif c == 1:
                            pe.wait_ge(f_ready, b + 1)
                        yb = bank[4 + c % 2]
                        if c >= 1:
                            pe.wait_ge(m_ready, (NC - 1) * b + c)
                            for k in range(KD):
                                mm(yb[:, k * P:(k + 1) * P], qT[:, k, cs], Ms[:, k, :], start=(k == 0), stop=False,
                                   skip_group_check=True)
                        for r in range(4):
                            pe.wait_ge(sm_ready, 16 * b + 4 * c + r + 1)
                            for h in range(4):
                                head = 8 * (h // 2) + 2 * r + h % 2
                                last = mm(yb[:, head * HD:(head + 1) * HD], sm[:, r, h, :], kv[:, c, DM + head * HD:DM + (head + 1) * HD],
                                          start=(c == 0 and r == 0 and h == 0), stop=(r == 3 and h == 3), skip_group_check=True)
                        last.then_inc(y_ps, 1)
                        if c < NC - 1:
                            if c == 0:
                                pe.wait_ge(g_sum, b + 1)
                            for k in range(KD):
                                last = mm(bank[6][:, k * P:(k + 1) * P], kv[:, c, k * P:(k + 1) * P],
                                          kv[:, c, DM + k * P:DM + (k + 1) * P], start=(c == 0 and k == 0), stop=True,
                                          skip_group_check=True)
                            last.then_inc(m_ps, 1)
                    pe.wait_ge(yt_ready, NC * (b + 1))
                    for k in range(KD):
                        for c in range(NC):
                            last = nc.tensor.transpose(bank[k][:, c * P:(c + 1) * P], yt[:, c, k * P:(k + 1) * P], ident[:, :])
                        last.then_inc(yT_ps, 1)
                    pe.wait_ge(yT_ready, KD * (b + 1))
                    for c in range(NC):
                        for k in range(KD):
                            last = mm(bank[2 + c // 2][:, DM * (c % 2):DM * (c % 2 + 1)], yT[:, k, c * P:(c + 1) * P], wo_sb[:, k, :],
                                      start=(k == 0), stop=(k == KD - 1))
                        if c % 2:
                            last.then_inc(wo_ps, 1)
                    pe.wait_ge(n2_ready, b + 1)
                    for k in range(KD):
                        for c in range(NC):
                            last = nc.tensor.transpose(bank[k][:, c * P:(c + 1) * P], xh[:, c, k * P:(k + 1) * P], ident[:, :])
                        last.then_inc(hT_ps, 1)
                    pe.wait_ge(hT_in, KD * (b + 1))
                    for lv in range(LV):
                        if lv > 0:
                            pe.wait_ge(l_ready, 2 * (LV - 1) * b + 2 * lv)

                        def second(m):
                            pe.wait_ge(gl_ready, 8 * LV * b + 8 * lv + m + 1)
                            if lv < LV - 1:
                                for k in range(KD):
                                    last = mm(bank[4 + k][:, :], cms2_sb[:, lv, m, k * P:(k + 1) * P], gl[:, m, :],
                                              start=(m == 0), stop=(m == HID // P - 1))
                                    if m == HID // P - 1:
                                        last.then_inc(l_ps, 1)
                            else:
                                for c in range(NC):
                                    last = mm(bank[4 + c // 2][:, DM * (c % 2):DM * (c % 2 + 1)], gl[:, m, c * P:(c + 1) * P],
                                              cms2_sb[:, lv, m, :], start=(m == 0 and c % 2 == 0), stop=(m == HID // P - 1),
                                              skip_group_check=True)
                                    if m == HID // P - 1 and c % 2:
                                        last.then_inc(l_ps, 1)

                        for m in range(HID // P):
                            if m >= 4 or lv > 0:
                                pe.wait_ge(gl_ready, 8 * LV * b + 8 * lv + m - 3)
                            for k in range(KD):
                                last = mm(bank[m % 4][:, :], cms1_sb[:, lv, k, m * P:(m + 1) * P], hT[:, k, :],
                                          start=(k == 0), stop=(k == KD - 1))
                            last.then_inc(h_ps, 1)
                            if m > 0:
                                second(m - 1)
                        second(HID // P - 1)






def kernel(**inputs):
    import numpy as _np
    import concourse.bacc as _bacc
    from concourse import mybir as _mybir
    from concourse.bass_utils import run_bass_kernel_spmd as _run

    a = {k: _np.asarray(v) for k, v in inputs.items()}
    f0, f1 = ("L0_attn_", "L0_ffn_"), ("L1_attn_", "L1_ffn_")

    def columns(v):
        return v.reshape(-1, P).T

    def pair(name, back):
        return a[f0[0] + name], a[f0[0] + back]

    cols0 = _np.concatenate(
        [w[:, 0, :].reshape(DB, P, KC).transpose(1, 0, 2).reshape(P, -1) for w in pair("conv_w", "conv_w_b")]
        + [columns(v) for v in pair("conv_b", "conv_b_b")]
        + [columns(v) for v in pair("bdt", "bdt_b")]
        + [columns(v) for v in pair("D", "D_b")]
        + [v.reshape(DB, P, NS).transpose(1, 0, 2).reshape(P, -1) for v in pair("A_log", "A_b_log")], axis=1)
    cols1 = _np.concatenate([columns(a[f1[0] + n]) for n in ("ln1_g", "ln1_b", "ln2_g", "ln2_b", "cms_b1", "cms_b2")], axis=1)
    arrays = {
        "x": a[f0[0] + "hidden"], "w_inT": a[f0[0] + "W_in"].T, "w_xT": _np.stack([w.T for w in pair("Wx", "Wx_b")]),
        "w_dtT": _np.stack([w.T for w in pair("Wdt", "Wdt_b")]), "w_outT": a[f0[0] + "W_out"].T, "cols0": cols0,
        "rows0": _np.stack([a[f0[1] + "br"], a[f0[1] + "biases_N"]]), "w_rT": a[f0[1] + "Wr"].T,
        "wl1": a[f0[1] + "Wl1"],
        "bl1c": a[f0[1] + "bl1"].reshape(NE, 2 * HB, P).transpose(0, 2, 1), "wl2": a[f0[1] + "Wl2"], "bl2": a[f0[1] + "bl2"],
        "wqkv": _np.concatenate([a[f1[0] + n] for n in ("wq", "wk", "wv")], axis=1), "wo": a[f1[0] + "wo"], "cols1": cols1,
        "rows1": _np.stack([a[f1[1] + "b"], a[f1[0] + "cms_b2"][LV - 1]]),
        "cms1": a[f1[0] + "cms_w1"], "cms2": a[f1[0] + "cms_w2"], "w_fT": a[f1[1] + "W"].T, "v_r": a[f1[1] + "V_r"],
        "c_fT": a[f1[1] + "C"].T,
    }
    arrays = {k: _np.ascontiguousarray(v) for k, v in arrays.items()}
    nc = _bacc.Bacc("TRN2", target_bir_lowering=False, num_devices=1)
    args = [nc.dram_tensor(k, v.shape, _mybir.dt.from_np(v.dtype), kind="ExternalInput").ap() for k, v in arrays.items()]
    args.append(nc.dram_tensor("out", (NB, L, DM), _mybir.dt.float32, kind="ExternalOutput").ap())
    bass_mamba_moe_then_linear_attention_mlp(nc, *args)
    r = _run(nc, [arrays], core_ids=[0])
    return r.results[0]["out"]
```

```python
import concourse.bass as bass
from concourse import mybir
from contextlib import ExitStack

P = 128
NB, L, DM = 8, 512, 256
DI, NS, R, KC = 512, 16, 64, 4
NE, HE = 8, 512
NH, HD = 16, 16
LV, HID = 3, 1024
RX = R + 2 * NS
RC = 32
NC = L // P
TC = NB * NC
KD = DM // P
DB = DI // P
HB = HE // P
SEG = L + 1
EPS = 1e-5
RING = 2
HS = 4
TPB = -(-(2 * TC + NE - 1) // (NB * RING)) * RING
T0 = (TPB + 1) // 2
NT = TPB * NB - T0
assert NT >= 2 * TC + NE - 1

CW = 0
CB = CW + 2 * DB * KC
BD = CB + 2 * DB
SD = BD + 2 * DB
AL = SD + 2 * DB
NCOL0 = AL + 2 * DB * NS
G1, O1, G2, O2 = 0, KD, 2 * KD, 3 * KD
C1 = 4 * KD
C2 = C1 + LV * HID // P
NCOL1 = C2 + LV * KD

LINKS1 = 23


class Chain:

    def __init__(self, eng, sem, base=0):
        self.eng, self.sem, self.base, self.n = eng, sem, base, 0

    def mark(self, ins):
        self.n += 1
        ins.then_inc(self.sem, 1)

    def link(self, ins):
        self.mark(ins)
        self.eng.wait_ge(self.sem, self.base + self.n)


def apart(eng, sem):
    eng.sem_inc(sem, 1)


def bass_mamba_moe_then_linear_attention_mlp(nc, x, w_inT, w_xT, w_dtT, w_outT, cols0, rows0, w_rT, wl1, bl1c, wl2, bl2,
                                             wqkv, wo, cols1, rows1, cms1, cms2, w_fT, v_r, c_fT, out):
    f32 = mybir.dt.float32
    u32 = mybir.dt.uint32
    i32 = mybir.dt.int32
    ALU = mybir.AluOpType
    ACT = mybir.ActivationFunctionType
    AX = mybir.AxisListType.X

    def scratch(name, shape):
        return nc.dram_tensor(name, shape, f32, kind="Internal").ap()

    xnT_dram = scratch("xnT_scratch", (NB, P, KD, L))
    xg_dram = scratch("xg_scratch", (NT * P, DM))
    yg_dram = scratch("yg_scratch", (NT * P, DM))
    b_dram = scratch("b_scratch", (2, NS, L))
    s_dram = scratch("s_scratch", (NB, P, NC, DM))
    x_v = x.rearrange("b (c p) d -> b p c d", p=P)
    out_v = out.rearrange("b (c p) d -> b p c d", p=P)

    ctx = ExitStack()
    with ctx:
        def sb(name, shape, dt=f32, where=ctx):
            return where.enter_context(nc.sbuf_tensor(name, shape, dt))

        def sem(name):
            return ctx.enter_context(nc.semaphore(name))

        bank = [ctx.enter_context(nc.psum_tensor(f"bank{i}", [P, 512], f32)) for i in range(8)]
        ident = sb("ident", [P, P])
        idle = sem("idle")
        slot = sb("slot", [P, 2, TC], u32)
        share = sb("share", [P, 2, TC])
        owner = sb("owner", [P, NT], i32)

        lay0 = ExitStack()

        def s0(name, shape, dt=f32):
            return sb(name, shape, dt, lay0)

        w_in = s0("w_in", [P, KD, 2 * DI])
        w_x = s0("w_x", [P, 2, DB, R + 2 * NS])
        w_dt = s0("w_dt", [R, 2, DI])
        w_out = s0("w_out", [P, DB, DM])
        cols = s0("cols", [P, NCOL0])
        held = s0("held", [P, TC * DM])
        xa = held[:, :].rearrange("p (c d) -> p c d", d=DM)

        def part(at, n, inner):
            return held[:, at:at + n].rearrange("p (k m) -> p k m", m=inner)

        N_W1, N_W2, N_YA = KD * 2 * HE, HB * DM, NC * DI
        assert RING * (N_W1 + N_W2) + N_YA <= TC * DM
        w_sem = sem("weights_in")
        N_W = 6
        placed, zeroed, grouped = sem("placed"), sem("zeroed"), [sem("grouped_early"), sem("grouped_late")]
        EARLY = 22

        layR = ExitStack()
        with layR:
            def sr(name, shape, dt=f32):
                return sb(name, shape, dt, layR)

            xaT = [sr(f"xaT{i}", [P, KD, L]) for i in range(2)]
            zero = sr("zero", [P, 2048])
            w_r = sr("w_r", [P, KD, NE])
            rows = sr("rows", [P, 2, NE])
            iota_e = sr("iota_e", [P, NE])
            iota_c = sr("iota_c", [P, TC])
            iota_t = sr("iota_t", [P, NT])
            before = sr("before", [P, P])
            ones = sr("ones", [P, P])
            st = sr("st", [P, TC, 6])
            mv = sr("mv", [P, TC, 2])
            sd = sr("sd", [P, TC])
            rs = sr("rs", [P, TC])
            sc, sb_, ex, idxf, m0, m1, ms, top, cum, tmp = (sr(f"rt{i}", [P, TC, NE]) for i in range(10))
            idx = sr("idx", [P, TC, NE], u32)
            red = sr("red", [P, TC, 1])
            cnt, ntl, ends, base = (sr(n, [P, NE, 1]) for n in ("cnt", "ntl", "ends", "base"))
            many = sr("many", [P, NE, TC])
            own = sr("own", [P, NT, NE])
            ownf = sr("ownf", [P, NT, 1])
            posf = sr("posf", [P, TC, 1])

            wr_in = sem("routing_in")
            xa_in = [sem(f"xa_in{b}") for b in range(NB)]
            g0, gz, v0 = sem("routing_consts"), sem("zero_tile"), sem("routing_chain")
            var0, std0, xa_ready, aT_ps, aT_ready = (sem(n) for n in ("var0", "std0", "xa_ready", "aT_ps", "aT_ready"))
            sc_ps, shift, exped, chosen, cnt_ps = (sem(n) for n in ("sc_ps", "shift", "exped", "chosen", "cnt_ps"))
            aT_outs = [sem("aT_out0"), sem("aT_out1")]
            blockR = layR.enter_context(nc.Block())

            @blockR.sync
            def _(sp):
                for b in range(NB):
                    sp.dma_start(xa[:, NC * b:NC * (b + 1), :], x_v[b]).then_inc(xa_in[b], 16)
                    if b == 0:
                        sp.dma_start(w_r[:, :, :], w_rT.rearrange("(k p) m -> p k m", p=P)).then_inc(wr_in, 16)
                        sp.dma_start(rows[:, :, :], rows0.partition_broadcast(P)).then_inc(wr_in, 16)
                sp.wait_ge(gz, 1)
                flat = xg_dram.rearrange("(p r) d -> p (r d)", p=P)
                per = NT * DM // TPB
                for i in range(TPB):
                    if i < NB:
                        sp.wait_ge(aT_ready, KD * (i + 1))
                        sp.dma_start(xnT_dram[i], xaT[i % 2][:, :, :]).then_inc(aT_outs[i % 2], 16)
                    sp.dma_start(flat[:, i * per:(i + 1) * per], zero[:, 0:per]).then_inc(zeroed, 16)
                sp.dma_start(w_in[:, :, :], w_inT.rearrange("(k p) m -> p k m", p=P)).then_inc(w_sem, 16)
                sp.dma_start(cols[:, :], cols0).then_inc(w_sem, 16)
                for d in range(2):
                    sp.dma_start(w_x[:, d, :, :], w_xT[d].rearrange("(k p) m -> p k m", p=P)).then_inc(w_sem, 16)
                sp.dma_start(w_dt[:, :, :], w_dtT.rearrange("d r m -> r d m")).then_inc(w_sem, 16)
                sp.dma_start(w_out[:, :, :], w_outT.rearrange("(k p) m -> p k m", p=P)).then_inc(w_sem, 16)
                for q in aT_outs:
                    sp.wait_ge(q, 16 * NB // 2)
                sp.wait_ge(zeroed, 16 * TPB)

            @blockR.gpsimd
            def _(pool):
                def step(ins):
                    count[0] += 1
                    ins.then_inc(g0, 1)
                    pool.wait_ge(g0, count[0])

                count = [0]
                nc.gpsimd.memset(zero[:, :], 0.0).then_inc(gz, 1)
                step(nc.gpsimd.memset(ident[:, :], 0.0))
                step(nc.gpsimd.affine_select(out=ident[:, :], in_=ident[:, :], compare_op=ALU.not_equal, fill=1.0, base=0,
                                             pattern=[[-1, P]], channel_multiplier=1))
                step(nc.gpsimd.memset(ones[:, :], 1.0))
                step(nc.gpsimd.affine_select(out=before[:, :], in_=ones[:, :], compare_op=ALU.is_gt, fill=0.0, base=0,
                                             pattern=[[1, P]], channel_multiplier=-1))
                for t, by, n in ((iota_e, 1, NE), (iota_c, P, TC), (iota_t, 1, NT)):
                    step(nc.gpsimd.iota(t[:, :], pattern=[[by, n]], base=0, channel_multiplier=0,
                                        allow_small_or_imprecise_dtypes=True))

            @blockR.scalar
            def _(act):
                for b in range(NB):
                    act.wait_ge(var0, b + 1)
                    nc.scalar.activation(sd[:, NC * b:NC * (b + 1)], rs[:, NC * b:NC * (b + 1)], ACT.Sqrt).then_inc(std0, 1)
                    for k in range(KD):
                        act.wait_ge(aT_ps, KD * b + k + 1)
                        if b >= 2 and k == 0:
                            act.wait_ge(aT_outs[b % 2], 16 * (b // 2))
                        nc.scalar.activation(xaT[b % 2][:, k, :], bank[2 * (b % 2) + k][:, :], ACT.Copy).then_inc(aT_ready, 1)
                act.wait_ge(shift, 1)
                nc.scalar.activation(ex[:, :, :], ex[:, :, :], ACT.Exp).then_inc(exped, 1)

            @blockR.vector
            def _(dve):
                ch = Chain(dve, v0)

                def tt(o, a, c, op):
                    ch.link(nc.vector.tensor_tensor(o, a, c, op))

                for b in range(NB):
                    cs = range(NC * b, NC * (b + 1))
                    dve.wait_ge(xa_in[b], 16)
                    for c in cs:
                        last = nc.vector.bn_stats(st[:, c, :], xa[:, c, :])
                    ch.link(last)
                    for c in cs:
                        last = nc.vector.bn_aggr(mv[:, c, :], st[:, c, :])
                    ch.link(last)
                    nc.vector.tensor_scalar(rs[:, cs[0]:cs[-1] + 1], mv[:, cs[0]:cs[-1] + 1, 1], EPS, None, ALU.add).then_inc(var0, 1)
                    dve.wait_ge(std0, b + 1)
                    ch.link(nc.vector.reciprocal(rs[:, cs[0]:cs[-1] + 1], sd[:, cs[0]:cs[-1] + 1]))
                    for c in cs:
                        last = nc.vector.tensor_scalar(xa[:, c, :], xa[:, c, :], mv[:, c, 0:1], rs[:, c:c + 1],
                                                       ALU.subtract, ALU.mult)
                    last.then_inc(xa_ready, 1)
                dve.wait_ge(g0, 7)
                dve.wait_ge(wr_in, 32)
                dve.wait_ge(sc_ps, 1)
                whole = [P, TC, NE]

                def over_chunks(row):
                    return row.rearrange("p (c e) -> p c e", c=1).broadcast_to(whole)

                tt(sc[:, :, :], bank[7][:, 0:TC * NE].rearrange("p (c e) -> p c e", e=NE), over_chunks(rows[:, 0, :]), ALU.add)
                tt(sb_[:, :, :], sc[:, :, :], over_chunks(rows[:, 1, :]), ALU.add)
                ch.link(nc.vector.reduce_max(red[:, :, :], sc[:, :, :], axis=AX))
                nc.vector.tensor_tensor(ex[:, :, :], sc[:, :, :], red[:, :, :].broadcast_to(whole), ALU.subtract).then_inc(shift, 1)
                for c in range(TC):
                    last = nc.vector.max(top[:, c, :], sb_[:, c, :])
                ch.link(last)
                for c in range(TC):
                    last = nc.vector.max_index(idx[:, c, :], top[:, c, :], sb_[:, c, :])
                ch.link(last)
                ch.link(nc.vector.tensor_copy(idxf[:, :, :], idx[:, :, :]))
                tt(m0[:, :, :], over_chunks(iota_e[:, :]), idxf[:, :, 0:1].broadcast_to(whole), ALU.is_equal)
                tt(m1[:, :, :], over_chunks(iota_e[:, :]), idxf[:, :, 1:2].broadcast_to(whole), ALU.is_equal)
                nc.vector.tensor_tensor(ms[:, :, :], m0[:, :, :], m1[:, :, :], ALU.add).then_inc(chosen, 1)
                dve.wait_ge(cnt_ps, 1)
                totals = bank[6][:, 0:TC * NE].rearrange("p (c e) -> p c e", e=NE)
                ch.link(nc.vector.tensor_copy(tmp[:, :, :], totals))
                for e in range(NE):
                    last = nc.vector.tensor_tensor_scan(cum[:, :, e], ones[:, 0:TC], tmp[:, :, e], 0.0, ALU.mult, ALU.add)
                ch.link(last)
                ch.link(nc.vector.tensor_copy(cnt[:, :, :], cum[:, TC - 1:TC, :].rearrange("p a e -> p e a")))
                tt(many[:, :, :], cnt[:, :, :].broadcast_to([P, NE, TC]),
                   iota_c[:, :].rearrange("p (a c) -> p a c", a=1).broadcast_to([P, NE, TC]), ALU.is_gt)
                ch.link(nc.vector.reduce_sum(ntl[:, :, :], many[:, :, :], axis=AX))
                ch.link(nc.vector.tensor_tensor_scan(ends[:, :, 0], ones[:, 0:NE], ntl[:, :, 0], 0.0, ALU.mult, ALU.add))
                tt(base[:, :, :], ends[:, :, :], ntl[:, :, :], ALU.subtract)
                ch.link(nc.vector.tensor_scalar(base[:, :, :], base[:, :, :], float(P), None, ALU.mult))
                tt(cum[:, :, :], cum[:, :, :], tmp[:, :, :], ALU.subtract)
                tt(cum[:, :, :], cum[:, :, :], bank[5][:, 0:TC * NE].rearrange("p (c e) -> p c e", e=NE), ALU.add)
                tt(cum[:, :, :], cum[:, :, :], base[:, :, 0].rearrange("p (c e) -> p c e", c=1).broadcast_to(whole), ALU.add)
                for k, m in enumerate((m0, m1)):
                    tt(tmp[:, :, :], m[:, :, :], cum[:, :, :], ALU.mult)
                    ch.link(nc.vector.reduce_sum(posf[:, :, :], tmp[:, :, :], axis=AX))
                    last = nc.vector.tensor_copy(slot[:, k, :], posf[:, :, 0])
                    if k == 0:
                        ch.link(last)
                last.then_inc(placed, 1)
                tt(own[:, :, :], ends[:, :, 0].rearrange("p (c e) -> p c e", c=1).broadcast_to([P, NT, NE]),
                   iota_t[:, :].rearrange("p (t a) -> p t a", a=1).broadcast_to([P, NT, NE]), ALU.is_le)
                ch.link(nc.vector.reduce_sum(ownf[:, :, :], own[:, :, :], axis=AX))
                ch.link(nc.vector.tensor_scalar(owner[:, :], ownf[:, :, 0], float(NE - 1), None, ALU.min))
                dve.wait_ge(exped, 1)
                ch.link(nc.vector.reduce_sum(red[:, :, :], ex[:, :, :], axis=AX))
                ch.link(nc.vector.reciprocal(red[:, :, :], red[:, :, :]))
                tt(ex[:, :, :], ex[:, :, :], red[:, :, :].broadcast_to(whole), ALU.mult)
                tt(tmp[:, :, :], ex[:, :, :], ms[:, :, :], ALU.mult)
                ch.link(nc.vector.reduce_sum(red[:, :, :], tmp[:, :, :], axis=AX))
                ch.link(nc.vector.reciprocal(red[:, :, :], red[:, :, :]))
                tt(ex[:, :, :], ex[:, :, :], red[:, :, :].broadcast_to(whole), ALU.mult)
                for k, m in enumerate((m0, m1)):
                    tt(tmp[:, :, :], m[:, :, :], ex[:, :, :], ALU.mult)
                    ch.link(nc.vector.reduce_sum(share[:, k, :].rearrange("p (c a) -> p c a", a=1), tmp[:, :, :], axis=AX))

            @blockR.tensor
            def _(pe):
                pe.wait_ge(g0, 7)
                pe.wait_ge(wr_in, 32)

                def scores(b):
                    for c in range(NC):
                        for k in range(KD):
                            last = nc.tensor.matmul(bank[7][:, (NC * b + c) * NE:(NC * b + c + 1) * NE],
                                                    xaT[b % 2][:, k, c * P:(c + 1) * P], w_r[:, k, :],
                                                    start=(k == 0), stop=(k == KD - 1))
                    return last

                for b in range(NB):
                    pe.wait_ge(xa_ready, b + 1)
                    for k in range(KD):
                        for c in range(NC):
                            last = nc.tensor.transpose(bank[2 * (b % 2) + k][:, c * P:(c + 1) * P],
                                                       xa[:, NC * b + c, k * P:(k + 1) * P], ident[:, :])
                        last.then_inc(aT_ps, 1)
                    pe.wait_ge(aT_ready, KD * (b + 1))
                    last = scores(b)
                last.then_inc(sc_ps, 1)
                pe.wait_ge(chosen, 1)
                flat = ms[:, :, :].rearrange("p c e -> p (c e)")
                nc.tensor.matmul(bank[5][:, 0:TC * NE], before[:, :], flat, start=True, stop=True)
                nc.tensor.matmul(bank[6][:, 0:TC * NE], ones[:, :], flat, start=True, stop=True).then_inc(cnt_ps, 1)

        with lay0:
            one_row = s0("one_row", [1, P])
            xnT = s0("xnT", [P, KD, L])
            xpad = s0("xpad", [P, DB, L + 2 * (KC - 1)])
            zs = s0("zs", [P, DB, L])
            xc = [s0(f"xc{i}", [P, DB, L]) for i in range(2)]
            dt = [s0(f"dt{i}", [P, DB, L]) for i in range(2)]
            u = [s0(f"u{i}", [P, DB, L]) for i in range(2)]
            xdT = s0("xdT", [R + 2 * NS, L])
            ct = [s0(f"ct{i}", [P, NC, NS]) for i in range(2)]
            bb = [s0(f"bb{i}", [P, 2, L]) for i in range(2)]
            dA = [s0(f"dA{i}", [P, DB, SEG]) for i in range(2)]
            hs = [s0(f"hs{i}", [P, DB, SEG]) for i in range(HS)]
            yacc = part(RING * (N_W1 + N_W2), N_YA, DI)
            ysum = s0("ysum", [P, DB, L])
            so = s0("so", [P, NC, DM])
            w1 = [part(i * N_W1, N_W1, 2 * HE) for i in range(RING)]
            w2 = [part(RING * N_W1 + i * N_W2, N_W2, DM) for i in range(RING)]
            b1 = [s0(f"b1_{i}", [P, 2 * HB]) for i in range(RING)]
            b2 = [s0(f"b2_{i}", [1, DM]) for i in range(RING)]
            xg = [s0(f"xg{i}", [P, DM]) for i in range(RING)]
            yg = [s0(f"yg{i}", [P, DM]) for i in range(RING)]
            xgT = s0("xgT", [P, KD, P])
            sa = s0("sa", [P, HB, P])
            hE = s0("hE", [P, HB, P])

            setup_v, setup_g, setup_a = sem("setup_v"), sem("setup_g"), sem("setup_a")
            xnT_in, p_ps, p_used = sem("xnT_in"), sem("prep_ps"), sem("prep_used")
            tap_done = sem("tap_done")
            conv_chain, conv_done, xc_ready = sem("conv_chain"), sem("conv_done"), sem("xc_ready")
            b_stored, bb_in = sem("b_stored"), [sem("bb_in0"), sem("bb_in1")]
            a_chain, sp_done, dt_sum, u_ready = sem("a_chain"), sem("sp_done"), sem("dt_sum"), sem("u_ready")
            dA_ready, dBu_ready, scan_done = sem("dA_ready"), sem("dBu_ready"), sem("scan_done")
            hT_ready, hT_used, yb_ps = sem("hT_ready"), sem("hT_used"), sem("yb_ps")
            y_read, y_chain, y_ready, o_ps, so_ready, so_stored = (sem(n) for n in ("y_read", "y_chain", "y_ready", "o_ps", "so_ready", "so_stored"))
            e_in = [sem(f"expert_in{i}") for i in range(RING)]
            y_st = [sem(f"yg_stored{i}") for i in range(RING)]
            xgT_ps, xgT_ready, ab_ps, sa_ready, hE_ready, l2_ps, yg_ready = (
                sem(n) for n in ("xgT_ps", "xgT_ready", "ab_ps", "sa_ready", "hE_ready", "l2_ps", "yg_ready"))

            PREP = {n: [] for n in range(NS)}
            for k in range(DB):
                PREP[k].append(("proj", k))
                PREP[min(1 + k, 3)].append(("conv", k))
                PREP[6 + k].append(("dt", k))
            PREP[4] += [("silu", k) for k in range(DB)] + [("gate z", 0)]
            PREP[5].append(("xd", 0))
            PREP[9] += [("soft", 0), ("c", 0)]
            USE = {"proj": 0, "xd": 4, "dt": 5, "c": 9}

            def soft(eng, d, unit, quarter):
                h = slice(quarter % 2 * DB // 2, (quarter % 2 + 1) * DB // 2)
                if quarter == 0:
                    eng.wait_ge(sp_done, unit + 1)
                if quarter < 2:
                    eng.tensor_tensor(dt[d][:, h, :], dt[d][:, h, :], u[d][:, h, :], ALU.add).then_inc(dt_sum, 1)
                else:
                    eng.wait_ge(dt_sum, 2 * unit + 2)
                    eng.tensor_tensor(u[d][:, h, :], dt[d][:, h, :], xc[d][:, h, :], ALU.mult).then_inc(u_ready, 1)

            def tapped(k, d, t):
                at = t if d == 0 else 2 * (KC - 1) - t
                return xpad[:, k, at:at + L], cols[:, CW + (d * DB + k) * KC + t:CW + (d * DB + k) * KC + t + 1]

            def tile_pieces(d):
                out = {n: [] for n in range(NS)}
                for i in range(TPB - T0) if d == 1 else range(-T0, 0):
                    for at, piece in enumerate(("x", "up", "gate", "down")):
                        out[3 * (i % T0) + at].append((piece, i))
                return out

            def units(b, last):
                for d in range(2):
                    yield d, 2 * b + d, tile_pieces(d) if d == 1 or later(b) else {n: [] for n in range(NS)}, not (last and d == 1)

            def batches(eng, body):
                body(0, False)
                with eng.Fori(0, NB - 2) as b:
                    body(b + 1, False)
                body(NB - 1, True)

            def later(number):
                return not (isinstance(number, int) and number == 0)

            block = lay0.enter_context(nc.Block())

            @block.sync
            def _(sp):
                def load_tile(t, i):
                    r = i % RING
                    e = sp.value_load(owner[0:1, bass.ds(t, 1)], min_val=0, max_val=NE - 1)
                    sp.dma_start(xg[r][:, :], xg_dram[bass.ds(t * P, P), :]).then_inc(e_in[r], 16)
                    sp.dma_start(w1[r][:, :, :], wl1[e].rearrange("(k p) h -> p k h", p=P)).then_inc(e_in[r], 16)
                    sp.dma_start(w2[r][:, :, :], wl2[e].rearrange("(k p) d -> p k d", p=P)).then_inc(e_in[r], 16)
                    sp.dma_start(b1[r][:, :], bl1c[e]).then_inc(e_in[r], 16)
                    sp.dma_start(b2[r][:, :], bl2[bass.ds(e, 1), :]).then_inc(e_in[r], 16)

                def load_pair(d, p):
                    sp.dma_start(bb[p % 2][:, :, :], b_dram[d, 2 * p:2 * p + 2, :].partition_broadcast(P)).then_inc(bb_in[p % 2], 16)

                def store_b(d, unit):
                    sp.wait_ge(p_used, 10 * unit + USE["xd"] + 1)
                    sp.dma_start(b_dram[d], xdT[R:R + NS, :]).then_inc(b_stored, 16)
                    sp.wait_ge(b_stored, 16 * (unit + 1))
                    apart(sp, idle)

                sp.dma_start(xnT[:, :, :], xnT_dram[0]).then_inc(xnT_in, 16)
                sp.sem_inc(so_stored, 16)
                for q in y_st:
                    sp.sem_inc(q, 16)
                store_b(0, 0)
                for p in range(2):
                    load_pair(0, p)
                sp.wait_ge(dBu_ready, 2)
                load_pair(0, 2)

                def body(b, last):
                    for d, unit, tiles, more in units(b, last):
                        for n in range(NS):
                            if n == 4 and d == 0 and later(b):
                                sp.wait_ge(so_ready, 2 * b)
                                sp.dma_start(s_dram[b - 1], so[:, :, :]).then_inc(so_stored, 16)
                            if n == 4 and d == 0 and not last:
                                sp.wait_ge(p_used, 10 * (unit + 1) + DB)
                                sp.dma_start(xnT[:, :, :], xnT_dram[b + 1]).then_inc(xnT_in, 16)
                            if n == NS - 2 and not later(unit):
                                sp.wait_ge(grouped[0], 16 * 2 * EARLY)
                                sp.wait_ge(grouped[1], 16 * 2 * (TC - EARLY))
                                for i in range(RING):
                                    load_tile(i, i)
                            if n == 8 and more:
                                store_b(1 - d, unit + 1)
                            for piece, i in tiles[n]:
                                if piece == "down":
                                    t = TPB * b + i
                                    sp.wait_ge(yg_ready, t + 2)
                                    sp.dma_start(yg_dram[bass.ds(t * P, P), :], yg[i % RING][:, :]).then_inc(y_st[i % RING], 16)
                                    if not (last and i + RING >= TPB - T0):
                                        load_tile(t + RING, i)
                            if n % 2 == 0:
                                p = n // 2 + 3
                                if p < NS // 2 or more:
                                    sp.wait_ge(dBu_ready, NS * unit + n + 4)
                                    load_pair(d if p < NS // 2 else 1 - d, p % (NS // 2))

                batches(sp, body)
                sp.wait_ge(so_ready, 2 * NB)
                sp.dma_start(s_dram[NB - 1], so[:, :, :]).then_inc(so_stored, 16)
                sp.wait_ge(so_stored, 16 * (NB + 1))
                for r, q in enumerate(y_st):
                    sp.wait_ge(q, 16 * (1 + len(range(r, NT, RING))))

            @block.gpsimd
            def _(pool):
                for i in range(HS):
                    nc.gpsimd.memset(hs[i][:, :, 0:1], 0.0).then_inc(setup_g, 1)
                nc.gpsimd.memset(one_row[:, :], 1.0).then_inc(setup_g, 1)
                def group(c, done):
                    for k in range(2):
                        nc.gpsimd.indirect_dma_start(
                            out=xg_dram, out_offset=bass.IndirectOffsetOnAxis(slot[:, k, c:c + 1], 0),
                            in_=xa[:, c, :], in_offset=None).then_inc(done, 16)

                pool.wait_ge(placed, 1)
                pool.wait_ge(zeroed, 16 * TPB)
                for c in range(TC - EARLY, TC):
                    group(c, grouped[0])

                def state(d, unit, n):
                    step = NS * unit + n
                    if n == 0:
                        pool.wait_ge(u_ready, 2 * unit + 2)
                    if n % 2 == 0:
                        pool.wait_ge(bb_in[n // 2 % 2], 16 * (4 * unit + n // 4 + 1))
                    if later(unit) or n >= HS:
                        pool.wait_ge(hT_ready, NC * (step - HS + 1))
                    row = bb[n // 2 % 2][:, n % 2:n % 2 + 1, :].broadcast_to([P, DB, L])
                    nc.gpsimd.tensor_tensor(hs[n % HS][:, :, 1:], u[d][:, :, :], row, ALU.mult).then_inc(dBu_ready, 1)

                def body(b, last):
                    for d, unit, _, more in units(b, last):
                        for n in range(NS):
                            state(d, unit, n)
                            if not later(unit) and n < TC - EARLY:
                                group(n, grouped[1])
                            if n >= NS - 3 and more:
                                for quarter in ((0,), (1,), (2, 3))[n - (NS - 3)]:
                                    soft(pool, 1 - d, unit + 1, quarter)

                batches(pool, body)

            @block.scalar
            def _(act):
                act.wait_ge(w_sem, 16 * N_W)
                a_cols = cols[:, AL:AL + 2 * DB * NS]
                nc.scalar.activation(a_cols, a_cols, ACT.Exp).then_inc(setup_a, 1)
                act.sem_inc(yg_ready, 1)
                act.wait_ge(hT_used, 2)

                def output(b, h, at):
                    act.wait_ge(o_ps, 2 * b + h + 1)
                    nc.scalar.activation(so[:, 2 * h:2 * h + 2, :], bank[at][:, :].rearrange("p (c d) -> p c d", d=DM), ACT.Copy)\
                      .then_inc(so_ready, 1)

                def prepare(what, k, d, unit, b=0, first=False):
                    use = 10 * unit + USE.get(what, 0) + k
                    if what in USE:
                        act.wait_ge(p_ps, use + 1)
                    if what == "proj" and d == 1 and k == 0 and later(b):
                        act.wait_ge(y_ready, b)
                    if what == "proj":
                        if d == 0:
                            nc.scalar.activation(xpad[:, k, KC - 1:KC - 1 + L], bank[7][:, :], ACT.Copy).then_inc(p_used, 1)
                        else:
                            nc.scalar.activation(zs[:, k, :], bank[7][:, :], ACT.Copy).then_inc(p_used, 1)
                    elif what == "conv":
                        if d == 0:
                            act.wait_ge(p_used, 10 * unit + k + 1)
                        if k == 0 and not (isinstance(unit, int) and unit < 2):
                            act.wait_ge(dBu_ready, NS * (unit - 1))
                        src, tap = tapped(k, d, 0)
                        nc.scalar.activation(u[d][:, k, :], src, ACT.Copy, scale=tap).then_inc(tap_done, 1)
                    elif what == "gate z":
                        if d == 1:
                            act.wait_ge(p_used, 10 * unit + DB)
                            nc.scalar.activation(zs[:, :, :], zs[:, :, :], ACT.Silu)
                    elif what == "silu":
                        act.wait_ge(conv_done, DB * unit + k + 1)
                        nc.scalar.activation(xc[d][:, k, :], u[d][:, k, :], ACT.Silu,
                                             bias=cols[:, CB + DB * d + k:CB + DB * d + k + 1]).then_inc(xc_ready, 1)
                    elif what == "xd":
                        if not first:
                            act.wait_ge(b_stored, 16 * unit)
                        nc.scalar.activation(xdT[:, :], bank[7][0:R + 2 * NS, :], ACT.Copy).then_inc(p_used, 1)
                    elif what == "c":
                        turned_c = bank[7][:, 0:NC * RX].rearrange("p (c n) -> p c n", n=RX)[:, :, R + NS:]
                        nc.scalar.activation(ct[d][:, :, :], turned_c, ACT.Copy)\
                          .then_inc(p_used, 1)
                    elif what == "dt":
                        bias = cols[:, BD + DB * d + k:BD + DB * d + k + 1]
                        nc.scalar.activation(dt[d][:, k, :], bank[7][:, :], ACT.Relu, bias=bias)
                        nc.scalar.activation(u[d][:, k, :], bank[7][:, :], ACT.Abs, bias=bias).then_inc(p_used, 1)
                        act.wait_ge(p_used, use + 1)
                        nc.scalar.activation(u[d][:, k, :], u[d][:, k, :], ACT.Exp, scale=-1.0).then_inc(a_chain, 1)
                    elif what == "soft":
                        act.wait_ge(a_chain, DB * unit + DB)
                        nc.scalar.activation(u[d][:, :, :], u[d][:, :, :], ACT.Ln, bias=1.0).then_inc(sp_done, 1)

                def state(d, unit, n):
                    step = NS * unit + n
                    if n == 0:
                        act.wait_ge(dt_sum, 2 * unit + 2)
                    act.wait_ge(scan_done, step + 1)
                    for k in range(DB):
                        at = AL + (d * DB + k) * NS + n
                        last = nc.scalar.activation(dA[n % 2][:, k, 1:], dt[d][:, k, :], ACT.Exp, scale=cols[:, at:at + 1])
                    last.then_inc(dA_ready, 1)

                def tile(piece, b, i):
                    t, r = TPB * b + i, i % RING
                    if piece == "x":
                        act.wait_ge(xgT_ps, t + 1)
                        nc.scalar.activation(xgT[:, :, :], bank[6][:, 0:DM].rearrange("p (k t) -> p k t", t=P), ACT.Copy)\
                          .then_inc(xgT_ready, 1)
                    elif piece == "up":
                        act.wait_ge(ab_ps, t + 1)
                        for m in range(HB):
                            last = nc.scalar.activation(sa[:, m, :], bank[4][:, m * P:(m + 1) * P], ACT.Silu, bias=b1[r][:, m:m + 1])
                        last.then_inc(sa_ready, 1)
                    elif piece == "down":
                        act.wait_ge(l2_ps, t + 1)
                        act.wait_ge(y_st[r], 16 * (TPB // RING * b + i // RING + 1))
                        nc.scalar.activation(yg[r][:, :], bank[5][:, 0:DM], ACT.Copy).then_inc(yg_ready, 1)

                def body(b, last):
                    for d, unit, tiles, more in units(b, last):
                        for n in range(NS):
                            if n + 3 < NS:
                                state(d, unit, n + 3)
                            elif more:
                                state(1 - d, unit + 1, n + 3 - NS)
                            for piece, i in sorted(tiles[n], key=lambda p: p[0] == "x"):
                                tile(piece, b, i)
                            if more:
                                for what, k in PREP[n]:
                                    prepare(what, k, 1 - d, unit + 1, b)
                            if d == 0 and n in (1, 2) and later(b):
                                if n == 1:
                                    act.wait_ge(so_stored, 16 * b)
                                output(b - 1, n - 1, 6)

                for n in range(NS):
                    for what, k in PREP[n]:
                        prepare(what, k, 0, 0, 0, True)
                act.wait_ge(setup_v, 1)
                for n in range(3):
                    state(0, 0, n)
                batches(act, body)
                act.wait_ge(so_stored, 16 * NB)
                for h in range(2):
                    output(NB - 1, h, h)

            @block.vector
            def _(dve):
                for i in range(2):
                    nc.vector.memset(dA[i][:, :, 0:1], 0.0).then_inc(scan_done, 1)
                nc.vector.memset(xpad[:, :, 0:KC - 1], 0.0).then_inc(hT_used, 1)
                nc.vector.memset(xpad[:, :, KC - 1 + L:], 0.0).then_inc(hT_used, 1)
                dve.wait_ge(hT_used, 2)
                dve.sem_inc(hT_used, NC - 2)
                dve.wait_ge(w_sem, 16 * N_W)
                dve.wait_ge(setup_a, 1)
                a_cols = cols[:, AL:AL + 2 * DB * NS]
                nc.vector.tensor_scalar(a_cols, a_cols, -1.0, None, ALU.mult).then_inc(setup_v, 1)

                def conv(k, d, unit):
                    dve.wait_ge(tap_done, DB * unit + k + 1)
                    ch = Chain(dve, conv_chain, (DB * unit + k) * (KC - 2))
                    for t in range(1, KC):
                        src, tap = tapped(k, d, t)
                        ins = nc.vector.scalar_tensor_tensor(out=u[d][:, k, :], in0=src, scalar=tap, in1=u[d][:, k, :],
                                                             op0=ALU.mult, op1=ALU.add)
                        if t < KC - 1:
                            ch.link(ins)
                    ins.then_inc(conv_done, 1)

                def scan(d, unit, n):
                    step = NS * unit + n
                    dve.wait_ge(dA_ready, step + 1)
                    dve.wait_ge(dBu_ready, step + 1)
                    h, decay = (t[:, :, :].rearrange("p k l -> p (k l)") for t in (hs[n % HS], dA[n % 2]))
                    if d == 1:
                        h, decay = h[:, ::-1], decay[:, ::-1]
                    dve.wait_ge(scan_done, step + 2)
                    nc.vector.tensor_tensor_scan(h, decay, h, 0.0, ALU.mult, ALU.add).then_inc(scan_done, 1)

                def weigh(d, unit, n):
                    step = NS * unit + n
                    if n == 0:
                        dve.wait_ge(p_used, 10 * unit + USE["c"] + 1)
                    for c in range(NC):
                        dve.wait_ge(hT_ready, 4 * step + c + 1)
                        if c == 0:
                            dve.wait_ge(hT_used, 4 * step + 4)
                        if n == 0:
                            ins = nc.vector.tensor_scalar(yacc[:, c, :], bank[c][:, :], ct[d][:, c, n:n + 1], None, ALU.mult)
                        else:
                            ins = nc.vector.scalar_tensor_tensor(out=yacc[:, c, :], in0=bank[c][:, :], scalar=ct[d][:, c, n:n + 1],
                                                                 in1=yacc[:, c, :], op0=ALU.mult, op1=ALU.add)
                        ins.then_inc(hT_used, 1)

                def gate(b, i):
                    t, r = TPB * b + i, i % RING
                    dve.wait_ge(sa_ready, t + 1)
                    for m in range(HB):
                        last = nc.vector.scalar_tensor_tensor(out=hE[:, m, :], in0=bank[5][:, m * P:(m + 1) * P],
                                                              scalar=b1[r][:, HB + m:HB + m + 1], in1=sa[:, m, :],
                                                              op0=ALU.add, op1=ALU.mult)
                    last.then_inc(hE_ready, 1)

                def finish(d, unit, b):
                    dst = ysum if d == 0 else xc[1]
                    if d == 0 and later(b):
                        dve.wait_ge(o_ps, 2 * b)
                    for k in range(DB):
                        dve.wait_ge(yb_ps, DB * unit + k + 1)
                        last = nc.vector.scalar_tensor_tensor(
                            out=dst[:, k, :], in0=xc[d][:, k, :], scalar=cols[:, SD + DB * d + k:SD + DB * d + k + 1],
                            in1=bank[k][:, :], op0=ALU.mult, op1=ALU.add)
                    last.then_inc(y_read, 1)
                    if d == 0:
                        return
                    dve.wait_ge(y_read, unit + 1)
                    Chain(dve, y_chain, b).link(nc.vector.tensor_tensor(ysum[:, :, :], ysum[:, :, :], xc[1][:, :, :], ALU.add))
                    nc.vector.scalar_tensor_tensor(out=ysum[:, :, :], in0=ysum[:, :, :], scalar=0.5, in1=zs[:, :, :],
                                                   op0=ALU.mult, op1=ALU.mult).then_inc(y_ready, 1)

                def body(b, last):
                    for d, unit, tiles, more in units(b, last):
                        for n in range(NS):
                            if n + 2 < NS:
                                scan(d, unit, n + 2)
                            elif more:
                                scan(1 - d, unit + 1, n + 2 - NS)
                            for piece, i in tiles[n]:
                                if piece == "gate":
                                    gate(b, i)
                            weigh(d, unit, n)
                            if more:
                                for what, k in PREP[n]:
                                    if what == "conv":
                                        conv(k, 1 - d, unit + 1)
                        finish(d, unit, b)

                for k in range(DB):
                    conv(k, 0, 0)
                for quarter in range(4):
                    soft(dve, 0, 0, quarter)
                for n in range(2):
                    scan(0, 0, n)
                dve.wait_ge(grouped[0], 16 * 2 * EARLY)
                batches(dve, body)

            @block.tensor
            def _(pe):
                mm = nc.tensor.matmul
                pe.wait_ge(w_sem, 16 * N_W)
                pe.wait_ge(setup_g, HS + 1)

                def prepare(what, k, d, unit, b, first=False):
                    if what not in USE:
                        return
                    use = 10 * unit + USE[what] + k
                    if what == "proj":
                        if k == 0 and d == 0:
                            pe.wait_ge(xnT_in, 16 * (b + 1))
                        if not (first and k == 0):
                            pe.wait_ge(p_used, use)
                        at = (d * DB + k) * P
                        for j in range(KD):
                            last = mm(bank[7][:, :], w_in[:, j, at:at + P], xnT[:, j, :], start=(j == 0), stop=(j == KD - 1))
                    elif what == "xd":
                        pe.wait_ge(xc_ready, DB * unit + DB)
                        pe.wait_ge(p_used, use)
                        for j in range(DB):
                            last = mm(bank[7][0:R + 2 * NS, :], w_x[:, d, j, :], xc[d][:, j, :], start=(j == 0), stop=(j == DB - 1))
                    elif what == "c":
                        pe.wait_ge(p_used, use)
                        for c in range(NC):
                            last = nc.tensor.transpose(bank[7][:, c * RX:(c + 1) * RX], xdT[:, c * P:(c + 1) * P], ident[0:RX, 0:RX])
                    elif what == "dt":
                        pe.wait_ge(p_used, use)
                        last = mm(bank[7][:, :], w_dt[:, d, k * P:(k + 1) * P], xdT[0:R, :], start=True, stop=True)
                    last.then_inc(p_ps, 1)

                def output(h, at):
                    for c in range(2 * h, 2 * h + 2):
                        for k in range(DB):
                            last = mm(bank[at][:, DM * (c % 2):DM * (c % 2 + 1)], ysum[:, k, c * P:(c + 1) * P],
                                      w_out[:, k, :], start=(k == 0), stop=(k == DB - 1))
                    last.then_inc(o_ps, 1)

                def turn(unit, n):
                    step = NS * unit + n
                    pe.wait_ge(scan_done, step + 3)
                    for c in range(NC):
                        pe.wait_ge(hT_used, 4 * step + c + 1)
                        for k in range(DB):
                            last = nc.tensor.transpose(bank[c][:, k * P:(k + 1) * P], hs[n % HS][:, k, 1 + c * P:1 + (c + 1) * P],
                                                       ident[:, :])
                        last.then_inc(hT_ready, 1)

                def tile(piece, b, i):
                    t, r = TPB * b + i, i % RING
                    if piece == "x":
                        pe.wait_ge(e_in[r], 80 * (TPB // RING * b + i // RING + 1))
                        if i == 1 - T0:
                            pe.wait_ge(so_ready, 2 * b)
                        for k in range(KD):
                            last = nc.tensor.transpose(bank[6][:, k * P:(k + 1) * P], xg[r][:, k * P:(k + 1) * P], ident[:, :])
                        last.then_inc(xgT_ps, 1)
                    elif piece == "up":
                        pe.wait_ge(xgT_ready, t + 1)
                        pe.wait_ge(yg_ready, t + 1)
                        for m in range(2 * HB):
                            for k in range(KD):
                                last = mm(bank[4 + m // HB][:, m % HB * P:(m % HB + 1) * P], w1[r][:, k, m * P:(m + 1) * P], xgT[:, k, :],
                                          start=(k == 0), stop=(k == KD - 1))
                        last.then_inc(ab_ps, 1)
                    elif piece == "down":
                        pe.wait_ge(hE_ready, t + 1)
                        for m in range(HB):
                            mm(bank[5][:, 0:DM], hE[:, m, :], w2[r][:, m, :], start=(m == 0), stop=False)
                        mm(bank[5][:, 0:DM], one_row[:, :], b2[r][:, :], start=False, stop=True).then_inc(l2_ps, 1)

                def body(b, last_batch):
                    for d, unit, tiles, more in units(b, last_batch):
                        if later(unit):
                            pe.wait_ge(y_read, unit)
                        for n in range(NS):
                            turn(unit, n)
                            for piece, i in sorted(tiles[n], key=lambda p: p[0] == "x"):
                                tile(piece, b, i)
                            if more:
                                for what, k in PREP[n]:
                                    prepare(what, k, 1 - d, unit + 1, b + d)
                            if d == 0 and n in (1, 2) and later(b):
                                if n == 1:
                                    pe.wait_ge(y_ready, b)
                                    pe.wait_ge(xgT_ready, TPB * b - T0 + 1)
                                else:
                                    pe.wait_ge(so_ready, 2 * b - 1)
                                output(n - 1, 6)
                        for k in range(DB):
                            if k == 0:
                                pe.wait_ge(hT_used, 4 * NS * (unit + 1) + 4)
                            for c in range(NC):
                                last = nc.tensor.transpose(bank[k][:, c * P:(c + 1) * P], yacc[:, c, k * P:(k + 1) * P], ident[:, :])
                            last.then_inc(yb_ps, 1)

                for n in range(NS):
                    for what, k in PREP[n]:
                        prepare(what, k, 0, 0, 0, True)
                batches(pe, body)
                pe.wait_ge(y_ready, NB)
                for h in range(2):
                    output(h, h)

        lay1 = ExitStack()
        with lay1:
            def s1(name, shape, dt=f32):
                return sb(name, shape, dt, lay1)

            HM = HID // P
            wqkv_sb = s1("wqkv_sb", [P, KD, 3 * DM])
            wo_sb = s1("wo_sb", [P, KD, DM])
            cms1_sb = s1("cms1_sb", [P, LV, KD, HID])
            cms2_sb = s1("cms2_sb", [P, LV, HM, DM])
            wf_sb = s1("wf_sb", [P, KD, DM])
            vr_sb = s1("vr_sb", [P, KD, RC])
            cf_sb = s1("cf_sb", [RC, DM])
            cols_sb = s1("cols_sb", [P, NCOL1])
            rows_sb = s1("rows_sb", [P, 2, DM])
            mask = s1("mask", [P, 4, P])
            hmask = s1("hmask", [P, KD, P])
            par = s1("par", [P, 2])
            cur = s1("cur", [P, 2, NC], u32)
            xin = s1("xin", [P, NC, DM])
            s_in = s1("s_in", [P, NC, DM])
            ya = s1("ya", [P, NC, DM])
            yb = s1("yb", [P, NC, DM])
            x1s = s1("x1s", [P, NC, DM])
            xm = s1("xm", [P, NC, DM])
            xh = s1("xh", [P, NC, DM])
            th = s1("th", [P, NC, DM])
            gt = s1("gt", [P, NC, DM])
            xmT = s1("xmT", [P, KD, L])
            hT = s1("hT", [P, KD, L])
            qT = s1("qT", [P, KD, L])
            kT = [s1(f"kT{i}", [P, KD, L]) for i in range(2)]
            kv = s1("kv", [P, NC, 2 * DM])
            sm = s1("sm", [P, 4, 4, P])
            Ms = s1("Ms", [P, KD, P])
            yt = s1("yt", [P, NC, DM])
            yT = s1("yT", [P, KD, L])
            fT = s1("fT", [RC, L])
            mT = [s1(f"mT{lv}", [P, KD, L]) for lv in range(LV)]
            gl = [s1(f"gl{i}", [P, L]) for i in range(2)]
            xo = s1("xo", [P, NC, DM])
            go = s1("go", [P, NC, DM])
            ot = s1("ot", [P, NC, DM])
            st1 = s1("st1", [P, NC, 6])
            mv1 = s1("mv1", [P, NC, 2])
            sd1 = s1("sd1", [P, NC])
            rs1 = s1("rs1", [P, NC])

            wa_sem, wc_sem, set1_g = sem("attention_weights_in"), sem("cms_weights_in"), sem("set1_g")
            xs_in, head_read, o_ready, o_stored, l_used = (sem(n) for n in ("xs_in", "head_read", "o_ready", "o_stored", "l_used"))
            cur_ready, y_in, moe_sum, moe_tanh = (sem(n) for n in ("cur_ready", "y_in", "moe_sum", "moe_tanh"))
            chain1, chain2, var1, std1, n1_ready = (sem(n) for n in ("stage1_chain", "stage2_chain", "var1", "std1", "n1_ready"))
            bT_ps, bT_ready, qk_ps, q_ready, kv_ps, kv_ready = (sem(n) for n in ("bT_ps", "bT_ready", "qk_ps", "q_ready", "kv_ps", "kv_ready"))
            f_ps, f_ready, g_ps, g_sum, g_tanh = (sem(n) for n in ("f_ps", "f_ready", "g_ps", "g_sum", "g_tanh"))
            s_ps, sm_ready, m_ps, m_ready, y_ps, yt_ready = (sem(n) for n in ("s_ps", "sm_ready", "m_ps", "m_ready", "y_ps", "yt_ready"))
            yT_ps, yT_ready, wo_ps, n2_ready = (sem(n) for n in ("yT_ps", "yT_ready", "wo_ps", "n2_ready"))
            t2_ps, m_in, h_ps, gl_ready, l_ps, l_ready = (sem(n) for n in ("t2_ps", "m_in", "h_ps", "gl_ready", "l_ps", "l_ready"))
            N_WA, N_WC = 7, 2

            BESIDE = {n: [] for n in range(LV * HM)}
            BESIDE[0].append(("moe", 0))
            BESIDE[2].append(("norm0", 0))
            BESIDE[3].append(("norm1", 0))
            for n, piece in ((5, "x"), (6, "q"), (6, "k"), (7, "kv01"), (8, "kv23"), (8, "f"), (9, "gate"), (10, "first"),
                             (11, "silu")):
                BESIDE[n].append((piece, 0))
            for c in range(NC):
                BESIDE[11 + 2 * c].append(("intra", c))
                BESIDE[12 + 2 * c].append(("state", c))
            for n, piece in ((19, "yT"), (20, "wo"), (21, "norm2"), (23, "t2")):
                BESIDE[n].append((piece, 0))

            def beside(stage1, stage2, a, m):
                for n in range(LV * HM):
                    if m is not None:
                        stage2(m, n // HM, n % HM)
                    if a is not None:
                        for piece, c in BESIDE[n]:
                            stage1(a, piece, c)

            def all_batches(eng, run):
                run(0, None)
                with eng.Fori(0, NB - 1) as i:
                    run(i + 1, i)
                run(None, NB - 1)

            block1 = lay1.enter_context(nc.Block())

            @block1.sync
            def _(sp):
                def load(b):
                    sp.dma_start(xin[:, :, :], x_v[b]).then_inc(xs_in, 16)
                    sp.dma_start(s_in[:, :, :], s_dram[b]).then_inc(xs_in, 16)

                def store(b):
                    sp.wait_ge(o_ready, b + 1)
                    sp.dma_start(out_v[b], ot[:, :, :]).then_inc(o_stored, 16)

                sp.sem_inc(o_stored, 16)
                load(0)
                for dst, src in ((wqkv_sb, wqkv), (wo_sb, wo), (wf_sb, w_fT), (vr_sb, v_r)):
                    sp.dma_start(dst[:, :, :], src.rearrange("(k p) m -> p k m", p=P)).then_inc(wa_sem, 16)
                sp.dma_start(cf_sb[:, :], c_fT).then_inc(wa_sem, 16)
                sp.dma_start(cols_sb[:, :], cols1).then_inc(wa_sem, 16)
                sp.dma_start(rows_sb[:, :, :], rows1.partition_broadcast(P)).then_inc(wa_sem, 16)
                sp.wait_ge(y_in, 16 * 2 * NC)
                for dst, src in ((cms1_sb, cms1), (cms2_sb, cms2)):
                    sp.dma_start(dst[:, :, :, :], src.rearrange("l (k p) m -> p l k m", p=P)).then_inc(wc_sem, 16)
                sp.wait_ge(head_read, 1)
                load(1)
                with sp.Fori(0, NB - 2) as b:
                    sp.wait_ge(head_read, b + 2)
                    load(b + 2)
                    store(b)
                store(NB - 2)
                store(NB - 1)
                sp.wait_ge(o_stored, 16 * (NB + 1))

            @block1.gpsimd
            def _(pool):
                def step(ins):
                    count[0] += 1
                    ins.then_inc(set1_g, 1)
                    pool.wait_ge(set1_g, count[0])

                def gather(b):
                    nc.gpsimd.tensor_copy(cur[:, :, :], slot[:, :, bass.ds(NC * b, NC)]).then_inc(cur_ready, 1)
                    pool.wait_ge(cur_ready, b + 1)
                    apart(pool, idle)
                    for c in range(NC):
                        for k, dst in enumerate((ya, yb)):
                            nc.gpsimd.indirect_dma_start(
                                out=dst[:, c, :], out_offset=None, in_=yg_dram,
                                in_offset=bass.IndirectOffsetOnAxis(cur[:, k, c:c + 1], 0)).then_inc(y_in, 16)

                gather(0)
                count = [0]
                for t in (mask, hmask, par):
                    step(nc.gpsimd.memset(t[:], 1.0))
                step(nc.gpsimd.affine_select(out=mask[:, :, :], in_=mask[:, :, :], compare_op=ALU.is_ge, fill=0.0, base=0,
                                             pattern=[[0, 4], [1, P]], channel_multiplier=-1))
                heads = hmask[:, :, :].rearrange("p k (h e) -> p k h e", e=HD)
                hp = [[0, KD], [-HD, P // HD], [0, HD]]
                step(nc.gpsimd.affine_select(out=heads, in_=heads, compare_op=ALU.is_ge, fill=0.0, base=0, pattern=hp,
                                             channel_multiplier=1))
                step(nc.gpsimd.affine_select(out=heads, in_=heads, compare_op=ALU.is_ge, fill=0.0, base=HD - 1,
                                             pattern=[[0, KD], [HD, P // HD], [0, HD]], channel_multiplier=-1))
                odd = hmask[:, 0, :].rearrange("p (h o e) -> p o h e", o=2, e=HD)
                for o in range(2):
                    step(nc.gpsimd.tensor_tensor(par[:, o:o + 1], odd[:, o, 0, 0:1], odd[:, o, 1, 0:1], ALU.add))
                    for h in range(2, P // HD // 2):
                        step(nc.gpsimd.tensor_tensor(par[:, o:o + 1], par[:, o:o + 1], odd[:, o, h, 0:1], ALU.add))

                with pool.Fori(0, NB - 1) as b:
                    pool.wait_ge(moe_sum, b + 1)
                    apart(pool, idle)
                    gather(b + 1)

            N_SET1 = 6 + 2 * (P // HD // 2 - 1)

            @block1.scalar
            def _(act):
                act.wait_ge(wa_sem, 16 * N_WA)

                def col(i):
                    return cols_sb[:, i:i + 1]

                def stage1(a, piece, c):
                    if piece == "moe":
                        act.wait_ge(moe_sum, a + 1)
                        nc.scalar.activation(th[:, :, :], xh[:, :, :], ACT.Tanh, scale=0.5).then_inc(moe_tanh, 1)
                    elif piece.startswith("norm"):
                        act.wait_ge(var1, 3 * a + int(piece[4:]) + 1)
                        nc.scalar.activation(sd1[:, :], rs1[:, :], ACT.Sqrt).then_inc(std1, 1)
                    elif piece == "x":
                        for k in range(KD):
                            act.wait_ge(bT_ps, 4 * a + k + 1)
                            nc.scalar.activation(hT[:, k, :], bank[k][:, :], ACT.Identity, bias=col(O1 + k), scale=col(G1 + k))\
                              .then_inc(bT_ready, 1)
                        for k in range(KD):
                            act.wait_ge(bT_ps, 4 * a + KD + k + 1)
                            nc.scalar.activation(xmT[:, k, :], bank[2 + k][:, :], ACT.Copy).then_inc(bT_ready, 1)
                    elif piece == "q":
                        for k in range(KD):
                            act.wait_ge(qk_ps, 4 * a + k + 1)
                            nc.scalar.activation(qT[:, k, :], bank[k][:, :], ACT.Copy).then_inc(q_ready, 1)
                    elif piece == "k":
                        for k in range(KD):
                            act.wait_ge(qk_ps, 4 * a + KD + k + 1)
                            if k == 0 and isinstance(a, int):
                                act.wait_ge(set1_g, N_SET1)
                            for o in range(2):
                                nc.scalar.activation(kT[o][:, k, :], bank[2 + k][:, :], ACT.Copy, scale=par[:, o:o + 1])\
                                  .then_inc(q_ready, 1)
                    elif piece == "f":
                        act.wait_ge(f_ps, a + 1)
                        nc.scalar.activation(fT[:, :], bank[0][0:RC, :], ACT.Copy).then_inc(f_ready, 1)
                    elif piece == "silu":
                        act.wait_ge(g_sum, a + 1)
                        nc.scalar.activation(th[:, :, :], gt[:, :, :], ACT.Tanh, scale=0.5).then_inc(g_tanh, 1)
                    elif piece == "state":
                        act.wait_ge(y_ps, NC * a + c + 1)
                        nc.scalar.activation(yt[:, c, :], bank[2][:, 0:DM], ACT.Copy).then_inc(yt_ready, 1)
                    elif piece == "yT":
                        for k in range(KD):
                            act.wait_ge(yT_ps, KD * a + k + 1)
                            nc.scalar.activation(yT[:, k, :], bank[k][:, :], ACT.Copy).then_inc(yT_ready, 1)
                    elif piece == "t2":
                        for k in range(KD):
                            act.wait_ge(t2_ps, KD * a + k + 1)
                            nc.scalar.activation(mT[0][:, k, :], bank[k][:, :], ACT.Identity, bias=col(O2 + k), scale=col(G2 + k))\
                              .then_inc(m_in, 1)

                def stage2(m, lv, h):
                    act.wait_ge(h_ps, HM * LV * m + HM * lv + h + 1)
                    nc.scalar.activation(gl[h % 2][:, :], bank[4 + h % 2][:, :], ACT.Gelu_apprx_tanh, bias=col(C1 + HM * lv + h))\
                      .then_inc(gl_ready, 1)
                    if h == HM - 1 and lv < LV - 1:
                        for k in range(KD):
                            act.wait_ge(l_ps, 2 * LV * m + 2 * lv + k + 1)
                            nc.scalar.activation(mT[lv + 1][:, k, :], bank[6 + k][:, :], ACT.Identity, bias=col(C2 + KD * lv + k))\
                              .then_inc(l_ready, 1)

                all_batches(act, lambda a, m: beside(stage1, stage2, a, m))

            @block1.vector
            def _(dve):
                dve.wait_ge(wa_sem, 16 * N_WA)
                dve.sem_inc(l_used, 1)

                def norm_head(src, ch):
                    for c in range(NC):
                        last = nc.vector.bn_stats(st1[:, c, :], src[:, c, :])
                    ch.link(last)
                    apart(dve, idle)
                    for c in range(NC):
                        last = nc.vector.bn_aggr(mv1[:, c, :], st1[:, c, :])
                    ch.link(last)
                    nc.vector.tensor_scalar(rs1[:, :], mv1[:, :, 1], EPS, None, ALU.add).then_inc(var1, 1)

                def norm_tail(dst, src, a, nth, ch):
                    dve.wait_ge(std1, 3 * a + nth + 1)
                    ch.link(nc.vector.reciprocal(rs1[:, :], sd1[:, :]))
                    for c in range(NC):
                        last = nc.vector.tensor_scalar(dst[:, c, :], src[:, c, :], mv1[:, c, 0:1], rs1[:, c:c + 1],
                                                       ALU.subtract, ALU.mult)
                    return last

                def pair(h):
                    return slice(2 * h, 2 * h + 2)

                def wide(i):
                    return bank[i][:, :].rearrange("p (c d) -> p c d", d=DM)

                def stage1(a, piece, c, ch):
                    if piece == "moe":
                        dve.wait_ge(y_in, 16 * 2 * NC * (a + 1))
                        if not (isinstance(a, int) and a == 0):
                            dve.wait_ge(t2_ps, KD * a)
                        for c in range(NC):
                            ch.link(nc.vector.tensor_scalar(xh[:, c, :], ya[:, c, :], share[:, 0, bass.ds(NC * a + c, 1)], None, ALU.mult))
                            last = nc.vector.scalar_tensor_tensor(out=xh[:, c, :], in0=yb[:, c, :], scalar=share[:, 1, bass.ds(NC * a + c, 1)],
                                                                  in1=xh[:, c, :], op0=ALU.mult, op1=ALU.add)
                        last.then_inc(moe_sum, 1)
                        dve.wait_ge(moe_tanh, a + 1)
                        dve.wait_ge(xs_in, 32 * (a + 1))
                        ch.link(nc.vector.scalar_tensor_tensor(out=xh[:, :, :], in0=th[:, :, :], scalar=1.0, in1=xh[:, :, :],
                                                               op0=ALU.add, op1=ALU.mult))
                        ch.link(nc.vector.scalar_tensor_tensor(out=xh[:, :, :], in0=xh[:, :, :], scalar=0.5, in1=s_in[:, :, :],
                                                               op0=ALU.mult, op1=ALU.mult))
                        nc.vector.tensor_tensor(x1s[:, :, :], xin[:, :, :], xh[:, :, :], ALU.add).then_inc(head_read, 1)
                        dve.wait_ge(head_read, a + 1)
                        apart(dve, idle)
                        norm_head(x1s, ch)
                    elif piece == "norm0":
                        ch.link(norm_tail(xm, x1s, a, 0, ch))
                        norm_head(xm, ch)
                    elif piece == "norm1":
                        norm_tail(xh, xm, a, 1, ch).then_inc(n1_ready, 1)
                    elif piece in ("kv01", "kv23"):
                        for c in (0, 1) if piece == "kv01" else (2, 3):
                            dve.wait_ge(kv_ps, NC * a + c + 1)
                            nc.vector.tensor_copy(kv[:, c, :], bank[c][:, :]).then_inc(kv_ready, 1)
                    elif piece == "gate":
                        for h in range(2):
                            dve.wait_ge(g_ps, 2 * a + h + 1)
                            last = nc.vector.tensor_tensor(gt[:, pair(h), :], wide(1 + h), rows_sb[:, 0:1, :].broadcast_to([P, 2, DM]),
                                                           ALU.add)
                        last.then_inc(g_sum, 1)
                    elif piece in ("first", "intra", "state"):
                        if piece == "first" and isinstance(a, int):
                            dve.wait_ge(set1_g, N_SET1)
                        nxt, rs = {"first": (0, (0, 1)), "intra": (c, (2, 3)), "state": (c + 1, (0, 1))}[piece]
                        if nxt == NC:
                            return
                        if piece == "state":
                            dve.wait_ge(m_ps, (NC - 1) * a + nxt)
                            nc.vector.tensor_tensor(Ms[:, :, :], bank[3][:, 0:DM].rearrange("p (k m) -> p k m", m=P), hmask[:, :, :],
                                                    ALU.mult).then_inc(m_ready, 1)
                        for r in rs:
                            dve.wait_ge(s_ps, 4 * NC * a + 4 * nxt + r + 1)
                            if r == 0 and nxt >= 1:
                                dve.wait_ge(y_ps, NC * a + nxt)
                            nc.vector.tensor_tensor(sm[:, r, :, :], bank[r % 2][:, :].rearrange("p (h q) -> p h q", q=P), mask[:, :, :],
                                                    ALU.mult).then_inc(sm_ready, 1)
                    elif piece == "silu":
                        dve.wait_ge(g_tanh, a + 1)
                        ch.link(nc.vector.scalar_tensor_tensor(out=gt[:, :, :], in0=th[:, :, :], scalar=1.0, in1=gt[:, :, :],
                                                               op0=ALU.add, op1=ALU.mult))
                    elif piece == "wo":
                        for h in range(2):
                            dve.wait_ge(wo_ps, 2 * a + h + 1)
                            last = nc.vector.tensor_tensor(xm[:, pair(h), :], xm[:, pair(h), :], wide(2 + h), ALU.add)
                        ch.link(last)
                        norm_head(xm, ch)
                    elif piece == "norm2":
                        norm_tail(xh, xm, a, 2, ch).then_inc(n2_ready, 1)
                        dve.wait_ge(n2_ready, a + 1)
                        ch.link(nc.vector.tensor_tensor(xm[:, :, :], xm[:, :, :], rows_sb[:, 1:2, :].broadcast_to([P, NC, DM]), ALU.add))
                        ch.link(nc.vector.scalar_tensor_tensor(out=xm[:, :, :], in0=xm[:, :, :], scalar=0.5, in1=gt[:, :, :],
                                                               op0=ALU.mult, op1=ALU.mult))
                        ch.link(nc.vector.tensor_tensor(x1s[:, :, :], x1s[:, :, :], xm[:, :, :], ALU.add))

                def run(a, m):
                    if a is not None:
                        ch = Chain(dve, chain1, LINKS1 * a)
                        beside(lambda a, piece, c: stage1(a, piece, c, ch), None, a, None)
                    if m is not None:
                        dve.wait_ge(o_stored, 16 * (m + 1))
                        apart(dve, idle)
                        for h in range(2):
                            dve.wait_ge(l_ps, 2 * LV * m + 2 * (LV - 1) + h + 1)
                            nc.vector.scalar_tensor_tensor(out=ot[:, pair(h), :], in0=wide(6 + h), scalar=0.5, in1=go[:, pair(h), :],
                                                           op0=ALU.mult, op1=ALU.mult).then_inc(chain2 if h else idle, 1)
                        dve.wait_ge(chain2, m + 1)
                        dve.sem_inc(l_used, 1)
                        nc.vector.tensor_tensor(ot[:, :, :], ot[:, :, :], xo[:, :, :], ALU.add).then_inc(o_ready, 1)
                        dve.wait_ge(o_ready, m + 1)
                        if a is None:
                            apart(dve, idle)
                    if a is not None:
                        ch.mark(nc.vector.tensor_copy(xo[:, :, :], x1s[:, :, :]))
                        ch.link(nc.vector.tensor_copy(go[:, :, :], gt[:, :, :]))
                        assert ch.n == LINKS1, ch.n

                all_batches(dve, run)

            @block1.tensor
            def _(pe):
                mm = nc.tensor.matmul
                pe.wait_ge(wa_sem, 16 * N_WA)

                def turn(src, at, done):
                    for k in range(KD):
                        for c in range(NC):
                            last = nc.tensor.transpose(bank[at + k][:, c * P:(c + 1) * P], src[:, c, k * P:(k + 1) * P], ident[:, :])
                        last.then_inc(done, 1)

                def scores(a, c, rs):
                    cs = slice(c * P, (c + 1) * P)
                    for r in rs:
                        if c >= 1 or r >= 2:
                            pe.wait_ge(sm_ready, 4 * NC * a + 4 * c + r - 1)
                        for h in range(4):
                            k, o = h // 2, h % 2
                            last = mm(bank[r % 2][:, h * P:(h + 1) * P], kT[o][32 * r:32 * r + 32, k, cs], qT[32 * r:32 * r + 32, k, cs],
                                      start=True, stop=True)
                        last.then_inc(s_ps, 1)

                def values(a, c, rs):
                    for r in rs:
                        pe.wait_ge(sm_ready, 4 * NC * a + 4 * c + r + 1)
                        for h in range(4):
                            head = 8 * (h // 2) + 2 * r + h % 2
                            last = mm(bank[2][:, head * HD:(head + 1) * HD], sm[:, r, h, :], kv[:, c, DM + head * HD:DM + (head + 1) * HD],
                                      start=(c == 0 and r == 0 and h == 0), stop=(r == 3 and h == 3), skip_group_check=True)
                    return last

                def stage1(a, piece, c):
                    if piece == "x":
                        pe.wait_ge(n1_ready, a + 1)
                        turn(xh, 0, bT_ps)
                        turn(xm, 2, bT_ps)
                    elif piece in ("q", "k"):
                        at = 0 if piece == "q" else 2
                        pe.wait_ge(bT_ready, 4 * a + 2 + at)
                        for m in range(at, at + KD):
                            for k in range(KD):
                                last = mm(bank[m][:, :], wqkv_sb[:, k, m * P:(m + 1) * P], hT[:, k, :], start=(k == 0), stop=(k == KD - 1))
                            last.then_inc(qk_ps, 1)
                    elif piece in ("kv01", "kv23"):
                        pe.wait_ge(q_ready, 6 * a + (2 if piece == "kv01" else 6))
                        for c in (0, 1) if piece == "kv01" else (2, 3):
                            for k in range(KD):
                                last = mm(bank[c][:, :], hT[:, k, c * P:(c + 1) * P], wqkv_sb[:, k, DM:], start=(k == 0), stop=(k == KD - 1))
                            last.then_inc(kv_ps, 1)
                    elif piece == "f":
                        pe.wait_ge(kv_ready, NC * a + 1)
                        for k in range(KD):
                            last = mm(bank[0][0:RC, :], vr_sb[:, k, :], xmT[:, k, :], start=(k == 0), stop=(k == KD - 1))
                        last.then_inc(f_ps, 1)
                    elif piece == "gate":
                        pe.wait_ge(f_ready, a + 1)
                        pe.wait_ge(kv_ready, NC * a + 4)
                        for c in range(NC):
                            dst = bank[1 + c // 2][:, DM * (c % 2):DM * (c % 2 + 1)]
                            for k in range(KD):
                                mm(dst, xmT[:, k, c * P:(c + 1) * P], wf_sb[:, k, :], start=(k == 0), stop=False)
                            last = mm(dst, fT[:, c * P:(c + 1) * P], cf_sb[:, :], start=False, stop=True)
                            if c % 2:
                                last.then_inc(g_ps, 1)
                    elif piece == "first":
                        pe.wait_ge(g_sum, a + 1)
                        scores(a, 0, (0, 1))
                    elif piece == "intra":
                        scores(a, c, (2, 3))
                        if c >= 1:
                            pe.wait_ge(yt_ready, NC * a + c)
                            pe.wait_ge(m_ready, (NC - 1) * a + c)
                            for k in range(KD):
                                mm(bank[2][:, k * P:(k + 1) * P], qT[:, k, c * P:(c + 1) * P], Ms[:, k, :], start=(k == 0), stop=False,
                                   skip_group_check=True)
                        values(a, c, (0, 1))
                    elif piece == "state":
                        values(a, c, (2, 3)).then_inc(y_ps, 1)
                        if c < NC - 1:
                            for k in range(KD):
                                last = mm(bank[3][:, k * P:(k + 1) * P], kv[:, c, k * P:(k + 1) * P],
                                          kv[:, c, DM + k * P:DM + (k + 1) * P], start=(c == 0 and k == 0), stop=True,
                                          skip_group_check=True)
                            last.then_inc(m_ps, 1)
                            scores(a, c + 1, (0, 1))
                    elif piece == "yT":
                        pe.wait_ge(yt_ready, NC * a + NC)
                        turn(yt, 0, yT_ps)
                    elif piece == "wo":
                        pe.wait_ge(yT_ready, KD * a + KD)
                        for c in range(NC):
                            for k in range(KD):
                                last = mm(bank[2 + c // 2][:, DM * (c % 2):DM * (c % 2 + 1)], yT[:, k, c * P:(c + 1) * P], wo_sb[:, k, :],
                                          start=(k == 0), stop=(k == KD - 1))
                            if c % 2:
                                last.then_inc(wo_ps, 1)
                    elif piece == "t2":
                        pe.wait_ge(n2_ready, a + 1)
                        turn(xh, 0, t2_ps)

                def up(m, lv, h):
                    if h == 0 and lv == 0:
                        pe.wait_ge(m_in, KD * m + KD)
                    elif h == 0:
                        pe.wait_ge(l_ready, 2 * (LV - 1) * m + 2 * lv)
                    for k in range(KD):
                        last = mm(bank[4 + h % 2][:, :], cms1_sb[:, lv, k, h * P:(h + 1) * P], mT[lv][:, k, :],
                                  start=(k == 0), stop=(k == KD - 1))
                    last.then_inc(h_ps, 1)

                def down(m, lv, h):
                    if h == 0 and lv == 0:
                        pe.wait_ge(l_used, m + 1)
                    pe.wait_ge(gl_ready, HM * LV * m + HM * lv + h + 1)
                    if lv < LV - 1:
                        for k in range(KD):
                            last = mm(bank[6 + k][:, :], cms2_sb[:, lv, h, k * P:(k + 1) * P], gl[h % 2][:, :],
                                      start=(h == 0), stop=(h == HM - 1))
                            if h == HM - 1:
                                last.then_inc(l_ps, 1)
                    else:
                        for c in range(NC):
                            last = mm(bank[6 + c // 2][:, DM * (c % 2):DM * (c % 2 + 1)], gl[h % 2][:, c * P:(c + 1) * P],
                                      cms2_sb[:, lv, h, :], start=(h == 0 and c % 2 == 0), stop=(h == HM - 1),
                                      skip_group_check=True)
                            if h == HM - 1 and c % 2:
                                last.then_inc(l_ps, 1)

                def run(a, m):
                    for n in range(LV * HM):
                        lv, h = n // HM, n % HM
                        level_ends = h == HM - 1
                        if m is not None:
                            up(m, lv, h)
                        if a is not None and not level_ends:
                            for piece, c in BESIDE[n]:
                                stage1(a, piece, c)
                        if m is not None and h > 0:
                            down(m, lv, h - 1)
                        if m is not None and level_ends:
                            down(m, lv, h)
                        if a is not None and level_ends:
                            for piece, c in BESIDE[n]:
                                stage1(a, piece, c)

                run(0, None)
                pe.wait_ge(wc_sem, 16 * N_WC)
                with pe.Fori(0, NB - 1) as i:
                    run(i + 1, i)
                run(None, NB - 1)


def kernel(**inputs):
    import numpy as _np
    import concourse.bacc as _bacc
    from concourse import mybir as _mybir
    from concourse.bass_utils import run_bass_kernel_spmd as _run

    a = {k: _np.asarray(v) for k, v in inputs.items()}
    f0, f1 = ("L0_attn_", "L0_ffn_"), ("L1_attn_", "L1_ffn_")

    def columns(v):
        return v.reshape(-1, P).T

    def pair(name, back):
        return a[f0[0] + name], a[f0[0] + back]

    cols0 = _np.concatenate(
        [w[:, 0, :].reshape(DB, P, KC).transpose(1, 0, 2).reshape(P, -1) for w in pair("conv_w", "conv_w_b")]
        + [columns(v) for v in pair("conv_b", "conv_b_b")]
        + [columns(v) for v in pair("bdt", "bdt_b")]
        + [columns(v) for v in pair("D", "D_b")]
        + [v.reshape(DB, P, NS).transpose(1, 0, 2).reshape(P, -1) for v in pair("A_log", "A_b_log")], axis=1)
    cols1 = _np.concatenate([columns(a[f1[0] + n]) for n in ("ln1_g", "ln1_b", "ln2_g", "ln2_b", "cms_b1", "cms_b2")], axis=1)
    arrays = {
        "x": a[f0[0] + "hidden"], "w_inT": a[f0[0] + "W_in"].T, "w_xT": _np.stack([w.T for w in pair("Wx", "Wx_b")]),
        "w_dtT": _np.stack([w.T for w in pair("Wdt", "Wdt_b")]), "w_outT": a[f0[0] + "W_out"].T, "cols0": cols0,
        "rows0": _np.stack([a[f0[1] + "br"], a[f0[1] + "biases_N"]]), "w_rT": a[f0[1] + "Wr"].T,
        "wl1": a[f0[1] + "Wl1"],
        "bl1c": a[f0[1] + "bl1"].reshape(NE, 2 * HB, P).transpose(0, 2, 1), "wl2": a[f0[1] + "Wl2"], "bl2": a[f0[1] + "bl2"],
        "wqkv": _np.concatenate([a[f1[0] + n] for n in ("wq", "wk", "wv")], axis=1), "wo": a[f1[0] + "wo"], "cols1": cols1,
        "rows1": _np.stack([a[f1[1] + "b"], a[f1[0] + "cms_b2"][LV - 1]]),
        "cms1": a[f1[0] + "cms_w1"], "cms2": a[f1[0] + "cms_w2"], "w_fT": a[f1[1] + "W"].T, "v_r": a[f1[1] + "V_r"],
        "c_fT": a[f1[1] + "C"].T,
    }
    arrays = {k: _np.ascontiguousarray(v) for k, v in arrays.items()}
    nc = _bacc.Bacc("TRN2", target_bir_lowering=False, num_devices=1)
    args = [nc.dram_tensor(k, v.shape, _mybir.dt.from_np(v.dtype), kind="ExternalInput").ap() for k, v in arrays.items()]
    args.append(nc.dram_tensor("out", (NB, L, DM), _mybir.dt.float32, kind="ExternalOutput").ap())
    bass_mamba_moe_then_linear_attention_mlp(nc, *args)
    r = _run(nc, [arrays], core_ids=[0])
    return r.results[0]["out"]
```
